# Optimizing a Trainium2 kernel written in Bass

```python
import numpy as np
import jax
import jax.numpy as jnp

def _softmax(x, axis=-1):
    return jax.nn.softmax(x, axis=axis)

def _gelu(x):
    return jax.nn.gelu(x, approximate=True)

def _silu(x):
    return jax.nn.silu(x)

def _sigmoid(x):
    return jax.nn.sigmoid(x)

def _layernorm(x, axis=-1, eps=1e-05):
    m = jnp.mean(x, axis=axis, keepdims=True)
    v = jnp.var(x, axis=axis, keepdims=True)
    return (x - m) / jnp.sqrt(v + eps)

def _scatter_add(tgt, idx, src, axis=0):
    return tgt.at[idx].add(src)

def _segment_sum(src, seg, n):
    return jax.ops.segment_sum(src, seg, n)
kernel_name = 'mk_conv_preact_d4_conv_nchw256_r2_aa28fd'

def setup_inputs(seed: int=0):
    np.random.seed(seed)
    _w = jnp.asarray

    def _rec_inputs():
        import jax
        import jax.numpy as jnp
        _gk = jax.random.key(seed)
        x = -0.0001732 + 1 * jax.random.normal(jax.random.fold_in(_gk, 1), (2, 128, 48, 48), jnp.float32)
        return x
    x = _rec_inputs()

    def _L0_conv_setup():
        import jax, jax.numpy as jnp
        import numpy as np
        EPS = 1e-05

        def _conv(x, w, pad):
            return jax.lax.conv_general_dilated(x, w, window_strides=(1, 1), padding=((pad, pad), (pad, pad)), dimension_numbers=('NCHW', 'OIHW', 'NCHW'))

        def _dyn_branch(x, w, d):
            N, C, H, W = x.shape
            xp = jnp.pad(x, ((0, 0), (0, 0), (d, d), (d, d)))
            out = jnp.zeros_like(x)
            k = 0
            for dy in (-d, 0, d):
                for dx in (-d, 0, d):
                    patch = xp[:, :, d + dy:d + dy + H, d + dx:d + dx + W]
                    out = out + patch * w[:, k:k + 1]
                    k += 1
            return out
        key = jax.random.key(seed)
        k1, k2, k3 = jax.random.split(key, 3)
        C = 128
        x = jax.random.normal(k1, (2, C, 48, 48), dtype=jnp.float32)
        W_cat = jax.random.normal(k2, (45, C, 3, 3), dtype=jnp.float32) * 0.05
        W_scale = jax.random.normal(k3, (C, 6 * C, 1, 1), dtype=jnp.float32) * 0.05
        gamma = jnp.ones((C,), dtype=jnp.float32)
        beta = jnp.zeros((C,), dtype=jnp.float32)
        return {'x': x, 'W_cat': W_cat, 'W_scale': W_scale, 'gamma': gamma, 'beta': beta}
    _L0_conv_all = _L0_conv_setup()
    _L0_conv_in = {k: v for k, v in _L0_conv_all.items() if k in ('W_cat', 'W_scale', 'gamma', 'beta')}
    del _L0_conv_all

    def _L1_conv_setup():
        import jax, jax.numpy as jnp
        import numpy as np
        N_E = 8192
        E_DIM = 128
        key = jax.random.key(seed)
        k1, k2 = jax.random.split(key)
        z = jax.random.normal(k1, (8, E_DIM, 32, 32), dtype=jnp.float32)
        codebook = jax.random.uniform(k2, (N_E, E_DIM), dtype=jnp.float32, minval=-1.0 / N_E, maxval=1.0 / N_E)
        return {'z': z, 'codebook': codebook}
    _L1_conv_all = _L1_conv_setup()
    _L1_conv_in = {k: v for k, v in _L1_conv_all.items() if k in ('codebook',)}
    del _L1_conv_all

    def _L2_conv_setup():
        import jax, jax.numpy as jnp
        import numpy as np
        from jax import lax
        B, C, H, W = (32, 128, 56, 56)
        K = 3
        key = jax.random.key(seed)
        k1, k2, k3 = jax.random.split(key, 3)
        x = jax.random.normal(k1, (B, C, H, W), dtype=jnp.float32)
        Wk = jax.random.normal(k2, (C * K * K, C), dtype=jnp.float32) * 0.02
        bk = jax.random.normal(k3, (C * K * K,), dtype=jnp.float32) * 0.02
        return {'x': x, 'Wk': Wk, 'bk': bk}
    _L2_conv_all = _L2_conv_setup()
    _L2_conv_in = {k: v for k, v in _L2_conv_all.items() if k in ('Wk', 'bk')}
    del _L2_conv_all

    def _L3_conv_setup():
        import jax, jax.numpy as jnp
        import numpy as np
        EPS = 1e-05

        def conv3x3(x, w, b):
            y = jax.lax.conv_general_dilated(x, w, window_strides=(1, 1), padding=((1, 1), (1, 1)), dimension_numbers=('NCHW', 'OIHW', 'NCHW'))
            return y + b[None, :, None, None]

        def deform_conv(x, offset, weight):
            B, C, H, W = x.shape
            off = offset.reshape(B, 9, 2, H, W)
            dy, dx = (off[:, :, 0], off[:, :, 1])
            ky, kx = jnp.meshgrid(jnp.arange(3), jnp.arange(3), indexing='ij')
            ky = ky.reshape(9).astype(x.dtype)
            kx = kx.reshape(9).astype(x.dtype)
            py = jnp.arange(H, dtype=x.dtype)[None, None, :, None] - 1.0 + ky[None, :, None, None] + dy
            px = jnp.arange(W, dtype=x.dtype)[None, None, None, :] - 1.0 + kx[None, :, None, None] + dx
            y0 = jnp.floor(py)
            x0 = jnp.floor(px)
            ty = py - y0
            tx = px - x0
            x_flat = x.reshape(B, C, H * W)

            def gather(yi, xi):
                valid = ((yi >= 0) & (yi < H) & (xi >= 0) & (xi < W)).astype(x.dtype)
                yc = jnp.clip(yi, 0, H - 1).astype(jnp.int32)
                xc = jnp.clip(xi, 0, W - 1).astype(jnp.int32)
                idx = (yc * W + xc).reshape(B, 1, 9 * H * W)
                vals = jnp.take_along_axis(x_flat, idx, axis=2).reshape(B, C, 9, H, W)
                return vals * valid.reshape(B, 1, 9, H, W)
            sampled = gather(y0, x0) * ((1 - ty) * (1 - tx))[:, None] + gather(y0, x0 + 1) * ((1 - ty) * tx)[:, None] + gather(y0 + 1, x0) * (ty * (1 - tx))[:, None] + gather(y0 + 1, x0 + 1) * (ty * tx)[:, None]
            return jnp.einsum('bckhw,ock->bohw', sampled, weight.reshape(weight.shape[0], C, 9))

        def group_norm(x, scale, bias, groups=8):
            B, C, H, W = x.shape
            xg = x.reshape(B, groups, C // groups, H, W)
            mu = xg.mean(axis=(2, 3, 4), keepdims=True)
            var = ((xg - mu) ** 2).mean(axis=(2, 3, 4), keepdims=True)
            xn = ((xg - mu) * jax.lax.rsqrt(var + EPS)).reshape(B, C, H, W)
            return xn * scale[None, :, None, None] + bias[None, :, None, None]
        key = jax.random.key(seed)
        ks = jax.random.split(key, 12)
        B, C, H, W = (2, 128, 32, 32)
        f = jnp.float32
        return {'x': jax.random.normal(ks[0], (B, C, H, W), dtype=f), 'off1_w': jax.random.normal(ks[1], (18, C, 3, 3), dtype=f) * 0.01, 'off1_b': jnp.zeros((18,), dtype=f), 'dw1': jax.random.normal(ks[2], (C, C, 3, 3), dtype=f) * 0.02, 'gn1_s': jnp.ones((C,), dtype=f), 'gn1_b': jnp.zeros((C,), dtype=f), 'off2_w': jax.random.normal(ks[3], (18, C, 3, 3), dtype=f) * 0.01, 'off2_b': jnp.zeros((18,), dtype=f), 'dw2': jax.random.normal(ks[4], (C, C, 3, 3), dtype=f) * 0.02, 'gn2_s': jnp.ones((C,), dtype=f), 'gn2_b': jnp.zeros((C,), dtype=f)}
    _L3_conv_all = _L3_conv_setup()
    _L3_conv_in = {k: v for k, v in _L3_conv_all.items() if k in ('off1_w', 'off1_b', 'dw1', 'gn1_s', 'gn1_b', 'off2_w', 'off2_b', 'dw2', 'gn2_s', 'gn2_b')}
    del _L3_conv_all
    return {'x': x, 'L0_conv_W_cat': _L0_conv_in['W_cat'], 'L0_conv_W_scale': _L0_conv_in['W_scale'], 'L0_conv_gamma': _L0_conv_in['gamma'], 'L0_conv_beta': _L0_conv_in['beta'], 'L1_conv_codebook': _L1_conv_in['codebook'], 'L2_conv_Wk': _L2_conv_in['Wk'], 'L2_conv_bk': _L2_conv_in['bk'], 'L3_conv_off1_w': _L3_conv_in['off1_w'], 'L3_conv_off1_b': _L3_conv_in['off1_b'], 'L3_conv_dw1': _L3_conv_in['dw1'], 'L3_conv_gn1_s': _L3_conv_in['gn1_s'], 'L3_conv_gn1_b': _L3_conv_in['gn1_b'], 'L3_conv_off2_w': _L3_conv_in['off2_w'], 'L3_conv_off2_b': _L3_conv_in['off2_b'], 'L3_conv_dw2': _L3_conv_in['dw2'], 'L3_conv_gn2_s': _L3_conv_in['gn2_s'], 'L3_conv_gn2_b': _L3_conv_in['gn2_b']}

def reference(x, L0_conv_W_cat, L0_conv_W_scale, L0_conv_gamma, L0_conv_beta, L1_conv_codebook, L2_conv_Wk, L2_conv_bk, L3_conv_off1_w, L3_conv_off1_b, L3_conv_dw1, L3_conv_gn1_s, L3_conv_gn1_b, L3_conv_off2_w, L3_conv_off2_b, L3_conv_dw2, L3_conv_gn2_s, L3_conv_gn2_b):
    import jax
    import jax.numpy as jnp

    def _L0_conv_ref(x, W_cat, W_scale, gamma, beta):
        import jax, jax.numpy as jnp
        import numpy as np
        EPS = 1e-05

        def _conv(x, w, pad):
            return jax.lax.conv_general_dilated(x, w, window_strides=(1, 1), padding=((pad, pad), (pad, pad)), dimension_numbers=('NCHW', 'OIHW', 'NCHW'))

        def _dyn_branch(x, w, d):
            N, C, H, W = x.shape
            xp = jnp.pad(x, ((0, 0), (0, 0), (d, d), (d, d)))
            out = jnp.zeros_like(x)
            k = 0
            for dy in (-d, 0, d):
                for dx in (-d, 0, d):
                    patch = xp[:, :, d + dy:d + dy + H, d + dx:d + dx + W]
                    out = out + patch * w[:, k:k + 1]
                    k += 1
            return out
        guidance = _conv(x, W_cat, pad=1)
        outs = [x]
        for i, d in enumerate((1, 6, 12, 24, 36)):
            w = jax.nn.softmax(guidance[:, 9 * i:9 * (i + 1)], axis=1)
            outs.append(_dyn_branch(x, w, d))
        cat = jnp.concatenate(outs, axis=1)
        y = _conv(cat, W_scale, pad=0)
        mean = jnp.mean(y, axis=(0, 2, 3), keepdims=True)
        var = jnp.var(y, axis=(0, 2, 3), keepdims=True)
        y = (y - mean) * jax.lax.rsqrt(var + EPS)
        return y * gamma[None, :, None, None] + beta[None, :, None, None]

    def _L1_conv_ref(z, codebook):
        import jax, jax.numpy as jnp
        import numpy as np
        N_E = 8192
        E_DIM = 128
        B, C, H, W = z.shape
        z_perm = jnp.transpose(z, (0, 2, 3, 1))
        z_flat = z_perm.reshape(-1, C)
        d = jnp.sum(z_flat ** 2, axis=1, keepdims=True) + jnp.sum(codebook ** 2, axis=1) - 2.0 * jnp.matmul(z_flat, codebook.T)
        idx = jnp.argmin(d, axis=1)
        z_q = codebook[idx].reshape(B, H, W, C)
        z_q = z_perm + jax.lax.stop_gradient(z_q - z_perm)
        return jnp.transpose(z_q, (0, 3, 1, 2))

    def _L2_conv_ref(x, Wk, bk):
        import jax, jax.numpy as jnp
        import numpy as np
        from jax import lax
        B, C, H, W = (32, 128, 56, 56)
        K = 3
        b, c, h, w = x.shape
        pooled = x.mean(axis=(2, 3))
        kern = jax.nn.relu(pooled @ Wk.T + bk)
        kern = kern.reshape(b * c, 1, K, K)
        xr = x.reshape(1, b * c, h, w)
        out = lax.conv_general_dilated(xr, kern, window_strides=(1, 1), padding=[(K // 2, K // 2), (K // 2, K // 2)], feature_group_count=b * c, dimension_numbers=('NCHW', 'OIHW', 'NCHW'))
        return out.reshape(b, c, h, w)

    def _L3_conv_ref(x, off1_w, off1_b, dw1, gn1_s, gn1_b, off2_w, off2_b, dw2, gn2_s, gn2_b):
        import jax, jax.numpy as jnp
        import numpy as np
        EPS = 1e-05

        def conv3x3(x, w, b):
            y = jax.lax.conv_general_dilated(x, w, window_strides=(1, 1), padding=((1, 1), (1, 1)), dimension_numbers=('NCHW', 'OIHW', 'NCHW'))
            return y + b[None, :, None, None]

        def deform_conv(x, offset, weight):
            B, C, H, W = x.shape
            off = offset.reshape(B, 9, 2, H, W)
            dy, dx = (off[:, :, 0], off[:, :, 1])
            ky, kx = jnp.meshgrid(jnp.arange(3), jnp.arange(3), indexing='ij')
            ky = ky.reshape(9).astype(x.dtype)
            kx = kx.reshape(9).astype(x.dtype)
            py = jnp.arange(H, dtype=x.dtype)[None, None, :, None] - 1.0 + ky[None, :, None, None] + dy
            px = jnp.arange(W, dtype=x.dtype)[None, None, None, :] - 1.0 + kx[None, :, None, None] + dx
            y0 = jnp.floor(py)
            x0 = jnp.floor(px)
            ty = py - y0
            tx = px - x0
            x_flat = x.reshape(B, C, H * W)

            def gather(yi, xi):
                valid = ((yi >= 0) & (yi < H) & (xi >= 0) & (xi < W)).astype(x.dtype)
                yc = jnp.clip(yi, 0, H - 1).astype(jnp.int32)
                xc = jnp.clip(xi, 0, W - 1).astype(jnp.int32)
                idx = (yc * W + xc).reshape(B, 1, 9 * H * W)
                vals = jnp.take_along_axis(x_flat, idx, axis=2).reshape(B, C, 9, H, W)
                return vals * valid.reshape(B, 1, 9, H, W)
            sampled = gather(y0, x0) * ((1 - ty) * (1 - tx))[:, None] + gather(y0, x0 + 1) * ((1 - ty) * tx)[:, None] + gather(y0 + 1, x0) * (ty * (1 - tx))[:, None] + gather(y0 + 1, x0 + 1) * (ty * tx)[:, None]
            return jnp.einsum('bckhw,ock->bohw', sampled, weight.reshape(weight.shape[0], C, 9))

        def group_norm(x, scale, bias, groups=8):
            B, C, H, W = x.shape
            xg = x.reshape(B, groups, C // groups, H, W)
            mu = xg.mean(axis=(2, 3, 4), keepdims=True)
            var = ((xg - mu) ** 2).mean(axis=(2, 3, 4), keepdims=True)
            xn = ((xg - mu) * jax.lax.rsqrt(var + EPS)).reshape(B, C, H, W)
            return xn * scale[None, :, None, None] + bias[None, :, None, None]
        offset1 = conv3x3(x, off1_w, off1_b)
        out = deform_conv(x, offset1, dw1)
        out = jax.nn.relu(group_norm(out, gn1_s, gn1_b))
        offset2 = conv3x3(out, off2_w, off2_b)
        out = deform_conv(out, offset2, dw2)
        out = jax.nn.relu(group_norm(out, gn2_s, gn2_b))
        return out

    def _gn(v, G=32, eps=1e-05):
        B_, C_, H_, W_ = v.shape
        g = v.reshape(B_, G, C_ // G, H_, W_)
        m = jnp.mean(g, axis=(2, 3, 4), keepdims=True)
        s = jnp.var(g, axis=(2, 3, 4), keepdims=True)
        return ((g - m) / jnp.sqrt(s + eps)).reshape(v.shape)

    def _ln_c(v, eps=1e-06):
        m = jnp.mean(v, axis=1, keepdims=True)
        s = jnp.var(v, axis=1, keepdims=True)
        return (v - m) / jnp.sqrt(s + eps)

    def _ln_t(v, eps=1e-05):
        m = jnp.mean(v, axis=-1, keepdims=True)
        s = jnp.var(v, axis=-1, keepdims=True)
        return (v - m) / jnp.sqrt(s + eps)

    def _to_tokens(v):
        B_, C_, H_, W_ = v.shape
        return v.reshape(B_, C_, H_ * W_).transpose(0, 2, 1)

    def _from_tokens(t, like):
        B_, C_, H_, W_ = like.shape
        return t.transpose(0, 2, 1).reshape(B_, C_, H_, W_)
    x = x + _L0_conv_ref(_gn(x), L0_conv_W_cat, L0_conv_W_scale, L0_conv_gamma, L0_conv_beta)
    x = x + _L1_conv_ref(_gn(x), L1_conv_codebook)
    x = x + _L2_conv_ref(_gn(x), L2_conv_Wk, L2_conv_bk)
    x = x + _L3_conv_ref(_gn(x), L3_conv_off1_w, L3_conv_off1_b, L3_conv_dw1, L3_conv_gn1_s, L3_conv_gn1_b, L3_conv_off2_w, L3_conv_off2_b, L3_conv_dw2, L3_conv_gn2_s, L3_conv_gn2_b)
    return x

_drawn_inputs = setup_inputs


def setup_inputs(seed=0):
    import zlib

    import numpy as np

    out = dict(_drawn_inputs(seed))
    spreads = {'L0_conv_gamma': (1.0, 0.2),
     'L0_conv_beta': (0.0, 0.1),
     'L3_conv_off1_b': (0.0, 0.1),
     'L3_conv_gn1_s': (1.0, 0.2),
     'L3_conv_gn1_b': (0.0, 0.1),
     'L3_conv_off2_b': (0.0, 0.1),
     'L3_conv_gn2_s': (1.0, 0.2),
     'L3_conv_gn2_b': (0.0, 0.1)}
    factors = {'L1_conv_codebook': 8.0, 'L2_conv_Wk': 2.916}
    for name, (base, spread) in spreads.items():
        noise = np.random.default_rng([zlib.crc32(name.encode()), seed]).standard_normal(out[name].shape)
        drawn = base * np.exp(spread * noise) if base else spread * noise
        out[name] = jnp.asarray(drawn.astype(out[name].dtype))
    for name, factor in factors.items():
        out[name] = (out[name] * factor).astype(out[name].dtype)
    return out
```

```python
from contextlib import ExitStack

import numpy as np

import concourse.bass as bass
from concourse import mybir

P = 128
B, H, W = 2, 48, 48
HW = H * W
N = B * HW
WP = W + 2
HP = H + 2
PADDED = HP * WP
EPS = 1e-5

ROWS = 8
CH = ROWS * W
NCH = H // ROWS
TPC = CH // P
TILES = N // P
DIL = (1, 6, 12, 24, 36)
NB = len(DIL)
TAPS = 9
NG = NB * TAPS
NA = 4 * TAPS

CODES = 8192
GROUPS = 8
PER = CODES // P // GROUPS
PX = 512
NPX = N // PX

ALU = mybir.AluOpType
ACT = mybir.ActivationFunctionType
AX = mybir.AxisListType.X
F32 = mybir.dt.float32
BF16 = mybir.dt.bfloat16
U32 = mybir.dt.uint32
ROUND = float(2 ** 23)


def bc(ap, n):
    return ap.unsqueeze(len(ap.shape)).to_broadcast([*ap.shape, n])


def overlapped(v, half, rows):
    part, row, col = v.ap
    ap = [list(part), [row[0] * (rows - half), 2], [row[0], half], list(col)]
    return bass.AP(tensor=v.tensor, offset=v.offset, ap=ap)


class Tools:

    def __init__(self, nc):
        self.nc, self.n = nc, 0

    def sb(self, ctx, name, shape, dt=F32):
        self.n += 1
        return ctx.enter_context(self.nc.sbuf_tensor(f"{name}_{self.n}", shape, dt))

    def ps(self, ctx, name, shape, dt=F32):
        self.n += 1
        return ctx.enter_context(self.nc.psum_tensor(f"{name}_{self.n}", shape, dt))

    def sem(self, ctx, name):
        self.n += 1
        return ctx.enter_context(self.nc.semaphore(f"{name}_{self.n}"))


class Apart:

    def __init__(self, eng, spare):
        self.eng, self.spare = eng, spare

    def wait_ge(self, sem, value):
        self.eng.wait_ge(sem, value)
        self.eng.sem_inc(self.spare, 1)


class Chain:

    def __init__(self, eng, sem):
        self.eng, self.sem, self.n = eng, sem, 0

    def __call__(self, ins):
        self.n += 1
        ins.then_inc(self.sem, 1)
        self.eng.wait_ge(self.sem, self.n)


def inv_sqrt(eng, act_eng, chain, var, tmp, out, ready, rooted):
    chain(eng.tensor_scalar(var, var, EPS, None, ALU.add))
    eng.sem_inc(ready, 1)
    eng.wait_ge(rooted, 1)
    chain(eng.reciprocal(out, tmp))
    chain(eng.tensor_tensor(tmp, out, out, ALU.mult))
    chain(eng.tensor_tensor(tmp, tmp, var, ALU.mult))
    chain(eng.tensor_scalar(tmp, tmp, -0.5, 1.5, ALU.mult, ALU.add))
    chain(eng.tensor_tensor(out, out, tmp, ALU.mult))


def group_norm_scale(nc, tools, src, gmat, scale, shift, pooled=None):
    with ExitStack() as ctx:
        stats = tools.sb(ctx, "gn_stats", [P, B, NCH, 6])
        mv = tools.sb(ctx, "gn_mean_var", [P, B, 2])
        mm = tools.sb(ctx, "gn_moments", [P, 2, B])
        gg = tools.sb(ctx, "gn_group", [P, 2, B])
        var = tools.sb(ctx, "gn_var", [P, B])
        tmp = tools.sb(ctx, "gn_tmp", [P, B])
        ps = tools.ps(ctx, "gn_ps", [P, 2, B])
        step = tools.sem(ctx, "gn_step")
        moments_ready = tools.sem(ctx, "gn_moments_ready")
        group_ready = tools.sem(ctx, "gn_group_ready")
        var_ready = tools.sem(ctx, "gn_var_ready")
        rooted = tools.sem(ctx, "gn_rooted")
        block = ctx.enter_context(nc.Block())

        @block.vector
        def _(dve):
            chain = Chain(dve, step)
            for b in range(B):
                for q in range(NCH):
                    last = dve.bn_stats(stats[:, b, q, :], src[:, b, q * CH:(q + 1) * CH])
            chain(last)
            for b in range(B):
                chain(dve.bn_aggr(mv[:, b, :], stats[:, b, :, :].rearrange("p q s -> p (q s)")))
            chain(dve.tensor_copy(mm[:, 0, :], mv[:, :, 0]))
            chain(dve.tensor_tensor(mm[:, 1, :], mm[:, 0, :], mm[:, 0, :], ALU.mult))
            chain(dve.tensor_tensor(mm[:, 1, :], mm[:, 1, :], mv[:, :, 1], ALU.add))
            dve.sem_inc(moments_ready, 1)
            dve.wait_ge(group_ready, 1)
            chain(dve.tensor_copy(gg[:], ps[:]))
            chain(dve.tensor_tensor(var[:], gg[:, 0, :], gg[:, 0, :], ALU.mult))
            chain(dve.tensor_tensor(var[:], gg[:, 1, :], var[:], ALU.subtract))
            inv_sqrt(dve, None, chain, var[:], tmp[:], scale, var_ready, rooted)
            chain(dve.tensor_tensor(shift, gg[:, 0, :], scale, ALU.mult))
            chain(dve.tensor_scalar(shift, shift, -1.0, None, ALU.mult))
            if pooled is not None:
                chain(dve.tensor_tensor(pooled, mm[:, 0, :], scale, ALU.mult))
                chain(dve.tensor_tensor(pooled, pooled, shift, ALU.add))

        @block.tensor
        def _(pe):
            pe.wait_ge(moments_ready, 1)
            pe.matmul(ps[:], gmat, mm[:], start=True, stop=True).then_inc(group_ready, 1)

        @block.scalar
        def _(act):
            act.wait_ge(var_ready, 1)
            act.sqrt(tmp[:], var[:]).then_inc(rooted, 1)


def apply_padded(nc, tools, src, scale, shift, padded):
    with ExitStack() as ctx:
        done = tools.sem(ctx, "applied")
        block = ctx.enter_context(nc.Block())
        inner = padded[:, 0:B * PADDED].rearrange("p (b r w) -> p b r w", b=B, w=WP)

        @block.vector
        def _(dve):
            dve.tensor_scalar(inner[:, 0, 1:H + 1, 1:W + 1], src[:, 0, :].rearrange("p (r w) -> p r w", w=W),
                              scale[:, 0:1], shift[:, 0:1], ALU.mult, ALU.add).then_inc(done, 1)

        @block.scalar
        def _(act):
            act.activation(inner[:, 1, 1:H + 1, 1:W + 1], src[:, 1, :].rearrange("p (r w) -> p r w", w=W),
                           ACT.Identity, bias=shift[:, 1:2], scale=scale[:, 1:2]).then_inc(done, 1)


def guidance(nc, tools, xpad, w_guide, ident, ident_b, wta, wtb):
    SLOTS = 2
    with ExitStack() as ctx:
        gps = [tools.ps(ctx, "g_ps", [P, 512])[0:NG, 0:CH] for _ in range(SLOTS)]
        gtp = [tools.ps(ctx, "gt_ps", [P, 512])[:, 0:CH].rearrange("p (t n) -> p t n", t=TPC)
               for _ in range(SLOTS)]
        wap = [tools.ps(ctx, "wa_ps", [P, 1024], BF16)[0:3 * NA, 0:CH] for _ in range(SLOTS)]
        wbp = [tools.ps(ctx, "wb_ps", [P, 1024], BF16)[0:3 * TAPS, 0:CH] for _ in range(SLOTS)]
        gsb = tools.sb(ctx, "g_sb", [P, SLOTS, CH])
        mx = tools.sb(ctx, "g_max", [P, SLOTS, TPC * NB])
        e = tools.sb(ctx, "g_exp", [P, SLOTS, TPC * NB, TAPS])
        den = tools.sb(ctx, "g_den", [P, SLOTS, TPC * NB])
        res = tools.sb(ctx, "g_res", [P, SLOTS, TPC, NG])
        wa = tools.sb(ctx, "w_a", [P, SLOTS, TPC, 3, NA], BF16)
        wb = tools.sb(ctx, "w_b", [P, SLOTS, TPC, 3, TAPS], BF16)
        zeroed = tools.sem(ctx, "g_sb_zeroed")
        conv_done = tools.sem(ctx, "conv_done")
        gps_free = tools.sem(ctx, "gps_free")
        g_saved = tools.sem(ctx, "g_saved")
        turned = tools.sem(ctx, "turned")
        step = [tools.sem(ctx, f"soft_step{b}") for b in range(SLOTS)]
        shifted = tools.sem(ctx, "shifted")
        exped = tools.sem(ctx, "exped")
        split_done = tools.sem(ctx, "split_done")
        back = tools.sem(ctx, "turned_back")
        saved = tools.sem(ctx, "weights_saved")
        STEPS = 12
        block = ctx.enter_context(nc.Block())

        @block.gpsimd
        def _(pool):
            pool.memset(gsb[:], 0.0).then_inc(zeroed, 1)

        @block.tensor
        def _(pe):
            pe.sem_inc(gps_free, SLOTS)
            with pe.Fori(0, NCH) as r:
                for b in range(B):
                    pe.wait_ge(gps_free, B * r + b + 1)
                    for t in range(TAPS):
                        at = b * PADDED + r * (ROWS * WP) + (t // 3) * WP + t % 3
                        win = xpad[:, bass.ds(at, ROWS * WP)]
                        win = win.rearrange("p (r w) -> p r w", w=WP)[:, :, 0:W]
                        mm = pe.matmul(gps[b], w_guide[:, t, :], win, start=t == 0, stop=t == TAPS - 1)
                    mm.then_inc(conv_done, 1)
                for b in range(B):
                    pe.wait_ge(g_saved, B * r + b + 1)
                    for t in range(TPC):
                        mm = pe.transpose(gtp[b][:, t, :], gsb[:, b, t * P:(t + 1) * P], ident)
                    mm.then_inc(turned, 1)
                for b in range(B):
                    pe.wait_ge(split_done, B * r + b + 1)
                    for t in range(TPC):
                        pe.transpose(wap[b][:, t * P:(t + 1) * P],
                                     wa[:, b, t, :, :].rearrange("p s k -> p (s k)"), ident_b)
                        mm = pe.transpose(wbp[b][:, t * P:(t + 1) * P],
                                          wb[:, b, t, :, :].rearrange("p s k -> p (s k)"), ident_b)
                    mm.then_inc(back, 1)

        @block.scalar
        def _(act):
            act.wait_ge(zeroed, 1)
            with act.Fori(0, NCH) as r:
                for b in range(B):
                    act.wait_ge(conv_done, B * r + b + 1)
                    act.copy(gsb[0:NG, b, :], gps[b]).then_inc(g_saved, 1)
                    act.wait_ge(g_saved, B * r + b + 1)
                    act.sem_inc(gps_free, 1)
                for b in range(B):
                    act.wait_ge(shifted, B * r + b + 1)
                    act.activation(e[:, b], e[:, b], ACT.Exp).then_inc(exped, 1)
                for b in range(B):
                    act.wait_ge(back, B * r + b + 1)
                    at = b * HW + r * CH
                    act.copy(wta[:, bass.ds(at, CH)], wap[b])
                    act.copy(wtb[:, bass.ds(at, CH)], wbp[b]).then_inc(saved, 1)
                act.wait_ge(saved, B * r + B)

        @block.vector
        def _(dve):
            with dve.Fori(0, NCH) as r:
                def chained(b, n, ins):
                    ins.then_inc(step[b], 1)
                    dve.wait_ge(step[b], STEPS * r + n)

                for b in range(B):
                    dve.wait_ge(turned, B * r + b + 1)
                    g = gtp[b][:, :, 0:NG].rearrange("p t (n k) -> p t n k", k=TAPS)
                    chained(b, 1, dve.tensor_reduce(mx[:, b], g, AX, ALU.max))
                    dve.tensor_tensor(e[:, b].rearrange("p (t n) k -> p t n k", t=TPC), g,
                                      bc(mx[:, b].rearrange("p (t n) -> p t n", t=TPC), TAPS),
                                      ALU.subtract).then_inc(shifted, 1)
                for b in range(B):
                    dve.wait_ge(exped, B * r + b + 1)
                    chained(b, 2, dve.tensor_reduce(den[:, b], e[:, b], AX, ALU.add))
                    chained(b, 3, dve.reciprocal(den[:, b], den[:, b]))
                    r4 = res[:, b].rearrange("p t (n k) -> p (t n) k", k=TAPS)
                    chained(b, 4, dve.tensor_tensor(r4, e[:, b], bc(den[:, b], TAPS), ALU.mult))
                    ra, rb = res[:, b, :, 0:NA], res[:, b, :, NA:NG]
                    dve.tensor_copy(wa[:, b, :, 0, :], ra).then_inc(step[b], 1)
                    chained(b, 6, dve.tensor_copy(wb[:, b, :, 0, :], rb))
                    dve.tensor_tensor(ra, ra, wa[:, b, :, 0, :], ALU.subtract).then_inc(step[b], 1)
                    chained(b, 8, dve.tensor_tensor(rb, rb, wb[:, b, :, 0, :], ALU.subtract))
                    dve.tensor_copy(wa[:, b, :, 1, :], ra).then_inc(step[b], 1)
                    chained(b, 10, dve.tensor_copy(wb[:, b, :, 1, :], rb))
                    dve.tensor_tensor(wa[:, b, :, 2, :], ra, wa[:, b, :, 1, :], ALU.subtract).then_inc(step[b], 1)
                    chained(b, STEPS, dve.tensor_tensor(wb[:, b, :, 2, :], rb, wb[:, b, :, 1, :], ALU.subtract))
                    dve.sem_inc(split_done, 1)


def branch_ops():
    ops = []
    for q in range(H // (2 * ROWS)):
        for i, d in enumerate(DIL):
            for k in range(TAPS):
                dy, dx = (k // 3 - 1) * d, (k % 3 - 1) * d
                r0, r1 = max(2 * ROWS * q, -dy), min(2 * ROWS * (q + 1), H - dy)
                c0, c1 = max(0, -dx), min(W, W - dx)
                if r1 <= r0 or c1 <= c0:
                    continue
                n = r1 - r0
                halves = 1 if n * (c1 - c0) <= 512 else 2
                ops.append((q, i, k, dy, dx, r0, -(-n // halves), n, halves, c0, c1))
    return ops


def pieces(r0, half, n, halves):
    out = []
    for h in range(halves):
        start = r0 + (n - half) * h
        at = start if h == 0 else r0 + half
        while at < start + half:
            to = min(start + half, (at // ROWS + 1) * ROWS)
            out.append((h, at - start, to - at, at, at // ROWS % 2))
            at = to
    return out


def branches(nc, tools, xpad, wta, wtb, sel_a, sel_b, w_scale, y):
    SLOTS, LAG = 3, 2
    ops = branch_ops()
    M, CHUNKS = len(ops), H // (2 * ROWS)
    first = [min(n for n, o in enumerate(ops) if o[0] == q) for q in range(CHUNKS)] + [M]
    with ExitStack() as ctx:
        spread = [tools.ps(ctx, "spread", [P, 2, 512]) for _ in range(SLOTS)]
        yps = tools.ps(ctx, "y_ps", [P, 2, 512])
        prod = [tools.sb(ctx, "prod", [P, 2 * ROWS * W]) for _ in range(SLOTS)]
        spread_ready = tools.sem(ctx, "spread_ready")
        prod_ready = tools.sem(ctx, "prod_ready")
        prod_free = tools.sem(ctx, "prod_free")
        y_ready = tools.sem(ctx, "y_ready")
        y_free = tools.sem(ctx, "y_free")
        block = ctx.enter_context(nc.Block())

        def window(b, r, rows, c, cols):
            v = xpad[:, bass.ds(b * PADDED + (r + 1) * WP, rows * WP)]
            return v.rearrange("p (r w) -> p r w", w=WP)[:, :, c + 1:c + 1 + cols]

        @block.tensor
        def _(pe):
            pe.sem_inc(prod_free, SLOTS)
            with pe.Fori(0, B) as b:
                def spread_op(n):
                    q, i, k, dy, dx, r0, half, rows, halves, c0, c1 = ops[n]
                    wt, sel, kk = (wta, sel_a, i * TAPS + k) if i < 4 else (wtb, sel_b, k)
                    for h in range(halves):
                        at = b * HW + (r0 + (rows - half) * h) * W
                        v = wt[:, bass.ds(at, half * W)].rearrange("p (r w) -> p r w", w=W)[:, :, c0:c1]
                        o = spread[n % SLOTS][:, h, 0:half * (c1 - c0)].rearrange("p (r w) -> p r w", r=half)
                        mm = pe.matmul(o, sel[:, kk, :], v, start=True, stop=True)
                    mm.then_inc(spread_ready, 1)

                def start_chunk(q):
                    pe.wait_ge(y_free, b * CHUNKS + q + 1)
                    for j in range(2):
                        pe.matmul(yps[:, j, 0:CH].rearrange("p (r w) -> p r w", w=W), w_scale[:, 0, :],
                                  window(b, (2 * q + j) * ROWS, ROWS, 0, W), start=True, stop=False,
                                  skip_group_check=True)

                def add_op(n):
                    q, i, k, dy, dx, r0, half, rows, halves, c0, c1 = ops[n]
                    pe.wait_ge(prod_ready, b * M + n + 1)
                    nc_ = c1 - c0
                    for h, hr, m, row, bank in pieces(r0, half, rows, halves):
                        src = prod[n % SLOTS][:, (h * half + hr) * nc_:(h * half + hr + m) * nc_]
                        dst = yps[:, bank, 0:CH].rearrange("p (r w) -> p r w", w=W)[
                            :, row % ROWS:row % ROWS + m, c0:c1]
                        mm = pe.matmul(dst, w_scale[:, i + 1, :], src.rearrange("p (r w) -> p r w", r=m),
                                       start=False, stop=n + 1 == first[q + 1], skip_group_check=True)
                    mm.then_inc(prod_free, 1)
                    if n + 1 == first[q + 1]:
                        pe.wait_ge(prod_free, SLOTS + b * M + n + 1)
                        pe.sem_inc(y_ready, 1)
                        if q + 1 < CHUNKS:
                            start_chunk(q + 1)

                for n in range(LAG):
                    spread_op(n)
                start_chunk(0)
                for n in range(M):
                    if n + LAG < M:
                        spread_op(n + LAG)
                    add_op(n)

        @block.vector
        def _(dve):
            with dve.Fori(0, B) as b:
                for n, (q, i, k, dy, dx, r0, half, rows, halves, c0, c1) in enumerate(ops):
                    dve.wait_ge(spread_ready, b * M + n + 1)
                    dve.wait_ge(prod_free, b * M + n + 1)
                    cols = c1 - c0
                    v = xpad[:, bass.ds(b * PADDED + (r0 + dy + 1) * WP, rows * WP)]
                    v = v.rearrange("p (r w) -> p r w", w=WP)[:, :, c0 + dx + 1:c1 + dx + 1]
                    o = prod[n % SLOTS][:, 0:halves * half * cols]
                    if halves == 1:
                        dve.tensor_tensor(o.rearrange("p (r w) -> p r w", r=half),
                                          spread[n % SLOTS][:, 0, 0:half * cols].rearrange("p (r w) -> p r w", r=half),
                                          v, ALU.mult).then_inc(prod_ready, 1)
                    else:
                        v = overlapped(v, half, rows)
                        dve.tensor_tensor(o.rearrange("p (h r w) -> p h r w", h=2, r=half),
                                          spread[n % SLOTS][:, :, 0:half * cols].rearrange("p h (r w) -> p h r w", r=half),
                                          v, ALU.mult).then_inc(prod_ready, 1)

        @block.scalar
        def _(act):
            act.sem_inc(y_free, 1)
            with act.Fori(0, B) as b:
                for q in range(CHUNKS):
                    act.wait_ge(y_ready, b * CHUNKS + q + 1)
                    to = y[:, bass.ds(b * HW + q * 2 * CH, 2 * CH)].rearrange("p (h n) -> p h n", h=2)
                    act.copy(to, yps[:, :, 0:CH]).then_inc(y_free, 1)


def load(nc, tools, pairs):
    with ExitStack() as ctx:
        loaded = tools.sem(ctx, "loaded")
        with nc.Block() as block:
            @block.sync
            def _(sp):
                for to, src in pairs:
                    sp.dma_start(to, src).then_inc(loaded, 16)
                sp.wait_ge(loaded, 16 * len(pairs))


def layer0(nc, tools, a, x, xpad, gm32, ident, scale, shift):
    with ExitStack() as ctx:
        w_guide = tools.sb(ctx, "w_guide", [P, TAPS, NG])
        w_scale = tools.sb(ctx, "w_scale", [P, NB + 1, P])
        gb = tools.sb(ctx, "gamma_beta", [P, 2])
        ident_b = tools.sb(ctx, "ident_b", [P, P], BF16)
        sel_a = tools.sb(ctx, "sel_a", [3 * NA, NA, P], BF16)
        sel_b = tools.sb(ctx, "sel_b", [3 * TAPS, TAPS, P], BF16)
        id3a = tools.sb(ctx, "id3a", [3 * NA, NA])
        id3b = tools.sb(ctx, "id3b", [3 * TAPS, TAPS])
        wta = tools.sb(ctx, "wta", [3 * NA, N], BF16)
        wtb = tools.sb(ctx, "wtb", [3 * TAPS, N], BF16)
        y = tools.sb(ctx, "y", [P, N])
        cast = tools.sem(ctx, "cast")
        group_norm_scale(nc, tools, x, gm32, scale, shift)
        apply_padded(nc, tools, x, scale, shift, xpad)
        load(nc, tools, [(w_guide[:], a["w_cat"]), (w_scale[:], a["w_scale"]), (gb[:], a["gamma_beta"]),
                         (id3a[:], a["id3a"]), (id3b[:], a["id3b"])])
        with nc.Block() as block:
            @block.vector
            def _(dve):
                dve.tensor_copy(ident_b[:], ident).then_inc(cast, 1)
                dve.tensor_copy(sel_a[:], bc(id3a[:], P)).then_inc(cast, 1)
                dve.tensor_copy(sel_b[:], bc(id3b[:], P)).then_inc(cast, 1)
        guidance(nc, tools, xpad, w_guide, ident, ident_b[:], wta, wtb)
        branches(nc, tools, xpad, wta, wtb, sel_a, sel_b, w_scale, y)
        batch_norm_add(nc, tools, y, gb, x)


def batch_norm_add(nc, tools, y, gb, x):
    with ExitStack() as ctx:
        stats = tools.sb(ctx, "bn_stats", [P, N // CH, 6])
        mv = tools.sb(ctx, "bn_mv", [P, 2])
        tmp = tools.sb(ctx, "bn_tmp", [P, 1])
        s = tools.sb(ctx, "bn_scale", [P, 1])
        t = tools.sb(ctx, "bn_shift", [P, 1])
        step = tools.sem(ctx, "bn_step")
        var_ready = tools.sem(ctx, "bn_var_ready")
        rooted = tools.sem(ctx, "bn_rooted")
        affine = tools.sem(ctx, "bn_affine")
        normed = tools.sem(ctx, "bn_normed")
        xf = x.rearrange("p b n -> p (b n)")
        block = ctx.enter_context(nc.Block())

        @block.vector
        def _(dve):
            chain = Chain(dve, step)
            for q in range(N // CH):
                last = dve.bn_stats(stats[:, q, :], y[:, q * CH:(q + 1) * CH])
            chain(last)
            chain(dve.bn_aggr(mv[:], stats.rearrange("p q s -> p (q s)")))
            inv_sqrt(dve, None, chain, mv[:, 1:2], tmp[:], s[:], var_ready, rooted)
            chain(dve.tensor_tensor(s[:], s[:], gb[:, 0:1], ALU.mult))
            chain(dve.tensor_tensor(t[:], mv[:, 0:1], s[:], ALU.mult))
            chain(dve.tensor_tensor(t[:], gb[:, 1:2], t[:], ALU.subtract))
            dve.sem_inc(affine, 1)
            for b in range(B):
                dve.wait_ge(normed, b + 1)
                dve.tensor_tensor(x[:, b, :], x[:, b, :], y[:, b * HW:(b + 1) * HW], ALU.add)

        @block.scalar
        def _(act):
            act.wait_ge(var_ready, 1)
            act.sqrt(tmp[:], mv[:, 1:2]).then_inc(rooted, 1)
            act.wait_ge(affine, 1)
            for b in range(B):
                v = y[:, b * HW:(b + 1) * HW]
                act.activation(v, v, ACT.Identity, bias=t[:], scale=s[:]).then_inc(normed, 1)


def codebook_parts(nc, tools, a, ch, cl, nc2, half_norms):
    SLOTS = 2
    with ExitStack() as ctx:
        ct = tools.sb(ctx, "codes_t", [P, SLOTS, PER * P])
        cn = tools.sb(ctx, "codes_n", [P, SLOTS, PER * P])
        junk = tools.sb(ctx, "squares", [P, PER, P])
        c2 = tools.sb(ctx, "c2", [P, GROUPS * PER])
        ct_in = [tools.sem(ctx, "codes_t_in") for _ in range(SLOTS)]
        cn_in = [tools.sem(ctx, "codes_n_in") for _ in range(SLOTS)]
        high = tools.sem(ctx, "high_ready")
        low = tools.sem(ctx, "low_ready")
        squared = tools.sem(ctx, "squared")
        halved = tools.sem(ctx, "halved")
        stored = tools.sem(ctx, "half_norms_stored")
        block = ctx.enter_context(nc.Block())

        @block.sync
        def _(sp):
            for g in range(GROUPS):
                s = g % SLOTS
                if g >= SLOTS:
                    sp.wait_ge(low, g - SLOTS + 1)
                    sp.wait_ge(squared, PER * (g - SLOTS + 1))
                sp.dma_start(ct[:, s, :], a["codes_t"][:, g, :]).then_inc(ct_in[s], 16)
                sp.dma_start(cn[:, s, :], a["codes"][g * P:(g + 1) * P, :]).then_inc(cn_in[s], 16)
            sp.wait_ge(halved, 2)
            sp.dma_start(half_norms.rearrange("(g p) j -> p g j", p=P),
                         c2.rearrange("p (g j) -> p g j", g=GROUPS)).then_inc(stored, 16)
            sp.wait_ge(stored, 16)

        @block.scalar
        def _(act):
            for g in range(GROUPS):
                act.wait_ge(cn_in[g % SLOTS], 16 * (g // SLOTS + 1))
                if g:
                    act.wait_ge(squared, PER * g)
                for j in range(PER):
                    act.activation(junk[:, j, :], cn[:, g % SLOTS, j * P:(j + 1) * P], ACT.Square,
                                   accum_out=c2[:, g * PER + j:g * PER + j + 1]).then_inc(squared, 1)

        @block.vector
        def _(dve):
            for g in range(GROUPS):
                sl = slice(g * PER * P, (g + 1) * PER * P)
                dve.wait_ge(ct_in[g % SLOTS], 16 * (g // SLOTS + 1))
                dve.tensor_copy(ch[:, sl], ct[:, g % SLOTS, :]).then_inc(high, 1)
                dve.wait_ge(high, g + 1)
                dve.tensor_tensor(cl[:, sl], ct[:, g % SLOTS, :], ch[:, sl], ALU.subtract).then_inc(low, 1)
            dve.wait_ge(squared, GROUPS * PER)
            dve.tensor_scalar(nc2, c2[:], -0.5, None, ALU.mult).then_inc(halved, 1)
            dve.wait_ge(halved, 1)
            dve.tensor_scalar(c2[:], c2[:], 0.5, None, ALU.mult).then_inc(halved, 1)


def normed_parts(nc, tools, x, scale, shift, z, zh, zl):
    with ExitStack() as ctx:
        normed = tools.sem(ctx, "z_ready")
        high = tools.sem(ctx, "zh_ready")
        block = ctx.enter_context(nc.Block())

        @block.scalar
        def _(act):
            for b in range(B):
                act.activation(z[:, b * HW:(b + 1) * HW], x[:, b, :], ACT.Identity,
                               bias=shift[:, b:b + 1], scale=scale[:, b:b + 1]).then_inc(normed, 1)

        @block.vector
        def _(dve):
            for b in range(B):
                v = slice(b * HW, (b + 1) * HW)
                dve.wait_ge(normed, b + 1)
                dve.tensor_copy(zh[:, v], z[:, v]).then_inc(high, 1)
                dve.wait_ge(high, b + 1)
                dve.tensor_tensor(zl[:, v], z[:, v], zh[:, v], ALU.subtract)


def search(nc, tools, a, half_norms, ident, z, zh, zl, ch, cl, nc2, x):
    SCORES, TILES_PX = 4, PX // P
    with ExitStack() as ctx:
        score = [tools.ps(ctx, "score", [P, PX]) for _ in range(SCORES)]
        turn_ps = [tools.ps(ctx, "turn_ps", [P, TILES_PX, P]) for _ in range(2)]
        zt_ps = tools.ps(ctx, "zt_ps", [P, TILES_PX, P])
        zq_ps = tools.ps(ctx, "zq_ps", [P, TILES_PX * P])
        run = [tools.sb(ctx, "run", [P, PX]) for _ in range(2)]
        maxima = [tools.sb(ctx, "maxima", [P, TILES_PX, GROUPS * P]) for _ in range(2)]
        best = tools.sb(ctx, "best", [P, TILES_PX, 8])
        block_id = tools.sb(ctx, "block_id", [P, TILES_PX, 8], U32)
        zc = tools.sb(ctx, "zc", [P, PX])
        zt = tools.sb(ctx, "zt", [P, TILES_PX, P])
        cand = [tools.sb(ctx, "cand", [P, PER * P]) for _ in range(2)]
        half = tools.sb(ctx, "half", [P, TILES_PX, PER])
        fine = tools.sb(ctx, "fine", [P, TILES_PX, PER])
        fine_best = tools.sb(ctx, "fine_best", [P, TILES_PX, 8])
        fine_id = tools.sb(ctx, "fine_id", [P, TILES_PX, 8], U32)
        code = tools.sb(ctx, "code", [P, TILES_PX], U32)
        zq = tools.sb(ctx, "zq", [P, TILES_PX, P])
        delta = tools.sb(ctx, "delta", [P, PX])

        score_ready = tools.sem(ctx, "score_ready")
        act_took = tools.sem(ctx, "act_took")
        dve_took = tools.sem(ctx, "dve_took")
        turned = tools.sem(ctx, "run_turned")
        kept = tools.sem(ctx, "maxima_kept")
        zc_ready = tools.sem(ctx, "zc_ready")
        zt_turned = tools.sem(ctx, "zt_turned")
        zt_ready = tools.sem(ctx, "zt_ready")
        max_done = tools.sem(ctx, "max_done")
        found = tools.sem(ctx, "found")
        cand_in = [tools.sem(ctx, "cand_in") for _ in range(2)]
        multiplied = tools.sem(ctx, "multiplied")
        sel_step = tools.sem(ctx, "sel_step")
        zq_in = tools.sem(ctx, "zq_in")
        zq_turned = tools.sem(ctx, "zq_turned")
        delta_ready = tools.sem(ctx, "delta_ready")
        added = tools.sem(ctx, "added")
        dve_spare = tools.sem(ctx, "dve_spare")
        pool_spare = tools.sem(ctx, "pool_spare")
        block = ctx.enter_context(nc.Block())

        def schedule(eng, step):
            for g in range(GROUPS):
                step(0, 0, g, True, False)
            with eng.Fori(0, (NPX - 1) // 2) as i:
                for h in range(2):
                    for g in range(GROUPS):
                        step(2 * i + 1 + h, (1 + h) % 2, g, True, True)
            for g in range(GROUPS):
                step(NPX, NPX % 2, g, False, True)

        def first(n):
            return isinstance(n, int) and n == 0

        @block.tensor
        def _(pe):
            def turn(n, g):
                G = n * GROUPS + g
                pe.wait_ge(dve_took, (PER - 1) * (G + 1))
                if not first(n) or g >= 2:
                    pe.wait_ge(kept, G - 1)
                for u in range(TILES_PX):
                    mm = pe.transpose(turn_ps[g % 2][:, u, :], run[g % 2][:, u * P:(u + 1) * P], ident)
                mm.then_inc(turned, 1)

            def step(n, par, g, main, post):
                G = n * GROUPS + g
                if main:
                    for j in range(PER):
                        if j == SCORES:
                            pe.wait_ge(act_took, G + 1)
                        elif j > SCORES:
                            pe.wait_ge(dve_took, (PER - 1) * G + j - SCORES)
                        elif not first(n) or g > 0:
                            pe.wait_ge(dve_took, (PER - 1) * (G - 1) + j + SCORES)
                        w = slice((g * PER + j) * P, (g * PER + j + 1) * P)
                        at = bass.ds(n * PX, PX)
                        o = score[j % SCORES][:]
                        pe.matmul(o, ch[:, w], zh[:, at], start=True, stop=False)
                        pe.matmul(o, ch[:, w], zl[:, at], start=False, stop=False)
                        pe.matmul(o, cl[:, w], zh[:, at], start=False, stop=True).then_inc(score_ready, 1)
                if main and g > 0:
                    turn(n, g - 1)
                elif g == 0 and post:
                    turn(n - 1, GROUPS - 1)
                if post and g == 1:
                    pe.wait_ge(zc_ready, n)
                    for u in range(TILES_PX):
                        mm = pe.transpose(zt_ps[:, u, :], zc[:, u * P:(u + 1) * P], ident)
                    mm.then_inc(zt_turned, 1)
                if post and g == GROUPS - 1:
                    pe.wait_ge(zq_in, 16 * TILES_PX * n)
                    for u in range(TILES_PX):
                        mm = pe.transpose(zq_ps[:, u * P:(u + 1) * P], zq[:, u, :], ident)
                    mm.then_inc(zq_turned, 1)

            pe.sem_inc(zq_turned, 1)
            schedule(pe, step)

        @block.scalar
        def _(act):
            def step(n, par, g, main, post):
                G = n * GROUPS + g
                if main:
                    old = not first(n) or g >= 2
                    m = g * PER
                    act.wait_ge(score_ready, PER * G + 1)
                    if old:
                        act.wait_ge(turned, G - 1)
                    act.activation(run[g % 2][:], score[0][:], ACT.Identity, bias=nc2[:, m:m + 1])\
                        .then_inc(act_took, 1)
                if (main and g >= 2) or (post and g < 2):
                    pg, ppar = (g - 2) % GROUPS, par if g >= 2 else 1 - par
                    act.wait_ge(turned, G - 1)
                    if pg == 0 and not first(n) and main:
                        act.wait_ge(found, 1 + TILES_PX * (n - 1))
                    act.copy(maxima[ppar][:, :, pg * P:(pg + 1) * P], turn_ps[pg % 2][:]).then_inc(kept, 1)
                if post and g == 0:
                    act.copy(zc[:], z[:, bass.ds((n - 1) * PX, PX)]).then_inc(zc_ready, 1)
                if post and g == 2:
                    act.wait_ge(zt_turned, n)
                    act.copy(zt[:], zt_ps[:]).then_inc(zt_ready, 1)

            schedule(act, step)

        @block.vector
        def _(dve):
            apart = Apart(dve, dve_spare)

            def step(n, par, g, main, post):
                G = n * GROUPS + g
                if main:
                    for j in range(1, PER):
                        m = g * PER + j
                        dve.wait_ge(score_ready, PER * G + j + 1)
                        if j == 1:
                            dve.wait_ge(act_took, G + 1)
                        else:
                            dve.wait_ge(dve_took, (PER - 1) * G + j - 1)
                        dve.scalar_tensor_tensor(run[g % 2][:], score[j % SCORES][:], nc2[:, m:m + 1],
                                                 run[g % 2][:], ALU.add, ALU.max).then_inc(dve_took, 1)
                c = n - 1
                if post and 2 <= g < 2 + TILES_PX:
                    u, v = g - 2, maxima[1 - par][:, g - 2, :]
                    if u == 0:
                        apart.wait_ge(kept, GROUPS * n)
                    dve.max(best[:, u, :], v).then_inc(max_done, 1)
                    apart.wait_ge(max_done, TILES_PX * c + u + 1)
                    dve.max_index(block_id[:, u, :], best[:, u, :], v).then_inc(found, 1)
                if post and g >= 4:
                    u = g - 4
                    at = 1 + 5 * (TILES_PX * c + u)
                    dve.wait_ge(multiplied, TILES_PX * c + u + 1)
                    dve.tensor_reduce(fine[:, u, :], cand[u % 2].rearrange("p (j c) -> p j c", c=P), AX,
                                      ALU.add).then_inc(sel_step, 1)
                    dve.wait_ge(sel_step, at + 1)
                    dve.tensor_tensor(fine[:, u, :], fine[:, u, :], half[:, u, :], ALU.subtract)\
                        .then_inc(sel_step, 1)
                    apart.wait_ge(sel_step, at + 2)
                    dve.max(fine_best[:, u, :], fine[:, u, :]).then_inc(sel_step, 1)
                    apart.wait_ge(sel_step, at + 3)
                    dve.max_index(fine_id[:, u, :], fine_best[:, u, :], fine[:, u, :]).then_inc(sel_step, 1)
                    dve.wait_ge(sel_step, at + 4)
                    dve.wait_ge(found, 1 + TILES_PX * c + u + 1)
                    dve.scalar_tensor_tensor(code[:, u:u + 1], block_id[:, u, 0:1], float(PER),
                                             fine_id[:, u, 0:1], ALU.mult, ALU.add).then_inc(sel_step, 1)
                if post and g == GROUPS - 1:
                    dve.wait_ge(zq_turned, 1 + n)
                    dve.wait_ge(added, 1 + 2 * c)
                    dve.tensor_tensor(delta[:], zq_ps[:], z[:, bass.ds((n - 1) * PX, PX)], ALU.subtract)\
                        .then_inc(delta_ready, 1)

            dve.sem_inc(found, 1)
            dve.sem_inc(sel_step, 1)
            schedule(dve, step)

        @block.gpsimd
        def _(pool):
            apart = Apart(pool, pool_spare)

            def step(n, par, g, main, post):
                G = n * GROUPS + g
                c = n - 1
                if post and 3 <= g < 3 + TILES_PX:
                    u = g - 3
                    pool.wait_ge(cand_in[u % 2], 32 * (2 * c + u // 2 + 1))
                    if u == 0:
                        pool.wait_ge(zt_ready, n)
                    v = cand[u % 2].rearrange("p (j c) -> p j c", c=P)
                    zb = zt[:, u, :].unsqueeze(1).to_broadcast([P, PER, P])
                    pool.tensor_tensor(v, v, zb, ALU.mult).then_inc(multiplied, 1)
                if post and 2 <= g < 2 + TILES_PX:
                    u = g - 2
                    apart.wait_ge(found, 1 + TILES_PX * c + u + 1)
                    if u >= 2:
                        apart.wait_ge(sel_step, 1 + 5 * (TILES_PX * c + u - 2) + 1)
                    else:
                        apart.wait_ge(sel_step, 1 + 5 * TILES_PX * c)
                    off = bass.IndirectOffsetOnAxis(block_id[:, u, 0:1], 0)
                    pool.indirect_dma_start(cand[u % 2][:], None, a["codes"], off).then_inc(cand_in[u % 2], 16)
                    pool.indirect_dma_start(half[:, u, :], None, half_norms, off).then_inc(cand_in[u % 2], 16)
                if post and g >= 4:
                    u = g - 4
                    apart.wait_ge(sel_step, 1 + 5 * (TILES_PX * c + u + 1))
                    if u == 0:
                        apart.wait_ge(zq_turned, 1 + c)
                    pool.indirect_dma_start(zq[:, u, :], None, a["codes"].rearrange("r (j c) -> (r j) c", c=P),
                                            bass.IndirectOffsetOnAxis(code[:, u:u + 1], 0)).then_inc(zq_in, 16)
                if post and g == GROUPS - 1:
                    at = bass.ds((n - 1) * PX, PX)
                    pool.wait_ge(delta_ready, n)
                    pool.tensor_tensor(delta[:], delta[:], z[:, at], ALU.add).then_inc(added, 1)
                    pool.wait_ge(added, 1 + 2 * c + 1)
                    pool.tensor_tensor(x[:, at], x[:, at], delta[:], ALU.add).then_inc(added, 1)

            pool.sem_inc(added, 1)
            schedule(pool, step)


def layer1(nc, tools, a, x, gm32, ident, scale, shift):
    with ExitStack() as ctx:
        z = tools.sb(ctx, "z", [P, N])
        zh = tools.sb(ctx, "zh", [P, N], BF16)
        zl = tools.sb(ctx, "zl", [P, N], BF16)
        ch = tools.sb(ctx, "ch", [P, CODES], BF16)
        cl = tools.sb(ctx, "cl", [P, CODES], BF16)
        nc2 = tools.sb(ctx, "nc2", [P, GROUPS * PER])
        half_norms = nc.dram_tensor("half_norms", [CODES // PER, PER], F32).ap()
        group_norm_scale(nc, tools, x, gm32, scale, shift)
        normed_parts(nc, tools, x, scale, shift, z, zh, zl)
        codebook_parts(nc, tools, a, ch, cl, nc2[:], half_norms)
        search(nc, tools, a, half_norms, ident, z, zh, zl, ch, cl, nc2, x.rearrange("p b n -> p (b n)"))


def layer2(nc, tools, a, x, xpad, gm32, scale, shift):
    with ExitStack() as ctx:
        wk = tools.sb(ctx, "wk", [P, TAPS, P])
        bk = tools.sb(ctx, "bk", [P, TAPS])
        kern = tools.sb(ctx, "kern", [P, TAPS, B])
        pooled = tools.sb(ctx, "pooled", [P, B])
        load(nc, tools, [(wk[:], a["wk"]), (bk[:], a["bk"])])
        group_norm_scale(nc, tools, x, gm32, scale, shift, pooled[:])
        apply_padded(nc, tools, x, scale, shift, xpad)
        kps = tools.ps(ctx, "kern_ps", [P, TAPS, B])
        kern_ready = tools.sem(ctx, "kern_ready")
        step = tools.sem(ctx, "kern_step")
        tap_done = [tools.sem(ctx, "tap_done") for _ in range(B)]
        block = ctx.enter_context(nc.Block())

        @block.tensor
        def _(pe):
            for k in range(TAPS):
                mm = pe.matmul(kps[:, k, :], wk[:, k, :], pooled[:], start=True, stop=True)
            mm.then_inc(kern_ready, 1)

        @block.vector
        def _(dve):
            chain = Chain(dve, step)
            dve.wait_ge(kern_ready, 1)
            chain(dve.tensor_tensor(kern[:], kps[:], bc(bk[:], B), ALU.add))
            chain(dve.tensor_scalar(kern[:], kern[:], 0.0, None, ALU.max))
            for k in range(TAPS):
                for b in range(B):
                    v = xpad[:, 0:B * PADDED].rearrange("p (b r w) -> p b r w", b=B, w=WP)[
                        :, b, k // 3:k // 3 + H, k % 3:k % 3 + W]
                    xb = x[:, b, :].rearrange("p (r w) -> p r w", w=W)
                    if k:
                        dve.wait_ge(tap_done[b], k)
                    dve.scalar_tensor_tensor(xb, v, kern[:, k, b:b + 1], xb, ALU.mult, ALU.add)\
                        .then_inc(tap_done[b], 1)


TABLE_PAD = W + 1
CORNERS = 4


def sampling_table(nc, tools, a, s, xpad, ident, table, pos):
    with ExitStack() as ctx:
        w_off = tools.sb(ctx, "w_off", [P, TAPS, 2 * TAPS])
        b_off = tools.sb(ctx, "b_off", [2 * TAPS, 1])
        base = tools.sb(ctx, "base", [P, TILES, 2 * TAPS])
        load(nc, tools, [(w_off[:], a[f"w_off{s}"]), (b_off[:], a[f"b_off{s}"]), (base[:], a["base"])])
        ops_ = [tools.ps(ctx, "off_ps", [P, 512])[0:2 * TAPS, 0:CH] for _ in range(B)]
        otp = [tools.ps(ctx, "off_t_ps", [P, 512])[:, 0:CH].rearrange("p (t n) -> p t n", t=TPC) for _ in range(B)]
        xtp = [tools.ps(ctx, "x_t_ps", [P, 512])[:, 0:CH].rearrange("p (t n) -> p t n", t=TPC) for _ in range(B)]
        osb = tools.sb(ctx, "off_sb", [P, B, CH])
        xc = tools.sb(ctx, "x_chunk", [P, B, CH])
        xt = tools.sb(ctx, "x_turned", [P, B, TPC, P])
        zeroed = tools.sem(ctx, "off_sb_zeroed")
        conv_done = tools.sem(ctx, "off_conv_done")
        off_saved = tools.sem(ctx, "off_saved")
        chunk_ready = tools.sem(ctx, "chunk_ready")
        x_turned = tools.sem(ctx, "x_turned")
        x_saved = tools.sem(ctx, "x_saved")
        off_turned = tools.sem(ctx, "off_turned")
        pos_ready = tools.sem(ctx, "pos_ready")
        ends_stored = tools.sem(ctx, "table_ends_stored")
        stored = [tools.sem(ctx, "table_stored") for _ in range(B)]
        block = ctx.enter_context(nc.Block())

        @block.gpsimd
        def _(pool):
            pool.memset(osb[:], 0.0).then_inc(zeroed, 1)
            pool.memset(xt[0:TABLE_PAD, 0], 0.0).then_inc(zeroed, 1)
            pool.memset(xt[0:TABLE_PAD, 1], 0.0).then_inc(zeroed, 1)

        @block.tensor
        def _(pe):
            pe.sem_inc(off_saved, B)
            pe.sem_inc(x_saved, B)
            pe.sem_inc(pos_ready, B)
            with pe.Fori(0, NCH) as r:
                for b in range(B):
                    pe.wait_ge(chunk_ready, B * r + b + 1)
                    pe.wait_ge(x_saved, B * r + b + 1)
                    for t in range(TPC):
                        mm = pe.transpose(xtp[b][:, t, :], xc[:, b, t * P:(t + 1) * P], ident)
                    mm.then_inc(x_turned, 1)
                for b in range(B):
                    pe.wait_ge(off_saved, B * r + b + 1)
                    for t in range(TAPS):
                        at = b * PADDED + r * (ROWS * WP) + (t // 3) * WP + t % 3
                        win = xpad[:, bass.ds(at, ROWS * WP)].rearrange("p (r w) -> p r w", w=WP)[:, :, 0:W]
                        mm = pe.matmul(ops_[b], w_off[:, t, :], win, start=t == 0, stop=t == TAPS - 1)
                    mm.then_inc(conv_done, 1)
                for b in range(B):
                    pe.wait_ge(off_saved, B * (r + 1) + b + 1)
                    pe.wait_ge(pos_ready, B * r + b + 1)
                    for t in range(TPC):
                        mm = pe.transpose(otp[b][:, t, :], osb[:, b, t * P:(t + 1) * P], ident)
                    mm.then_inc(off_turned, 1)

        @block.scalar
        def _(act):
            act.wait_ge(zeroed, 3)
            act.wait_ge(ends_stored, 32)
            for b in range(B):
                act.sem_inc(stored[b], 16 * CORNERS)
            with act.Fori(0, NCH) as r:
                for b in range(B):
                    act.wait_ge(x_turned, B * r + b + 1)
                    act.wait_ge(stored[b], 16 * CORNERS * (r + 1))
                    act.copy(xt[:, b], xtp[b]).then_inc(x_saved, 1)
                for b in range(B):
                    act.wait_ge(conv_done, B * r + b + 1)
                    act.activation(osb[0:2 * TAPS, b, :], ops_[b], ACT.Identity, bias=b_off[:])\
                        .then_inc(off_saved, 1)

        @block.vector
        def _(dve):
            with dve.Fori(0, NCH) as r:
                for b in range(B):
                    at = b * PADDED + (r * ROWS + 1) * WP + 1
                    v = xpad[:, bass.ds(at, ROWS * WP)].rearrange("p (r w) -> p r w", w=WP)[:, :, 0:W]
                    dve.tensor_copy(xc[:, b].rearrange("p (r w) -> p r w", w=W), v).then_inc(chunk_ready, 1)
                for b in range(B):
                    dve.wait_ge(off_turned, B * r + b + 1)
                    at = bass.ds((b * NCH + r) * TPC * 2 * TAPS, TPC * 2 * TAPS)
                    dve.tensor_tensor(pos[:, at].rearrange("p (t k) -> p t k", t=TPC), otp[b][:, :, 0:2 * TAPS],
                                      base.rearrange("p t k -> p (t k)")[:, at].rearrange("p (t k) -> p t k", t=TPC),
                                      ALU.add).then_inc(pos_ready, 1)

        @block.sync
        def _(sp):
            flat = table.rearrange("n s c -> n (s c)")
            sp.wait_ge(zeroed, 3)
            zeros = xt.rearrange("p b t c -> p (b t c)")[0:TABLE_PAD, 0:CORNERS * P]
            sp.dma_start(flat[0:TABLE_PAD, :], zeros).then_inc(ends_stored, 16)
            sp.dma_start(flat[N:N + TABLE_PAD, :], zeros).then_inc(ends_stored, 16)
            with sp.Fori(0, NCH) as r:
                for b in range(B):
                    sp.wait_ge(x_saved, B * (r + 1) + b + 1)
                    for s_ in range(CORNERS):
                        at = TABLE_PAD + b * HW + r * CH - (s_ // 2 * W + s_ % 2)
                        to = flat[bass.ds(at, CH), s_ * P:(s_ + 1) * P].rearrange("(t p) c -> p t c", p=P)
                        sp.dma_start(to, xt[:, b]).then_inc(stored[b], 16)
            for b in range(B):
                sp.wait_ge(stored[b], 16 * CORNERS * (NCH + 1))


def corner_weights(nc, tools, pos, weights, index):
    M = TILES * TAPS
    with ExitStack() as ctx:
        low = tools.sb(ctx, "low", [P, 2 * M])
        side = tools.sb(ctx, "side_weights", [P, 2 * M, 2])
        step = tools.sem(ctx, "corner_step")
        block = ctx.enter_context(nc.Block())

        @block.vector
        def _(dve):
            chain = Chain(dve, step)
            chain(dve.tensor_scalar(low[:], pos, -0.5, 0.0, ALU.add, ALU.max))
            chain(dve.tensor_scalar(low[:], low[:], float(H - 2), ROUND, ALU.min, ALU.add))
            chain(dve.tensor_scalar(low[:], low[:], -ROUND, None, ALU.add))
            chain(dve.tensor_tensor(pos, pos, low[:], ALU.subtract))
            chain(dve.tensor_scalar(side[:, :, 0], pos, -1.0, 1.0, ALU.mult, ALU.add))
            chain(dve.tensor_scalar(side[:, :, 1], pos, -1.0, 2.0, ALU.mult, ALU.add))
            chain(dve.scalar_tensor_tensor(side[:, :, 0], pos, 1.0, side[:, :, 0], ALU.add, ALU.min))
            chain(dve.tensor_tensor(side[:, :, 1], pos, side[:, :, 1], ALU.min))
            chain(dve.tensor_scalar(side[:], side[:], 0.0, None, ALU.max))
            lo = low.rearrange("p (m a) -> p m a", a=2)
            chain(dve.scalar_tensor_tensor(pos[:, 0:M], lo[:, :, 0], float(W), lo[:, :, 1], ALU.mult, ALU.add))
            for b in range(B):
                half = slice(b * M // B, (b + 1) * M // B)
                chain(dve.tensor_scalar(index[:, half], pos[:, half], float(TABLE_PAD + b * HW), None, ALU.add))
            sd = side.rearrange("p (m a) s -> p m a s", a=2)
            for dy in range(2):
                yw = sd[:, :, 0, dy:dy + 1].to_broadcast([P, M, 2])
                chain(dve.tensor_tensor(weights.rearrange("p (m d s) -> p m d s", d=2, s=2)[:, :, dy, :],
                                        sd[:, :, 1, :], yw, ALU.mult))


def sample_and_mix(nc, tools, w_tap, ident, table, weights, index, y):
    SLOTS = 2
    QUAD = CORNERS * P
    with ExitStack() as ctx:
        quads = [tools.sb(ctx, "quads", [P, TAPS, QUAD]) for _ in range(SLOTS)]
        pairs = tools.sb(ctx, "pairs", [P, TAPS, 2 * P])
        sampled = [tools.sb(ctx, "sampled", [P, TAPS, P]) for _ in range(SLOTS)]
        turned = [tools.sb(ctx, "sampled_t", [P, 3, 3 * P]) for _ in range(SLOTS)]
        idx = [tools.sb(ctx, "tile_index", [P, TAPS], U32) for _ in range(SLOTS)]
        tps = [tools.ps(ctx, "sampled_t_ps", [P, 3, 512]) for _ in range(SLOTS)]
        yps = [tools.ps(ctx, "mixed_ps", [P, 512])[:, 0:P] for _ in range(SLOTS)]
        idx_ready = tools.sem(ctx, "idx_ready")
        quads_in = [tools.sem(ctx, "quads_in") for _ in range(SLOTS)]
        weighted = tools.sem(ctx, "weighted")
        quads_free = tools.sem(ctx, "quads_free")
        sampled_ready = tools.sem(ctx, "sampled_ready")
        turn_done = tools.sem(ctx, "turn_done")
        turn_saved = tools.sem(ctx, "turn_saved")
        mixed = tools.sem(ctx, "mixed")
        y_saved = tools.sem(ctx, "y_saved")
        pool_spare = tools.sem(ctx, "pool_spare")
        ROUNDS = TILES // SLOTS
        block = ctx.enter_context(nc.Block())

        @block.gpsimd
        def _(pool):
            apart = Apart(pool, pool_spare)
            pool.sem_inc(quads_free, SLOTS)
            src = table.rearrange("n s c -> n (s c)")
            with pool.Fori(0, ROUNDS) as i:
                for s in range(SLOTS):
                    t = SLOTS * i + s
                    apart.wait_ge(quads_free, t + 1)
                    pool.tensor_copy(idx[s][:], index[:, bass.ds(t * TAPS, TAPS)]).then_inc(idx_ready, 1)
                    apart.wait_ge(idx_ready, t + 1)
                    for k in range(TAPS):
                        pool.indirect_dma_start(quads[s][:, k, :], None, src,
                                                bass.IndirectOffsetOnAxis(idx[s][:, k:k + 1], 0))\
                            .then_inc(quads_in[s], 16)

        @block.vector
        def _(dve):
            dve.sem_inc(turn_done, SLOTS)
            dve.sem_inc(sampled_ready, 1)
            with dve.Fori(0, ROUNDS) as i:
                for s in range(SLOTS):
                    t = SLOTS * i + s
                    q4 = quads[s].rearrange("p k (j c) -> p (k j) c", c=P)
                    w = weights[:, bass.ds(t * TAPS * CORNERS, TAPS * CORNERS)]
                    dve.wait_ge(quads_in[s], 16 * TAPS * (i + 1))
                    dve.tensor_tensor(q4, q4, bc(w, P), ALU.mult).then_inc(weighted, 1)
                    dve.wait_ge(weighted, t + 1)
                    dve.wait_ge(sampled_ready, t + 1)
                    dve.tensor_tensor(pairs[:], quads[s][:, :, 0:2 * P], quads[s][:, :, 2 * P:], ALU.add)\
                        .then_inc(quads_free, 1)
                    dve.wait_ge(quads_free, SLOTS + t + 1)
                    dve.wait_ge(turn_done, t + 1)
                    dve.tensor_tensor(sampled[s][:], pairs[:, :, 0:P], pairs[:, :, P:], ALU.add)\
                        .then_inc(sampled_ready, 1)

        @block.tensor
        def _(pe):
            pe.sem_inc(turn_saved, SLOTS)
            pe.sem_inc(y_saved, SLOTS)
            with pe.Fori(0, ROUNDS) as i:
                for s in range(SLOTS):
                    t = SLOTS * i + s
                    pe.wait_ge(sampled_ready, t + 2)
                    pe.wait_ge(turn_saved, t + 1)
                    for k in range(TAPS):
                        mm = pe.transpose(tps[s][:, k // 3, k % 3 * P:(k % 3 + 1) * P], sampled[s][:, k, :], ident)
                    mm.then_inc(turn_done, 1)
                    pe.wait_ge(turn_saved, SLOTS + t + 1)
                    pe.wait_ge(y_saved, t + 1)
                    for k in range(TAPS):
                        mm = pe.matmul(yps[s], w_tap[:, k, :], turned[s][:, k // 3, k % 3 * P:(k % 3 + 1) * P],
                                       start=k == 0, stop=k == TAPS - 1)
                    mm.then_inc(mixed, 1)

        @block.scalar
        def _(act):
            act.sem_inc(mixed, SLOTS)
            with act.Fori(0, ROUNDS) as i:
                for s in range(SLOTS):
                    t = SLOTS * i + s
                    act.wait_ge(turn_done, SLOTS + t + 1)
                    act.wait_ge(mixed, t + 1)
                    act.copy(turned[s][:], tps[s][:, :, 0:3 * P]).then_inc(turn_saved, 1)
                    act.wait_ge(mixed, SLOTS + t + 1)
                    act.copy(y[:, bass.ds(t * P, P)], yps[s]).then_inc(y_saved, 1)


def layer3(nc, tools, a, x, xpad, gm32, gm8, ident, scale, shift):
    with ExitStack() as ctx:
        y = tools.sb(ctx, "y3", [P, B, HW])
        w_tap = tools.sb(ctx, "w_tap", [P, TAPS, P])
        gn = tools.sb(ctx, "gn_sb", [P, 2])
        pos = tools.sb(ctx, "pos", [P, TILES * TAPS * 2])
        weights = tools.sb(ctx, "weights", [P, TILES * TAPS * CORNERS])
        index = tools.sb(ctx, "index", [P, TILES * TAPS], U32)
        group_norm_scale(nc, tools, x, gm32, scale, shift)
        apply_padded(nc, tools, x, scale, shift, xpad)
        for s in (1, 2):
            table = nc.dram_tensor(f"corners{s}", [TABLE_PAD + N, CORNERS, P], F32).ap()
            load(nc, tools, [(w_tap[:], a[f"w_tap{s}"]), (gn[:], a[f"gn{s}"])])
            sampling_table(nc, tools, a, s, xpad, ident, table, pos)
            corner_weights(nc, tools, pos[:], weights, index)
            sample_and_mix(nc, tools, w_tap, ident, table, weights, index, y.rearrange("p b n -> p (b n)"))
            group_norm_scale(nc, tools, y, gm8, scale, shift)
            norm_relu(nc, tools, y, gn, scale, shift, xpad if s == 1 else None, x)


def norm_relu(nc, tools, y, gn, scale, shift, padded, x):
    with ExitStack() as ctx:
        step = tools.sem(ctx, "affine_step")
        affine = tools.sem(ctx, "affine_ready")
        relued = tools.sem(ctx, "relued")
        block = ctx.enter_context(nc.Block())

        @block.vector
        def _(dve):
            chain = Chain(dve, step)
            chain(dve.tensor_scalar(scale, scale, gn[:, 0:1], None, ALU.mult))
            chain(dve.tensor_scalar(shift, shift, gn[:, 0:1], gn[:, 1:2], ALU.mult, ALU.add))
            dve.sem_inc(affine, 1)
            if padded is None:
                for b in range(B):
                    dve.wait_ge(relued, b + 1)
                    dve.tensor_tensor(x[:, b, :], x[:, b, :], y[:, b, :], ALU.add)

        @block.scalar
        def _(act):
            act.wait_ge(affine, 1)
            for b in range(B):
                if padded is None:
                    src = to = y[:, b, :]
                else:
                    src = y[:, b, :].rearrange("p (r w) -> p r w", w=W)
                    to = padded[:, 0:B * PADDED].rearrange("p (b r w) -> p b r w", b=B, w=WP)[:, b, 1:H + 1, 1:W + 1]
                act.activation(to, src, ACT.Relu, bias=shift[:, b:b + 1], scale=scale[:, b:b + 1])\
                    .then_inc(relued, 1)


def program(nc, a, out, layers=(0, 1, 2, 3)):
    tools = Tools(nc)
    with ExitStack() as ctx:
        x = tools.sb(ctx, "x", [P, B, HW])
        xpad = tools.sb(ctx, "xpad", [P, B * PADDED + WP])
        ident = tools.sb(ctx, "ident", [P, P])[:]
        gm32 = tools.sb(ctx, "gm32", [P, P])[:]
        gm8 = tools.sb(ctx, "gm8", [P, P])[:]
        scale = tools.sb(ctx, "scale", [P, B])[:]
        shift = tools.sb(ctx, "shift", [P, B])[:]
        zeroed = tools.sem(ctx, "xpad_zeroed")
        stored = tools.sem(ctx, "stored")

        load(nc, tools, [(x[:], a["x"]), (ident, a["ident"]), (gm32, a["gm32"]), (gm8, a["gm8"])])
        with nc.Block() as block:
            @block.gpsimd
            def _(pool):
                pool.memset(xpad[:], 0.0).then_inc(zeroed, 1)

        if 0 in layers:
            layer0(nc, tools, a, x, xpad, gm32, ident, scale, shift)
        if 1 in layers:
            layer1(nc, tools, a, x, gm32, ident, scale, shift)
        if 2 in layers:
            layer2(nc, tools, a, x, xpad, gm32, scale, shift)
        if 3 in layers:
            layer3(nc, tools, a, x, xpad, gm32, gm8, ident, scale, shift)

        with nc.Block() as block:
            @block.sync
            def _(sp):
                sp.dma_start(out, x[:]).then_inc(stored, 16)
                sp.wait_ge(stored, 16)


def layouts(i):
    f = np.float32
    t = np.ascontiguousarray

    def taps(w):
        return t(w.reshape(w.shape[0], P, TAPS).transpose(1, 2, 0))

    n = np.arange(N).reshape(TILES, P).T % HW
    k = np.arange(TAPS)
    base = np.stack([(n // W)[:, :, None] - 1 + k // 3, (n % W)[:, :, None] - 1 + k % 3], -1)
    base = base.reshape(P, TILES, 2 * TAPS)
    return {
        "x": t(i["x"].reshape(B, P, HW).transpose(1, 0, 2)),
        "w_cat": taps(i["L0_conv_W_cat"]),
        "w_scale": t(i["L0_conv_W_scale"].reshape(P, NB + 1, P).transpose(2, 1, 0)),
        "gamma_beta": t(np.stack([i["L0_conv_gamma"], i["L0_conv_beta"]], 1)),
        "codes_t": t(i["L1_conv_codebook"].reshape(GROUPS, P, PER, P).transpose(3, 0, 2, 1))
        .reshape(P, GROUPS, PER * P),
        "codes": i["L1_conv_codebook"].reshape(CODES // PER, PER * P),
        "wk": t(i["L2_conv_Wk"].reshape(P, TAPS, P).transpose(2, 1, 0)),
        "bk": i["L2_conv_bk"].reshape(P, TAPS),
        **{f"w_off{s}": taps(i[f"L3_conv_off{s}_w"]) for s in (1, 2)},
        **{f"b_off{s}": i[f"L3_conv_off{s}_b"].reshape(2 * TAPS, 1) for s in (1, 2)},
        **{f"w_tap{s}": taps(i[f"L3_conv_dw{s}"]) for s in (1, 2)},
        **{f"gn{s}": t(np.stack([i[f"L3_conv_gn{s}_s"], i[f"L3_conv_gn{s}_b"]], 1)) for s in (1, 2)},
        "base": base.astype(f),
        "ident": np.eye(P, dtype=f),
        "gm32": np.kron(np.eye(32), np.full((4, 4), 1 / 4)).astype(f),
        "gm8": np.kron(np.eye(8), np.full((16, 16), 1 / 16)).astype(f),
        "id3a": np.tile(np.eye(NA, dtype=f), (3, 1)),
        "id3b": np.tile(np.eye(TAPS, dtype=f), (3, 1)),
    }


def kernel(**inputs):
    import concourse.bacc as bacc
    from concourse.bass_utils import run_bass_kernel_spmd

    arrays = layouts({k: np.asarray(v) for k, v in inputs.items()})
    nc = bacc.Bacc("TRN2", target_bir_lowering=False, num_devices=1)
    a = {k: nc.dram_tensor(f"in_{k}", v.shape, mybir.dt.from_np(v.dtype), kind="ExternalInput").ap()
         for k, v in arrays.items()}
    out = nc.dram_tensor("out", [P, B, HW], F32, kind="ExternalOutput").ap()
    program(nc, a, out)
    r = run_bass_kernel_spmd(nc, [{f"in_{k}": v for k, v in arrays.items()}], core_ids=[0])
    return r.results[0]["out"].transpose(1, 0, 2).reshape(B, P, H, W)
```

```python
from contextlib import ExitStack

import numpy as np

import concourse.bass as bass
from concourse import mybir

P = 128
B, H, W = 2, 48, 48
HW = H * W
N = B * HW
WP = W + 2
HP = H + 2
PADDED = HP * WP
EPS = 1e-5

ROWS = 8
CH = ROWS * W
NCH = H // ROWS
TPC = CH // P
TILES = N // P
DIL = (1, 6, 12, 24, 36)
NB = len(DIL)
TAPS = 9
NG = NB * TAPS
NA = 4 * TAPS

CODES = 8192
GROUPS = 8
PER = CODES // P // GROUPS
PX = 512
NPX = N // PX

ALU = mybir.AluOpType
ACT = mybir.ActivationFunctionType
AX = mybir.AxisListType.X
F32 = mybir.dt.float32
BF16 = mybir.dt.bfloat16
U32 = mybir.dt.uint32
ROUND = float(2 ** 23)


def bc(ap, n):
    return ap.unsqueeze(len(ap.shape)).to_broadcast([*ap.shape, n])


def overlapped(v, half, rows):
    part, row, col = v.ap
    ap = [list(part), [row[0] * (rows - half), 2], [row[0], half], list(col)]
    return bass.AP(tensor=v.tensor, offset=v.offset, ap=ap)


class Tools:

    def __init__(self, nc):
        self.nc, self.n = nc, 0

    def sb(self, ctx, name, shape, dt=F32):
        self.n += 1
        return ctx.enter_context(self.nc.sbuf_tensor(f"{name}_{self.n}", shape, dt))

    def ps(self, ctx, name, shape, dt=F32):
        self.n += 1
        return ctx.enter_context(self.nc.psum_tensor(f"{name}_{self.n}", shape, dt))

    def sem(self, ctx, name):
        self.n += 1
        return ctx.enter_context(self.nc.semaphore(f"{name}_{self.n}"))


class Apart:

    def __init__(self, eng, spare):
        self.eng, self.spare = eng, spare

    def wait_ge(self, sem, value):
        self.eng.wait_ge(sem, value)
        self.eng.sem_inc(self.spare, 1)


class Chain:

    def __init__(self, eng, sem):
        self.eng, self.sem, self.n = eng, sem, 0

    def __call__(self, ins):
        self.n += 1
        ins.then_inc(self.sem, 1)
        self.eng.wait_ge(self.sem, self.n)


def inv_sqrt(eng, act_eng, chain, var, tmp, out, ready, rooted):
    chain(eng.tensor_scalar(var, var, EPS, None, ALU.add))
    eng.sem_inc(ready, 1)
    eng.wait_ge(rooted, 1)
    chain(eng.reciprocal(out, tmp))
    chain(eng.tensor_tensor(tmp, out, out, ALU.mult))
    chain(eng.tensor_tensor(tmp, tmp, var, ALU.mult))
    chain(eng.tensor_scalar(tmp, tmp, -0.5, 1.5, ALU.mult, ALU.add))
    chain(eng.tensor_tensor(out, out, tmp, ALU.mult))


def group_norm_scale(nc, tools, src, gmat, scale, shift, pooled=None):
    with ExitStack() as ctx:
        stats = tools.sb(ctx, "gn_stats", [P, B, NCH, 6])
        mv = tools.sb(ctx, "gn_mean_var", [P, B, 2])
        mm = tools.sb(ctx, "gn_moments", [P, 2, B])
        gg = tools.sb(ctx, "gn_group", [P, 2, B])
        var = tools.sb(ctx, "gn_var", [P, B])
        tmp = tools.sb(ctx, "gn_tmp", [P, B])
        ps = tools.ps(ctx, "gn_ps", [P, 2, B])
        step = tools.sem(ctx, "gn_step")
        moments_ready = tools.sem(ctx, "gn_moments_ready")
        group_ready = tools.sem(ctx, "gn_group_ready")
        var_ready = tools.sem(ctx, "gn_var_ready")
        rooted = tools.sem(ctx, "gn_rooted")
        block = ctx.enter_context(nc.Block())

        @block.vector
        def _(dve):
            chain = Chain(dve, step)
            for b in range(B):
                for q in range(NCH):
                    last = dve.bn_stats(stats[:, b, q, :], src[:, b, q * CH:(q + 1) * CH])
            chain(last)
            for b in range(B):
                chain(dve.bn_aggr(mv[:, b, :], stats[:, b, :, :].rearrange("p q s -> p (q s)")))
            chain(dve.tensor_copy(mm[:, 0, :], mv[:, :, 0]))
            chain(dve.tensor_tensor(mm[:, 1, :], mm[:, 0, :], mm[:, 0, :], ALU.mult))
            chain(dve.tensor_tensor(mm[:, 1, :], mm[:, 1, :], mv[:, :, 1], ALU.add))
            dve.sem_inc(moments_ready, 1)
            dve.wait_ge(group_ready, 1)
            chain(dve.tensor_copy(gg[:], ps[:]))
            chain(dve.tensor_tensor(var[:], gg[:, 0, :], gg[:, 0, :], ALU.mult))
            chain(dve.tensor_tensor(var[:], gg[:, 1, :], var[:], ALU.subtract))
            inv_sqrt(dve, None, chain, var[:], tmp[:], scale, var_ready, rooted)
            chain(dve.tensor_tensor(shift, gg[:, 0, :], scale, ALU.mult))
            chain(dve.tensor_scalar(shift, shift, -1.0, None, ALU.mult))
            if pooled is not None:
                chain(dve.tensor_tensor(pooled, mm[:, 0, :], scale, ALU.mult))
                chain(dve.tensor_tensor(pooled, pooled, shift, ALU.add))

        @block.tensor
        def _(pe):
            pe.wait_ge(moments_ready, 1)
            pe.matmul(ps[:], gmat, mm[:], start=True, stop=True).then_inc(group_ready, 1)

        @block.scalar
        def _(act):
            act.wait_ge(var_ready, 1)
            act.sqrt(tmp[:], var[:]).then_inc(rooted, 1)


def apply_padded(nc, tools, src, scale, shift, padded):
    with ExitStack() as ctx:
        done = tools.sem(ctx, "applied")
        block = ctx.enter_context(nc.Block())
        inner = padded[:, 0:B * PADDED].rearrange("p (b r w) -> p b r w", b=B, w=WP)

        @block.vector
        def _(dve):
            dve.tensor_scalar(inner[:, 0, 1:H + 1, 1:W + 1], src[:, 0, :].rearrange("p (r w) -> p r w", w=W),
                              scale[:, 0:1], shift[:, 0:1], ALU.mult, ALU.add).then_inc(done, 1)

        @block.scalar
        def _(act):
            act.activation(inner[:, 1, 1:H + 1, 1:W + 1], src[:, 1, :].rearrange("p (r w) -> p r w", w=W),
                           ACT.Identity, bias=shift[:, 1:2], scale=scale[:, 1:2]).then_inc(done, 1)


def guidance(nc, tools, xpad, w_guide, ident, ident_b, wta, wtb, beside):
    SLOTS = 2
    with ExitStack() as ctx:
        gps = [tools.ps(ctx, "g_ps", [P, 512])[0:NG, 0:CH] for _ in range(SLOTS)]
        gtp = [tools.ps(ctx, "gt_ps", [P, 512])[:, 0:CH].rearrange("p (t n) -> p t n", t=TPC)
               for _ in range(SLOTS)]
        wap = [tools.ps(ctx, "wa_ps", [P, 1024], BF16)[0:3 * NA, 0:CH] for _ in range(SLOTS)]
        wbp = [tools.ps(ctx, "wb_ps", [P, 1024], BF16)[0:3 * TAPS, 0:CH] for _ in range(SLOTS)]
        gsb = tools.sb(ctx, "g_sb", [P, SLOTS, CH])
        mx = tools.sb(ctx, "g_max", [P, SLOTS, TPC * NB])
        e = tools.sb(ctx, "g_exp", [P, SLOTS, TPC * NB, TAPS])
        den = tools.sb(ctx, "g_den", [P, SLOTS, TPC * NB])
        res = tools.sb(ctx, "g_res", [P, SLOTS, TPC, NG])
        wa = tools.sb(ctx, "w_a", [P, SLOTS, TPC, 3, NA], BF16)
        wb = tools.sb(ctx, "w_b", [P, SLOTS, TPC, 3, TAPS], BF16)
        zeroed = tools.sem(ctx, "g_sb_zeroed")
        conv_done = tools.sem(ctx, "conv_done")
        gps_free = tools.sem(ctx, "gps_free")
        g_saved = tools.sem(ctx, "g_saved")
        turned = tools.sem(ctx, "turned")
        step = [tools.sem(ctx, f"soft_step{b}") for b in range(SLOTS)]
        shifted = tools.sem(ctx, "shifted")
        exped = tools.sem(ctx, "exped")
        split_done = tools.sem(ctx, "split_done")
        back = tools.sem(ctx, "turned_back")
        saved = tools.sem(ctx, "weights_saved")
        STEPS = 12
        block = ctx.enter_context(nc.Block())

        @block.gpsimd
        def _(pool):
            pool.memset(gsb[:], 0.0).then_inc(zeroed, 1)
            beside.pool(pool)

        @block.sync
        def _(sp):
            beside.sp(sp)

        @block.tensor
        def _(pe):
            def conv(r, b):
                pe.wait_ge(gps_free, B * r + b + 1)
                for t in range(TAPS):
                    at = b * PADDED + r * (ROWS * WP) + (t // 3) * WP + t % 3
                    win = xpad[:, bass.ds(at, ROWS * WP)].rearrange("p (r w) -> p r w", w=WP)[:, :, 0:W]
                    mm = pe.matmul(gps[b], w_guide[:, t, :], win, start=t == 0, stop=t == TAPS - 1)
                mm.then_inc(conv_done, 1)

            def turn(r):
                for b in range(B):
                    pe.wait_ge(g_saved, B * r + b + 1)
                    for t in range(TPC):
                        mm = pe.transpose(gtp[b][:, t, :], gsb[:, b, t * P:(t + 1) * P], ident)
                    mm.then_inc(turned, 1)

            def turn_back(r):
                for b in range(B):
                    pe.wait_ge(split_done, B * r + b + 1)
                    for t in range(TPC):
                        pe.transpose(wap[b][:, t * P:(t + 1) * P],
                                     wa[:, b, t, :, :].rearrange("p s k -> p (s k)"), ident_b)
                        mm = pe.transpose(wbp[b][:, t * P:(t + 1) * P],
                                          wb[:, b, t, :, :].rearrange("p s k -> p (s k)"), ident_b)
                    mm.then_inc(back, 1)

            pe.sem_inc(gps_free, SLOTS)
            for b in range(B):
                conv(0, b)
            with pe.Fori(0, NCH - 1) as r:
                turn(r)
                conv(r + 1, 0)
                turn_back(r)
                conv(r + 1, 1)
            turn(NCH - 1)
            turn_back(NCH - 1)

        @block.scalar
        def _(act):
            act.wait_ge(zeroed, 1)
            with act.Fori(0, NCH) as r:
                for b in range(B):
                    act.wait_ge(conv_done, B * r + b + 1)
                    act.copy(gsb[0:NG, b, :], gps[b]).then_inc(g_saved, 1)
                    act.wait_ge(g_saved, B * r + b + 1)
                    act.sem_inc(gps_free, 1)
                for b in range(B):
                    act.wait_ge(shifted, B * r + b + 1)
                    act.activation(e[:, b], e[:, b], ACT.Exp).then_inc(exped, 1)
                for b in range(B):
                    act.wait_ge(back, B * r + b + 1)
                    at = b * HW + r * CH
                    act.copy(wta[:, bass.ds(at, CH)], wap[b])
                    act.copy(wtb[:, bass.ds(at, CH)], wbp[b]).then_inc(saved, 1)
                act.wait_ge(saved, B * r + B)

        @block.vector
        def _(dve):
            with dve.Fori(0, NCH) as r:
                def chained(b, n, ins):
                    ins.then_inc(step[b], 1)
                    dve.wait_ge(step[b], STEPS * r + n)

                for b in range(B):
                    dve.wait_ge(turned, B * r + b + 1)
                    g = gtp[b][:, :, 0:NG].rearrange("p t (n k) -> p t n k", k=TAPS)
                    chained(b, 1, dve.tensor_reduce(mx[:, b], g, AX, ALU.max))
                    dve.tensor_tensor(e[:, b].rearrange("p (t n) k -> p t n k", t=TPC), g,
                                      bc(mx[:, b].rearrange("p (t n) -> p t n", t=TPC), TAPS),
                                      ALU.subtract).then_inc(shifted, 1)
                for b in range(B):
                    dve.wait_ge(exped, B * r + b + 1)
                    chained(b, 2, dve.tensor_reduce(den[:, b], e[:, b], AX, ALU.add))
                    chained(b, 3, dve.reciprocal(den[:, b], den[:, b]))
                    r4 = res[:, b].rearrange("p t (n k) -> p (t n) k", k=TAPS)
                    chained(b, 4, dve.tensor_tensor(r4, e[:, b], bc(den[:, b], TAPS), ALU.mult))
                    ra, rb = res[:, b, :, 0:NA], res[:, b, :, NA:NG]
                    dve.tensor_copy(wa[:, b, :, 0, :], ra).then_inc(step[b], 1)
                    chained(b, 6, dve.tensor_copy(wb[:, b, :, 0, :], rb))
                    dve.tensor_tensor(ra, ra, wa[:, b, :, 0, :], ALU.subtract).then_inc(step[b], 1)
                    chained(b, 8, dve.tensor_tensor(rb, rb, wb[:, b, :, 0, :], ALU.subtract))
                    dve.tensor_copy(wa[:, b, :, 1, :], ra).then_inc(step[b], 1)
                    chained(b, 10, dve.tensor_copy(wb[:, b, :, 1, :], rb))
                    dve.tensor_tensor(wa[:, b, :, 2, :], ra, wa[:, b, :, 1, :], ALU.subtract).then_inc(step[b], 1)
                    chained(b, STEPS, dve.tensor_tensor(wb[:, b, :, 2, :], rb, wb[:, b, :, 1, :], ALU.subtract))
                    dve.sem_inc(split_done, 1)


POOLED = 4
DIRECT = (1, 3, 5)


def branch_ops():
    ops = []
    for q in range(H // (2 * ROWS)):
        for i, d in enumerate(DIL):
            taps = []
            for k in range(TAPS):
                dy, dx = (k // 3 - 1) * d, (k % 3 - 1) * d
                r0, r1 = max(2 * ROWS * q, -dy), min(2 * ROWS * (q + 1), H - dy)
                c0, c1 = max(0, -dx), min(W, W - dx)
                if r1 <= r0 or c1 <= c0:
                    continue
                n = r1 - r0
                halves = 1 if n * (c1 - c0) <= 512 else 2
                half = -(-n // halves)
                taps.append(dict(q=q, i=i, k=k, dy=dy, dx=dx, r0=r0, n=n, half=half, halves=halves,
                                 c0=c0, c1=c1, way="pe"))
            if i < POOLED:
                taps.sort(key=lambda o: o["k"] != TAPS // 2)
                whole = [o for o in taps[1:] if o["half"] * o["halves"] == o["n"]]
                odd = len(taps) - 1 - len(whole)
                for m, o in enumerate(whole):
                    if m not in DIRECT[odd:]:
                        o["way"] = "pool"
                taps[0]["way"] = "acc"
            ops += taps
    return ops


def pieces(o):
    out = []
    for h in range(o["halves"]):
        start = o["r0"] + (o["n"] - o["half"]) * h
        at = start if h == 0 else o["r0"] + o["half"]
        while at < start + o["half"]:
            to = min(start + o["half"], (at // ROWS + 1) * ROWS)
            out.append((h, at - start, to - at, at, at // ROWS % 2))
            at = to
    return out


def last_use(m, count, slots):
    return m - slots if m >= slots else max(j for j in range(count) if j % slots == m % slots) - count


def branches(nc, tools, xpad, wta, wtb, sel_a, sel_b, w_scale, y, beside):
    SPREADS, LAG, ACCS, POOLS, DIRECTS = 3, 3, POOLED, 5, 4
    ops = branch_ops()
    M, CHUNKS = len(ops), H // (2 * ROWS)
    ways = {way: [n for n, o in enumerate(ops) if o["way"] == way] for way in ("acc", "pool", "pe")}
    of_way = {n: m for ns in ways.values() for m, n in enumerate(ns)}
    n_acc, n_pool, n_pe = (len(ways[way]) for way in ("acc", "pool", "pe"))
    ends = [max(n for n, o in enumerate(ops) if o["q"] == q) for q in range(CHUNKS)]
    adds = [[n] if o["way"] == "pe" else [] for n, o in enumerate(ops)]
    for n in ways["acc"]:
        q, i = ops[n]["q"], ops[n]["i"]
        at = max(m for m, o in enumerate(ops) if o["q"] == q and o["i"] == i + 1)
        adds[at if i + 1 < POOLED else ends[q]].append(n)
    with ExitStack() as ctx:
        spread = [tools.ps(ctx, "spread", [P, 2, 512]) for _ in range(SPREADS)]
        yps = tools.ps(ctx, "y_ps", [P, 2, 512])
        buf = {way: [tools.sb(ctx, f"prod_{way}", [P, 2 * ROWS * W]) for _ in range(slots)]
               for way, slots in (("acc", ACCS), ("pool", POOLS), ("pe", DIRECTS))}
        spread_ready = tools.sem(ctx, "spread_ready")
        prod_ready = tools.sem(ctx, "prod_ready")
        pooled = tools.sem(ctx, "pooled")
        direct_free = tools.sem(ctx, "direct_free")
        acc_free = tools.sem(ctx, "acc_free")
        y_ready = tools.sem(ctx, "y_ready")
        y_free = tools.sem(ctx, "y_free")
        pe_spare = tools.sem(ctx, "pe_spare")
        block = ctx.enter_context(nc.Block())

        def product(n):
            slots = buf[ops[n]["way"]]
            return slots[of_way[n] % len(slots)]

        @block.tensor
        def _(pe):
            apart = Apart(pe, pe_spare)
            pe.sem_inc(direct_free, DIRECTS)
            pe.sem_inc(acc_free, ACCS)
            with pe.Fori(0, B) as b:
                def spread_op(n):
                    o = ops[n]
                    half, c0, c1 = o["half"], o["c0"], o["c1"]
                    apart.wait_ge(prod_ready, SPREADS + b * M + last_use(n, M, SPREADS) + 1)
                    wt, sel, kk = (wta, sel_a, o["i"] * TAPS + o["k"]) if o["i"] < 4 else (wtb, sel_b, o["k"])
                    for h in range(o["halves"]):
                        at = b * HW + (o["r0"] + (o["n"] - half) * h) * W
                        v = wt[:, bass.ds(at, half * W)].rearrange("p (r w) -> p r w", w=W)[:, :, c0:c1]
                        to = spread[n % SPREADS][:, h, 0:half * (c1 - c0)].rearrange("p (r w) -> p r w", r=half)
                        mm = pe.matmul(to, sel[:, kk, :], v, start=True, stop=True)
                    mm.then_inc(spread_ready, 1)

                def start_chunk(q):
                    pe.wait_ge(y_free, b * CHUNKS + q + 1)
                    for j in range(2):
                        v = xpad[:, bass.ds(b * PADDED + ((2 * q + j) * ROWS + 1) * WP, ROWS * WP)]
                        pe.matmul(yps[:, j, 0:CH].rearrange("p (r w) -> p r w", w=W), w_scale[:, 0, :],
                                  v.rearrange("p (r w) -> p r w", w=WP)[:, :, 1:W + 1], start=True, stop=False,
                                  skip_group_check=True)

                def add_op(n, last):
                    o, m = ops[n], of_way[n]
                    cols = o["c1"] - o["c0"]
                    if o["way"] == "acc":
                        m_last = max(of_way[j] for j in ways["pool"] if (ops[j]["q"], ops[j]["i"]) == (o["q"], o["i"]))
                        pe.wait_ge(pooled, POOLS + b * n_pool + m_last + 1)
                    else:
                        pe.wait_ge(prod_ready, SPREADS + b * M + n + 1)
                    for h, hr, rows, row, bank in pieces(o):
                        src = product(n)[:, (h * o["half"] + hr) * cols:(h * o["half"] + hr + rows) * cols]
                        dst = yps[:, bank, 0:CH].rearrange("p (r w) -> p r w", w=W)[
                            :, row % ROWS:row % ROWS + rows, o["c0"]:o["c1"]]
                        mm = pe.matmul(dst, w_scale[:, o["i"] + 1, :], src.rearrange("p (r w) -> p r w", r=rows),
                                       start=False, stop=last, skip_group_check=True)
                    mm.then_inc(acc_free if o["way"] == "acc" else direct_free, 1)

                for n in range(LAG):
                    spread_op(n)
                begun = -1
                for n in range(M):
                    if n + LAG < M:
                        spread_op(n + LAG)
                    q = ops[n]["q"]
                    for m in adds[n]:
                        if q > begun:
                            start_chunk(q)
                            begun = q
                        add_op(m, last=n == ends[q] and m == adds[n][-1])
                    if n == ends[q]:
                        pe.wait_ge(acc_free, ACCS + b * n_acc + (q + 1) * POOLED)
                        pe.sem_inc(y_ready, 1)

        @block.vector
        def _(dve):
            dve.sem_inc(prod_ready, SPREADS)
            free = {"acc": (acc_free, ACCS, n_acc), "pool": (pooled, POOLS, n_pool), "pe": (direct_free, DIRECTS, n_pe)}
            with dve.Fori(0, B) as b:
                for n, o in enumerate(ops):
                    sem, slots, count = free[o["way"]]
                    dve.wait_ge(sem, slots + b * count + last_use(of_way[n], count, slots) + 1)
                    dve.wait_ge(spread_ready, b * M + n + 1)
                    half, halves, cols = o["half"], o["halves"], o["c1"] - o["c0"]
                    v = xpad[:, bass.ds(b * PADDED + (o["r0"] + o["dy"] + 1) * WP, o["n"] * WP)]
                    v = v.rearrange("p (r w) -> p r w", w=WP)[:, :, o["c0"] + o["dx"] + 1:o["c1"] + o["dx"] + 1]
                    to = product(n)[:, 0:halves * half * cols]
                    w = spread[n % SPREADS]
                    if halves == 1:
                        to = to.rearrange("p (r w) -> p r w", r=half)
                        w = w[:, 0, 0:half * cols].rearrange("p (r w) -> p r w", r=half)
                    else:
                        to = to.rearrange("p (h r w) -> p h r w", h=2, r=half)
                        w = w[:, :, 0:half * cols].rearrange("p h (r w) -> p h r w", r=half)
                        v = overlapped(v, half, o["n"])
                    dve.tensor_tensor(to, w, v, ALU.mult).then_inc(prod_ready, 1)

        @block.sync
        def _(sp):
            beside.sp(sp)

        @block.gpsimd
        def _(pool):
            pool.sem_inc(pooled, POOLS)
            with pool.Fori(0, B) as b:
                acc = None
                for n, o in enumerate(ops):
                    if o["way"] == "acc":
                        acc = product(n).rearrange("p (r w) -> p r w", w=W)
                    if o["way"] != "pool":
                        continue
                    pool.wait_ge(prod_ready, SPREADS + b * M + n + 1)
                    pool.wait_ge(pooled, POOLS + b * n_pool + of_way[n])
                    row, cols = o["r0"] - 2 * ROWS * o["q"], o["c1"] - o["c0"]
                    to = acc[:, row:row + o["n"], o["c0"]:o["c1"]]
                    v = product(n)[:, 0:o["n"] * cols].rearrange("p (r w) -> p r w", w=cols)
                    pool.tensor_tensor(to, to, v, ALU.add).then_inc(pooled, 1)

        @block.scalar
        def _(act):
            act.sem_inc(y_free, 1)
            beside.act(act)
            with act.Fori(0, B) as b:
                for q in range(CHUNKS):
                    act.wait_ge(y_ready, b * CHUNKS + q + 1)
                    to = y[:, bass.ds(b * HW + q * 2 * CH, 2 * CH)].rearrange("p (h n) -> p h n", h=2)
                    act.copy(to, yps[:, :, 0:CH]).then_inc(y_free, 1)


def load(nc, tools, pairs):
    with ExitStack() as ctx:
        loaded = tools.sem(ctx, "loaded")
        with nc.Block() as block:
            @block.sync
            def _(sp):
                for to, src in pairs:
                    sp.dma_start(to, src).then_inc(loaded, 16)
                sp.wait_ge(loaded, 16 * len(pairs))


def layer0(nc, tools, a, x, xpad, gm32, ident, scale, shift, codes):
    with ExitStack() as ctx:
        w_guide = tools.sb(ctx, "w_guide", [P, TAPS, NG])
        w_scale = tools.sb(ctx, "w_scale", [P, NB + 1, P])
        gb = tools.sb(ctx, "gamma_beta", [P, 2])
        ident_b = tools.sb(ctx, "ident_b", [P, P], BF16)
        sel_a = tools.sb(ctx, "sel_a", [3 * NA, NA, P], BF16)
        sel_b = tools.sb(ctx, "sel_b", [3 * TAPS, TAPS, P], BF16)
        id3a = tools.sb(ctx, "id3a", [3 * NA, NA])
        id3b = tools.sb(ctx, "id3b", [3 * TAPS, TAPS])
        wta = tools.sb(ctx, "wta", [3 * NA, N], BF16)
        wtb = tools.sb(ctx, "wtb", [3 * TAPS, N], BF16)
        y = tools.sb(ctx, "y", [P, N])
        cast = tools.sem(ctx, "cast")
        group_norm_scale(nc, tools, x, gm32, scale, shift)
        apply_padded(nc, tools, x, scale, shift, xpad)
        load(nc, tools, [(w_guide[:], a["w_cat"]), (w_scale[:], a["w_scale"]), (gb[:], a["gamma_beta"]),
                         (id3a[:], a["id3a"]), (id3b[:], a["id3b"])])
        with nc.Block() as block:
            @block.vector
            def _(dve):
                dve.tensor_copy(ident_b[:], ident).then_inc(cast, 1)
                dve.tensor_copy(sel_a[:], bc(id3a[:], P)).then_inc(cast, 1)
                dve.tensor_copy(sel_b[:], bc(id3b[:], P)).then_inc(cast, 1)
        ch, cl, nc2, half_norms = codes
        with ExitStack() as parts:
            guidance(nc, tools, xpad, w_guide, ident, ident_b[:], wta, wtb, CodeSplit(nc, tools, parts, a, ch, cl))
        with ExitStack() as parts:
            beside = CodeNorms(nc, tools, parts, a, nc2, half_norms)
            branches(nc, tools, xpad, wta, wtb, sel_a, sel_b, w_scale, y, beside)
        batch_norm_add(nc, tools, y, gb, x)


def batch_norm_add(nc, tools, y, gb, x):
    with ExitStack() as ctx:
        stats = tools.sb(ctx, "bn_stats", [P, N // CH, 6])
        mv = tools.sb(ctx, "bn_mv", [P, 2])
        tmp = tools.sb(ctx, "bn_tmp", [P, 1])
        s = tools.sb(ctx, "bn_scale", [P, 1])
        t = tools.sb(ctx, "bn_shift", [P, 1])
        step = tools.sem(ctx, "bn_step")
        var_ready = tools.sem(ctx, "bn_var_ready")
        rooted = tools.sem(ctx, "bn_rooted")
        affine = tools.sem(ctx, "bn_affine")
        normed = tools.sem(ctx, "bn_normed")
        xf = x.rearrange("p b n -> p (b n)")
        block = ctx.enter_context(nc.Block())

        @block.vector
        def _(dve):
            chain = Chain(dve, step)
            for q in range(N // CH):
                last = dve.bn_stats(stats[:, q, :], y[:, q * CH:(q + 1) * CH])
            chain(last)
            chain(dve.bn_aggr(mv[:], stats.rearrange("p q s -> p (q s)")))
            inv_sqrt(dve, None, chain, mv[:, 1:2], tmp[:], s[:], var_ready, rooted)
            chain(dve.tensor_tensor(s[:], s[:], gb[:, 0:1], ALU.mult))
            chain(dve.tensor_tensor(t[:], mv[:, 0:1], s[:], ALU.mult))
            chain(dve.tensor_tensor(t[:], gb[:, 1:2], t[:], ALU.subtract))
            dve.sem_inc(affine, 1)
            for b in range(B):
                dve.wait_ge(normed, b + 1)
                dve.tensor_tensor(x[:, b, :], x[:, b, :], y[:, b * HW:(b + 1) * HW], ALU.add)

        @block.scalar
        def _(act):
            act.wait_ge(var_ready, 1)
            act.sqrt(tmp[:], mv[:, 1:2]).then_inc(rooted, 1)
            act.wait_ge(affine, 1)
            for b in range(B):
                v = y[:, b * HW:(b + 1) * HW]
                act.activation(v, v, ACT.Identity, bias=t[:], scale=s[:]).then_inc(normed, 1)


class CodeSplit:
    SLOTS = 2

    def __init__(self, nc, tools, ctx, a, ch, cl):
        self.a, self.ch, self.cl = a, ch, cl
        self.ct = tools.sb(ctx, "codes_t", [P, self.SLOTS, PER * P])
        self.ct_in = [tools.sem(ctx, "codes_t_in") for _ in range(self.SLOTS)]
        self.high = tools.sem(ctx, "high_ready")
        self.low = tools.sem(ctx, "low_ready")

    def sp(self, sp):
        for g in range(GROUPS):
            s = g % self.SLOTS
            if g >= self.SLOTS:
                sp.wait_ge(self.low, g - self.SLOTS + 1)
            sp.dma_start(self.ct[:, s, :], self.a["codes_t"][:, g, :]).then_inc(self.ct_in[s], 16)

    def pool(self, pool):
        for g in range(GROUPS):
            s, v = g % self.SLOTS, slice(g * PER * P, (g + 1) * PER * P)
            pool.wait_ge(self.ct_in[s], 16 * (g // self.SLOTS + 1))
            pool.tensor_copy(self.ch[:, v], self.ct[:, s, :]).then_inc(self.high, 1)
            pool.wait_ge(self.high, g + 1)
            pool.tensor_tensor(self.cl[:, v], self.ct[:, s, :], self.ch[:, v], ALU.subtract).then_inc(self.low, 1)


class CodeNorms:
    SLOTS = 2

    def __init__(self, nc, tools, ctx, a, nc2, half_norms):
        self.a, self.nc2, self.half_norms = a, nc2, half_norms
        self.cn = tools.sb(ctx, "codes_n", [P, self.SLOTS, PER * P])
        self.junk = tools.sb(ctx, "squares", [P, PER, P])
        self.c2 = tools.sb(ctx, "c2", [P, GROUPS * PER])
        self.cn_in = [tools.sem(ctx, "codes_n_in") for _ in range(self.SLOTS)]
        self.squared = tools.sem(ctx, "squared")
        self.halved = tools.sem(ctx, "halved")
        self.stored = tools.sem(ctx, "half_norms_stored")

    def sp(self, sp):
        for g in range(GROUPS):
            s = g % self.SLOTS
            if g >= self.SLOTS:
                sp.wait_ge(self.squared, PER * (g - self.SLOTS + 1))
            sp.dma_start(self.cn[:, s, :], self.a["codes"][g * P:(g + 1) * P, :]).then_inc(self.cn_in[s], 16)
        sp.wait_ge(self.halved, 2)
        sp.dma_start(self.half_norms.rearrange("(g p) j -> p g j", p=P),
                     self.c2.rearrange("p (g j) -> p g j", g=GROUPS)).then_inc(self.stored, 16)
        sp.wait_ge(self.stored, 16)

    def act(self, act):
        for g in range(GROUPS):
            s = g % self.SLOTS
            act.wait_ge(self.cn_in[s], 16 * (g // self.SLOTS + 1))
            if g:
                act.wait_ge(self.squared, PER * g)
            for j in range(PER):
                act.activation(self.junk[:, j, :], self.cn[:, s, j * P:(j + 1) * P], ACT.Square,
                               accum_out=self.c2[:, g * PER + j:g * PER + j + 1]).then_inc(self.squared, 1)
        act.wait_ge(self.squared, GROUPS * PER)
        act.mul(self.nc2, self.c2[:], -0.5).then_inc(self.halved, 1)
        act.wait_ge(self.halved, 1)
        act.mul(self.c2[:], self.c2[:], 0.5).then_inc(self.halved, 1)


def normed_parts(nc, tools, x, scale, shift, z, zh, zl):
    with ExitStack() as ctx:
        normed = tools.sem(ctx, "z_ready")
        high = tools.sem(ctx, "zh_ready")
        block = ctx.enter_context(nc.Block())

        @block.scalar
        def _(act):
            for b in range(B):
                act.activation(z[:, b * HW:(b + 1) * HW], x[:, b, :], ACT.Identity,
                               bias=shift[:, b:b + 1], scale=scale[:, b:b + 1]).then_inc(normed, 1)

        @block.vector
        def _(dve):
            for b in range(B):
                v = slice(b * HW, (b + 1) * HW)
                dve.wait_ge(normed, b + 1)
                dve.tensor_copy(zh[:, v], z[:, v]).then_inc(high, 1)
                dve.wait_ge(high, b + 1)
                dve.tensor_tensor(zl[:, v], z[:, v], zh[:, v], ALU.subtract)


def search(nc, tools, a, half_norms, ident, z, zh, zl, ch, cl, nc2, x):
    PXT, STEPS = PX // P, GROUPS // 2
    NPR = 2 * PER
    BY_ACT = 2
    BY_DVE = NPR - BY_ACT
    TURN_AT = 9
    Z_TURN_AT = 12
    SLOT = [0, 1, 2, 3, 0, 4, 1, 2, 0, 3, 4, 1, 0, 2, 3, 4]
    LAST = [max(j for j in range(k - NPR, k) if SLOT[j % NPR] == SLOT[k]) for k in range(NPR)]
    with ExitStack() as ctx:
        score = [tools.ps(ctx, "score", [P, PX]) for _ in range(max(SLOT) + 1)]
        turn_ps = tools.ps(ctx, "turn_ps", [P, 2, PXT, P])
        z_ps = tools.ps(ctx, "z_ps", [P, PXT, P])
        run = [[tools.sb(ctx, "run", [P, PX]) for _ in range(2)] for _ in range(2)]
        maxima = [tools.sb(ctx, "maxima", [P, PXT, GROUPS * P]) for _ in range(2)]
        best = tools.sb(ctx, "best", [P, PXT, 8])
        block_id = tools.sb(ctx, "block_id", [P, PXT, 8], U32)
        zc = tools.sb(ctx, "zc", [P, PX])
        zt = tools.sb(ctx, "zt", [P, PXT, P])
        cand = [tools.sb(ctx, "cand", [P, PER * P]) for _ in range(2)]
        half = tools.sb(ctx, "half", [P, PXT, PER])
        fine = tools.sb(ctx, "fine", [P, PXT, PER])
        fine_best = tools.sb(ctx, "fine_best", [P, PXT, 8])
        fine_id = tools.sb(ctx, "fine_id", [P, PXT, 8], U32)
        code = tools.sb(ctx, "code", [P, PXT], U32)
        zq = tools.sb(ctx, "zq", [P, PXT, P])
        delta = tools.sb(ctx, "delta", [P, PX])

        score_ready = tools.sem(ctx, "score_ready")
        act_took = tools.sem(ctx, "act_took")
        dve_took = tools.sem(ctx, "dve_took")
        turned = tools.sem(ctx, "runs_turned")
        kept = tools.sem(ctx, "maxima_kept")
        zc_ready = tools.sem(ctx, "zc_ready")
        zt_turned = tools.sem(ctx, "zt_turned")
        zt_ready = tools.sem(ctx, "zt_ready")
        max_done = tools.sem(ctx, "max_done")
        found = tools.sem(ctx, "found")
        cand_in = [tools.sem(ctx, "cand_in") for _ in range(2)]
        multiplied = tools.sem(ctx, "multiplied")
        summed = tools.sem(ctx, "summed")
        sel_step = tools.sem(ctx, "sel_step")
        zq_in = tools.sem(ctx, "zq_in")
        zq_turned = tools.sem(ctx, "zq_turned")
        delta_ready = tools.sem(ctx, "delta_ready")
        added = tools.sem(ctx, "added")
        dve_spare = tools.sem(ctx, "dve_spare")
        pool_spare = tools.sem(ctx, "pool_spare")
        block = ctx.enter_context(nc.Block())

        def schedule(eng, step):
            for s in range(STEPS):
                step(0, 0, s, True, False)
            with eng.Fori(0, (NPX - 1) // 2) as i:
                for h in range(2):
                    for s in range(STEPS):
                        step(2 * i + 1 + h, (1 + h) % 2, s, True, True)
            for s in range(STEPS):
                step(NPX, NPX % 2, s, False, True)

        def first(n):
            return isinstance(n, int) and n == 0

        @block.tensor
        def _(pe):
            def turn(n, s):
                S = n * STEPS + s
                pe.wait_ge(dve_took, BY_DVE * (S + 1))
                if not first(n) or s >= 1:
                    pe.wait_ge(kept, S)
                for h in range(2):
                    for u in range(PXT):
                        mm = pe.transpose(turn_ps[:, h, u, :], run[s % 2][h][:, u * P:(u + 1) * P], ident)
                mm.then_inc(turned, 1)

            def turn_z(n):
                pe.wait_ge(zc_ready, n)
                pe.wait_ge(delta_ready, n)
                for u in range(PXT):
                    mm = pe.transpose(z_ps[:, u, :], zc[:, u * P:(u + 1) * P], ident)
                mm.then_inc(zt_turned, 1)

            def step(n, par, s, main, post):
                S = n * STEPS + s
                for k in range(NPR if main else 0):
                    last = LAST[k]
                    if last >= BY_ACT:
                        pe.wait_ge(dve_took, BY_DVE * S + last - BY_ACT + 1)
                    elif last >= 0:
                        pe.wait_ge(act_took, BY_ACT * S + last + 1)
                    elif not first(n) or s > 0:
                        pe.wait_ge(dve_took, BY_DVE * S + last + 1)
                    m = (2 * s + k % 2) * PER + k // 2
                    w = slice(m * P, (m + 1) * P)
                    at = bass.ds(n * PX, PX)
                    o = score[SLOT[k]][:]
                    pe.matmul(o, ch[:, w], zh[:, at], start=True, stop=False)
                    pe.matmul(o, ch[:, w], zl[:, at], start=False, stop=False)
                    pe.matmul(o, cl[:, w], zh[:, at], start=False, stop=True).then_inc(score_ready, 1)
                    if k == TURN_AT and (s or not first(n)):
                        turn(n, s - 1)
                    if k == Z_TURN_AT and post and s == 0:
                        turn_z(n)
                if not main and s == 0:
                    turn(n, -1)
                if post and s == 0 and not main:
                    turn_z(n)
                if post and s == STEPS - 1:
                    pe.wait_ge(zq_in, 16 * PXT * n)
                    for u in range(PXT):
                        mm = pe.transpose(z_ps[:, u, :], zq[:, u, :], ident)
                    mm.then_inc(zq_turned, 1)

            pe.sem_inc(zq_turned, 1)
            schedule(pe, step)

        @block.scalar
        def _(act):
            def sum_products(n, u):
                act.wait_ge(multiplied, PXT * (n - 1) + u + 1)
                for j in range(PER):
                    v = cand[u % 2][:, j * P:(j + 1) * P]
                    act.activation(v, v, ACT.Identity, accum_out=fine[:, u, j:j + 1]).then_inc(summed, 1)

            def step(n, par, s, main, post):
                S = n * STEPS + s
                if main:
                    if not first(n) or s >= 2:
                        act.wait_ge(turned, S - 1)
                    for k in range(BY_ACT):
                        m = (2 * s + k) * PER
                        act.wait_ge(score_ready, NPR * S + k + 1)
                        act.activation(run[s % 2][k][:], score[SLOT[k]][:], ACT.Identity, bias=nc2[:, m:m + 1])\
                            .then_inc(act_took, 1)
                if post and s == 0:
                    act.copy(zc[:], z[:, bass.ds((n - 1) * PX, PX)]).then_inc(zc_ready, 1)
                if post and s >= 2:
                    sum_products(n, 2 * (s - 2) + 1)
                if (main and (s or not first(n))) or (not main and s == 0):
                    ps, ppar = (s - 1) % STEPS, par if s else 1 - par
                    if ps == 0 and main and not first(n):
                        act.wait_ge(found, 1 + PXT * (n - 1))
                    act.wait_ge(turned, S)
                    for h in range(2):
                        g = 2 * ps + h
                        cp = act.copy(maxima[ppar][:, :, g * P:(g + 1) * P], turn_ps[:, h])
                    cp.then_inc(kept, 1)
                if post and s == 0:
                    act.wait_ge(zt_turned, n)
                    act.copy(zt[:], z_ps[:]).then_inc(zt_ready, 1)
                if post and s in (1, 2):
                    sum_products(n, 2 * (s - 1))

            schedule(act, step)

        @block.vector
        def _(dve):
            apart = Apart(dve, dve_spare)

            def find(n, u):
                if u == 0:
                    apart.wait_ge(kept, STEPS * n)
                dve.max(best[:, u, :], maxima[1 - par_of[0]][:, u, :]).then_inc(max_done, 1)

            def place(n, u):
                apart.wait_ge(max_done, PXT * (n - 1) + u + 1)
                dve.max_index(block_id[:, u, :], best[:, u, :], maxima[1 - par_of[0]][:, u, :]).then_inc(found, 1)

            def select(n, u):
                c = n - 1
                at = 1 + 4 * (PXT * c + u)
                dve.wait_ge(summed, PER * (PXT * c + u + 1))
                dve.tensor_tensor(fine[:, u, :], fine[:, u, :], half[:, u, :], ALU.subtract).then_inc(sel_step, 1)
                apart.wait_ge(sel_step, at + 1)
                dve.max(fine_best[:, u, :], fine[:, u, :]).then_inc(sel_step, 1)
                apart.wait_ge(sel_step, at + 2)
                dve.max_index(fine_id[:, u, :], fine_best[:, u, :], fine[:, u, :]).then_inc(sel_step, 1)
                dve.wait_ge(sel_step, at + 3)
                dve.wait_ge(found, 1 + PXT * c + u + 1)
                dve.scalar_tensor_tensor(code[:, u:u + 1], block_id[:, u, 0:1], float(PER),
                                         fine_id[:, u, 0:1], ALU.mult, ALU.add).then_inc(sel_step, 1)

            par_of = [0]
            parts = {(0, 12): (find, 0), (0, 14): (place, 0), (1, 2): (find, 1), (1, 4): (place, 1),
                     (1, 6): (find, 2), (1, 8): (place, 2), (1, 10): (find, 3), (1, 12): (place, 3),
                     (2, 5): (select, 0), (2, 9): (select, 1), (3, 2): (select, 2), (3, 7): (select, 3)}

            def step(n, par, s, main, post):
                S = n * STEPS + s
                par_of[0] = par
                for k in range(BY_ACT, NPR):
                    if main:
                        g, m = 2 * s + k % 2, (2 * s + k % 2) * PER + k // 2
                        dve.wait_ge(score_ready, NPR * S + k + 1)
                        if k < 2 * BY_ACT:
                            dve.wait_ge(act_took, BY_ACT * S + k - BY_ACT + 1)
                        else:
                            dve.wait_ge(dve_took, BY_DVE * S + k - BY_ACT - 1)
                        r = run[s % 2][k % 2][:]
                        dve.scalar_tensor_tensor(r, score[SLOT[k]][:], nc2[:, m:m + 1], r,
                                                 ALU.add, ALU.max).then_inc(dve_took, 1)
                    if post and (s, k) in parts:
                        part, u = parts[s, k]
                        part(n, u)
                if post and s == STEPS - 1:
                    dve.wait_ge(zq_turned, 1 + n)
                    dve.wait_ge(added, 1 + 2 * (n - 1))
                    dve.tensor_tensor(delta[:], z_ps.rearrange("p u c -> p (u c)"), z[:, bass.ds((n - 1) * PX, PX)], ALU.subtract)\
                        .then_inc(delta_ready, 1)

            dve.sem_inc(found, 1)
            dve.sem_inc(delta_ready, 1)
            dve.sem_inc(sel_step, 1)
            schedule(dve, step)

        @block.gpsimd
        def _(pool):
            apart = Apart(pool, pool_spare)

            def gather(n, u):
                c = n - 1
                apart.wait_ge(found, 1 + PXT * c + u + 1)
                if u >= 2:
                    apart.wait_ge(summed, PER * (PXT * c + u - 1))
                else:
                    apart.wait_ge(sel_step, 1 + 4 * PXT * c)
                off = bass.IndirectOffsetOnAxis(block_id[:, u, 0:1], 0)
                pool.indirect_dma_start(cand[u % 2][:], None, a["codes"], off).then_inc(cand_in[u % 2], 16)
                pool.indirect_dma_start(half[:, u, :], None, half_norms, off).then_inc(cand_in[u % 2], 16)

            def multiply(n, u):
                pool.wait_ge(cand_in[u % 2], 32 * (2 * (n - 1) + u // 2 + 1))
                if u == 0:
                    pool.wait_ge(zt_ready, n)
                v = cand[u % 2].rearrange("p (j c) -> p j c", c=P)
                zb = zt[:, u, :].unsqueeze(1).to_broadcast([P, PER, P])
                pool.tensor_tensor(v, v, zb, ALU.mult).then_inc(multiplied, 1)

            def fetch(n, u):
                c = n - 1
                apart.wait_ge(sel_step, 1 + 4 * (PXT * c + u + 1))
                if u == 0:
                    apart.wait_ge(zq_turned, 1 + c)
                pool.indirect_dma_start(zq[:, u, :], None, a["codes"].rearrange("r (j c) -> (r j) c", c=P),
                                        bass.IndirectOffsetOnAxis(code[:, u:u + 1], 0)).then_inc(zq_in, 16)

            def step(n, par, s, main, post):
                if not post:
                    return
                if s == 1:
                    gather(n, 0)
                    gather(n, 1)
                    multiply(n, 0)
                    multiply(n, 1)
                if s == 2:
                    gather(n, 2)
                    multiply(n, 2)
                    gather(n, 3)
                    fetch(n, 0)
                    multiply(n, 3)
                    fetch(n, 1)
                if s == STEPS - 1:
                    fetch(n, 2)
                    fetch(n, 3)
                    at = bass.ds((n - 1) * PX, PX)
                    pool.wait_ge(delta_ready, 1 + n)
                    pool.tensor_tensor(delta[:], delta[:], z[:, at], ALU.add).then_inc(added, 1)
                    pool.wait_ge(added, 1 + 2 * (n - 1) + 1)
                    pool.tensor_tensor(x[:, at], x[:, at], delta[:], ALU.add).then_inc(added, 1)

            pool.sem_inc(added, 1)
            schedule(pool, step)


def layer1(nc, tools, a, x, gm32, ident, scale, shift, codes):
    ch, cl, nc2, half_norms = codes
    with ExitStack() as ctx:
        z = tools.sb(ctx, "z", [P, N])
        zh = tools.sb(ctx, "zh", [P, N], BF16)
        zl = tools.sb(ctx, "zl", [P, N], BF16)
        group_norm_scale(nc, tools, x, gm32, scale, shift)
        normed_parts(nc, tools, x, scale, shift, z, zh, zl)
        search(nc, tools, a, half_norms, ident, z, zh, zl, ch, cl, nc2, x.rearrange("p b n -> p (b n)"))


def layer2(nc, tools, a, x, xpad, gm32, scale, shift):
    with ExitStack() as ctx:
        wk = tools.sb(ctx, "wk", [P, TAPS, P])
        bk = tools.sb(ctx, "bk", [P, TAPS])
        kern = tools.sb(ctx, "kern", [P, TAPS, B])
        pooled = tools.sb(ctx, "pooled", [P, B])
        load(nc, tools, [(wk[:], a["wk"]), (bk[:], a["bk"])])
        group_norm_scale(nc, tools, x, gm32, scale, shift, pooled[:])
        apply_padded(nc, tools, x, scale, shift, xpad)
        kps = tools.ps(ctx, "kern_ps", [P, TAPS, B])
        kern_ready = tools.sem(ctx, "kern_ready")
        step = tools.sem(ctx, "kern_step")
        tap_done = [tools.sem(ctx, "tap_done") for _ in range(B)]
        block = ctx.enter_context(nc.Block())

        @block.tensor
        def _(pe):
            for k in range(TAPS):
                mm = pe.matmul(kps[:, k, :], wk[:, k, :], pooled[:], start=True, stop=True)
            mm.then_inc(kern_ready, 1)

        @block.vector
        def _(dve):
            chain = Chain(dve, step)
            dve.wait_ge(kern_ready, 1)
            chain(dve.tensor_tensor(kern[:], kps[:], bc(bk[:], B), ALU.add))
            chain(dve.tensor_scalar(kern[:], kern[:], 0.0, None, ALU.max))
            for k in range(TAPS):
                for b in range(B):
                    v = xpad[:, 0:B * PADDED].rearrange("p (b r w) -> p b r w", b=B, w=WP)[
                        :, b, k // 3:k // 3 + H, k % 3:k % 3 + W]
                    xb = x[:, b, :].rearrange("p (r w) -> p r w", w=W)
                    if k:
                        dve.wait_ge(tap_done[b], k)
                    dve.scalar_tensor_tensor(xb, v, kern[:, k, b:b + 1], xb, ALU.mult, ALU.add)\
                        .then_inc(tap_done[b], 1)


TABLE_PAD = W + 1
CORNERS = 4
JOBS = 2 * B
ITILES = TILES // B


def deformable(nc, tools, a, x, xpad, ident, gm8, out):
    QUAD = CORNERS * P
    M = ITILES * TAPS
    HALVES = [slice(h * HW // 2, (h + 1) * HW // 2) for h in range(2)]
    with ExitStack() as ctx:
        y = tools.sb(ctx, "y3", [P, B, HW])
        w_tap = [tools.sb(ctx, "w_tap", [P, TAPS, P]) for _ in range(2)]
        gn = [tools.sb(ctx, "gn_sb", [P, 2]) for _ in range(2)]
        w_off = [tools.sb(ctx, "w_off", [P, TAPS, 2 * TAPS]) for _ in range(2)]
        b_off = [tools.sb(ctx, "b_off", [2 * TAPS, 1]) for _ in range(2)]
        base = tools.sb(ctx, "base", [P, ITILES, 2 * TAPS])
        table = [nc.dram_tensor(f"corners{j}", [TABLE_PAD + HW, CORNERS, P], F32).ap() for j in range(JOBS)]
        zeros = tools.sb(ctx, "zeros", [TABLE_PAD, QUAD])
        osb = tools.sb(ctx, "off_sb", [P, CH])
        xc = tools.sb(ctx, "x_chunk", [P, CH])
        xt = tools.sb(ctx, "x_turned", [P, TPC, P])
        pos = tools.sb(ctx, "pos", [P, 2 * M])
        low = tools.sb(ctx, "low", [P, 2 * M])
        side = tools.sb(ctx, "side_weights", [P, 2 * M, 2])
        weights = [tools.sb(ctx, "weights", [P, M * CORNERS]) for _ in range(B)]
        index = [tools.sb(ctx, "index", [P, M], U32) for _ in range(B)]
        off_ps = tools.ps(ctx, "off_ps", [P, 512])[0:2 * TAPS, 0:CH]
        otp = tools.ps(ctx, "off_t_ps", [P, 512])[:, 0:CH].rearrange("p (t n) -> p t n", t=TPC)
        xtp = tools.ps(ctx, "x_t_ps", [P, 512])[:, 0:CH].rearrange("p (t n) -> p t n", t=TPC)
        idx = [tools.sb(ctx, "tile_index", [P, TAPS], U32) for _ in range(TPC)]
        quads = [tools.sb(ctx, "quads", [P, TAPS, QUAD]) for _ in range(TPC)]
        sampled = [tools.sb(ctx, "sampled", [P, TAPS, P]) for _ in range(TPC)]
        turned = [tools.sb(ctx, "sampled_t", [P, 3 * P]) for _ in range(3)]
        tps = [tools.ps(ctx, "sampled_t_ps", [P, 512])[:, 0:3 * P] for _ in range(3)]
        yps = tools.ps(ctx, "mixed_ps", [P, 512])[:, 0:P]
        stats = tools.sb(ctx, "n_stats", [P, NCH, 6])
        mv = tools.sb(ctx, "n_mean_var", [P, 2])
        gg = tools.sb(ctx, "n_group", [P, 2])
        var = tools.sb(ctx, "n_var", [P, 1])
        tmp = tools.sb(ctx, "n_tmp", [P, 1])
        scale = tools.sb(ctx, "n_scale", [P, 1])
        shift = tools.sb(ctx, "n_shift", [P, 1])
        gps = tools.ps(ctx, "n_ps", [P, 2])

        zeroed = tools.sem(ctx, "zeroed")
        chunk_ready = tools.sem(ctx, "chunk_ready")
        x_turned = tools.sem(ctx, "x_turned")
        x_saved = tools.sem(ctx, "x_saved")
        ends_stored = tools.sem(ctx, "table_ends_stored")
        stored = tools.sem(ctx, "table_stored")
        conv_done = tools.sem(ctx, "off_conv_done")
        off_saved = tools.sem(ctx, "off_saved")
        off_turned = tools.sem(ctx, "off_turned")
        pos_ready = tools.sem(ctx, "pos_ready")
        corner_step = tools.sem(ctx, "corner_step")
        index_ready = tools.sem(ctx, "index_ready")
        idx_ready = tools.sem(ctx, "idx_ready")
        quads_in = [tools.sem(ctx, "quads_in") for _ in range(TPC)]
        weighted = tools.sem(ctx, "weighted")
        paired = tools.sem(ctx, "paired")
        sampled_ready = tools.sem(ctx, "sampled_ready")
        turn_done = tools.sem(ctx, "turn_done")
        turn_saved = tools.sem(ctx, "turn_saved")
        mixed = tools.sem(ctx, "mixed")
        y_saved = tools.sem(ctx, "y_saved")
        norm_step = tools.sem(ctx, "norm_step")
        moments_ready = tools.sem(ctx, "moments_ready")
        group_ready = tools.sem(ctx, "group_ready")
        var_ready = tools.sem(ctx, "var_ready")
        rooted = tools.sem(ctx, "rooted")
        affine = tools.sem(ctx, "affine_ready")
        relued = tools.sem(ctx, "relued")
        added = tools.sem(ctx, "added")
        out_stored = tools.sem(ctx, "out_stored")
        pool_spare = tools.sem(ctx, "pool_spare")

        load(nc, tools, [(base[:], a["base"][:, 0:ITILES])]
             + [(to[s][:], a[f"{name}{s + 1}"]) for s in range(2)
                for to, name in ((w_off, "w_off"), (b_off, "b_off"), (w_tap, "w_tap"), (gn, "gn"))])
        block = ctx.enter_context(nc.Block())

        def sections(eng, norm, prepare, tile, finish=lambda j: None, late=False):
            def double(k, r, c):
                nxt = k + 1 < JOBS
                tile(k, r, 0)
                if nxt and not late:
                    prepare(k + 1, c, "turn")
                    prepare(k + 1, c + 1, "conv")
                    prepare(k + 1, c + 1, "turn")
                tile(k, r, 1)
                if nxt and late:
                    prepare(k + 1, c, "turn")
                tile(k, r, 2)
                if nxt and late:
                    prepare(k + 1, c + 1, "turn")

            prepare(0, 0, "conv")
            with eng.Fori(0, NCH - 1) as r:
                prepare(0, r, "turn")
                prepare(0, r + 1, "conv")
            prepare(0, NCH - 1, "turn")
            finish(0)
            for k in range(JOBS):
                nxt = k + 1 < JOBS
                tile(k, 0, 0)
                if k and not late:
                    norm(k - 1)
                tile(k, 0, 1)
                if k and late:
                    norm(k - 1)
                tile(k, 0, 2)
                if nxt:
                    prepare(k + 1, 0, "conv")
                double(k, 1, 0)
                if nxt:
                    prepare(k + 1, 2, "conv")
                with eng.Fori(2, NCH - 2) as r:
                    tile(k, r, 0)
                    if nxt and not late:
                        prepare(k + 1, r, "turn")
                    tile(k, r, 1)
                    if nxt and late:
                        prepare(k + 1, r, "turn")
                    tile(k, r, 2)
                    if nxt:
                        prepare(k + 1, r + 1, "conv")
                double(k, NCH - 2, NCH - 2)
                if nxt:
                    finish(k + 1)
                for u in range(TPC):
                    tile(k, NCH - 1, u)
            norm(JOBS - 1)

        def tile_no(j, r, u):
            return ITILES * j + TPC * r + u

        def chunk_no(j, r):
            return NCH * j + r

        def inner(b):
            return xpad[:, b * PADDED:(b + 1) * PADDED].rearrange("p (r w) -> p r w", w=WP)[:, 1:H + 1, 1:W + 1]

        @block.tensor
        def _(pe):
            def norm(j):
                pe.wait_ge(moments_ready, j + 1)
                pe.matmul(gps[:], gm8, mv[:], start=True, stop=True).then_inc(group_ready, 1)

            def prepare(j, r, part):
                C = chunk_no(j, r)
                if part == "conv":
                    pe.wait_ge(chunk_ready, C + 1)
                    pe.wait_ge(x_saved, C + 1)
                    for t in range(TPC):
                        mm = pe.transpose(xtp[:, t, :], xc[:, t * P:(t + 1) * P], ident)
                    mm.then_inc(x_turned, 1)
                    pe.wait_ge(off_saved, C + 1)
                    for t in range(TAPS):
                        at = j % B * PADDED + r * (ROWS * WP) + (t // 3) * WP + t % 3
                        win = xpad[:, bass.ds(at, ROWS * WP)].rearrange("p (r w) -> p r w", w=WP)[:, :, 0:W]
                        mm = pe.matmul(off_ps, w_off[j // B][:, t, :], win, start=t == 0, stop=t == TAPS - 1)
                    mm.then_inc(conv_done, 1)
                else:
                    pe.wait_ge(off_saved, C + 2)
                    pe.wait_ge(pos_ready, C + 1)
                    for t in range(TPC):
                        mm = pe.transpose(otp[:, t, :], osb[:, t * P:(t + 1) * P], ident)
                    mm.then_inc(off_turned, 1)

            def tile(j, r, u):
                T = tile_no(j, r, u)
                pe.wait_ge(sampled_ready, T + 1)
                for g in range(3):
                    pe.wait_ge(turn_saved, 3 * T + g + 1)
                    for k in range(3):
                        mm = pe.transpose(tps[g][:, k * P:(k + 1) * P], sampled[u][:, 3 * g + k, :], ident)
                    mm.then_inc(turn_done, 1)
                pe.wait_ge(y_saved, T + 1)
                for g in range(3):
                    pe.wait_ge(turn_saved, 3 + 3 * T + g + 1)
                    for k in range(3):
                        mm = pe.matmul(yps, w_tap[j // B][:, 3 * g + k, :], turned[g][:, k * P:(k + 1) * P],
                                       start=g + k == 0, stop=g + k == 4)
                    mm.then_inc(mixed, 1)

            pe.sem_inc(x_turned, 1)
            pe.sem_inc(off_turned, 1)
            pe.sem_inc(turn_done, 3 * TPC)
            pe.sem_inc(mixed, 3)
            sections(pe, norm, prepare, tile)

        @block.scalar
        def _(act):
            def norm(j):
                b = j % B
                act.wait_ge(var_ready, j + 1)
                act.sqrt(tmp[:], var[:]).then_inc(rooted, 1)
                act.wait_ge(affine, j + 1)
                for h in range(2):
                    if j < B:
                        src = y[:, b, HALVES[h]].rearrange("p (r w) -> p r w", w=W)
                        to = inner(b)[:, h * H // 2:(h + 1) * H // 2, :]
                    else:
                        src = to = y[:, b, HALVES[h]]
                    act.activation(to, src, ACT.Relu, bias=shift[:], scale=scale[:]).then_inc(relued, 1)

            def prepare(j, r, part):
                if part != "conv":
                    return
                C = chunk_no(j, r)
                at = j % B * PADDED + (r * ROWS + 1) * WP + 1
                v = xpad[:, bass.ds(at, ROWS * WP)].rearrange("p (r w) -> p r w", w=WP)[:, :, 0:W]
                act.wait_ge(x_turned, C + 1)
                if j >= B:
                    act.wait_ge(relued, 2 * (j - B + 1))
                act.copy(xc.rearrange("p (r w) -> p r w", w=W), v).then_inc(chunk_ready, 1)
                act.wait_ge(x_turned, C + 2)
                act.wait_ge(stored, 16 * CORNERS * (C + 1))
                act.copy(xt[:], xtp).then_inc(x_saved, 1)
                act.wait_ge(conv_done, C + 1)
                act.wait_ge(off_turned, C + 1)
                act.activation(osb[0:2 * TAPS, :], off_ps, ACT.Identity, bias=b_off[j // B][:])\
                    .then_inc(off_saved, 1)

            def tile(j, r, u):
                T = tile_no(j, r, u)
                for g in range(3):
                    act.wait_ge(turn_done, 3 * TPC + 3 * T + g + 1)
                    act.wait_ge(mixed, 3 * T + g + 1)
                    act.copy(turned[g][:], tps[g]).then_inc(turn_saved, 1)
                act.wait_ge(mixed, 3 + 3 * T + 3)
                act.copy(y[:, j % B, bass.ds((TPC * r + u) * P, P)], yps).then_inc(y_saved, 1)

            act.sem_inc(x_saved, 1)
            act.sem_inc(off_saved, 1)
            act.sem_inc(stored, 16 * CORNERS)
            act.sem_inc(turn_saved, 3)
            act.sem_inc(y_saved, 1)
            act.wait_ge(zeroed, 2)
            sections(act, norm, prepare, tile)

        @block.vector
        def _(dve):
            norm_chain = Chain(dve, norm_step)
            corner_chain = Chain(dve, corner_step)

            def norm(j):
                chain, b = norm_chain, j % B
                dve.wait_ge(y_saved, 1 + ITILES * (j + 1))
                for q in range(NCH):
                    last = dve.bn_stats(stats[:, q, :], y[:, b, q * CH:(q + 1) * CH])
                chain(last)
                chain(dve.bn_aggr(mv[:], stats.rearrange("p q s -> p (q s)")))
                chain(dve.scalar_tensor_tensor(mv[:, 1:2], mv[:, 0:1], mv[:, 0:1], mv[:, 1:2], ALU.mult, ALU.add))
                dve.sem_inc(moments_ready, 1)
                dve.wait_ge(group_ready, j + 1)
                chain(dve.tensor_copy(gg[:], gps[:]))
                chain(dve.tensor_tensor(var[:], gg[:, 0:1], gg[:, 0:1], ALU.mult))
                chain(dve.tensor_tensor(var[:], gg[:, 1:2], var[:], ALU.subtract))
                chain(dve.tensor_scalar(var[:], var[:], EPS, None, ALU.add))
                dve.sem_inc(var_ready, 1)
                dve.wait_ge(rooted, j + 1)
                chain(dve.reciprocal(scale[:], tmp[:]))
                chain(dve.tensor_tensor(tmp[:], scale[:], scale[:], ALU.mult))
                chain(dve.tensor_tensor(tmp[:], tmp[:], var[:], ALU.mult))
                chain(dve.tensor_scalar(tmp[:], tmp[:], -0.5, 1.5, ALU.mult, ALU.add))
                chain(dve.tensor_tensor(scale[:], scale[:], tmp[:], ALU.mult))
                chain(dve.tensor_tensor(scale[:], scale[:], gn[j // B][:, 0:1], ALU.mult))
                chain(dve.tensor_tensor(shift[:], gg[:, 0:1], scale[:], ALU.mult))
                chain(dve.tensor_tensor(shift[:], gn[j // B][:, 1:2], shift[:], ALU.subtract))
                dve.sem_inc(affine, 1)
                if j >= B:
                    for h in range(2):
                        v = HALVES[h]
                        dve.wait_ge(relued, 2 * j + h + 1)
                        dve.tensor_tensor(x[:, b, v], x[:, b, v], y[:, b, v], ALU.add).then_inc(added, 1)

            def prepare(j, r, part):
                if part == "turn":
                    C = chunk_no(j, r)
                    dve.wait_ge(off_turned, 1 + C + 1)
                    at = bass.ds(r * (TPC * 2 * TAPS), TPC * 2 * TAPS)
                    dve.tensor_tensor(pos[:, at].rearrange("p (t k) -> p t k", t=TPC), otp[:, :, 0:2 * TAPS],
                                      base.rearrange("p t k -> p (t k)")[:, at].rearrange("p (t k) -> p t k", t=TPC),
                                      ALU.add).then_inc(pos_ready, 1)

            def finish(j):
                chain, b = corner_chain, j % B
                dve.wait_ge(pos_ready, 1 + NCH * (j + 1))
                chain(dve.tensor_scalar(low[:], pos[:], -0.5, 0.0, ALU.add, ALU.max))
                chain(dve.tensor_scalar(low[:], low[:], float(H - 2), ROUND, ALU.min, ALU.add))
                chain(dve.tensor_scalar(low[:], low[:], -ROUND, None, ALU.add))
                lo = low.rearrange("p (m a) -> p m a", a=2)
                chain(dve.tensor_tensor(pos[:], pos[:], low[:], ALU.subtract))
                dve.tensor_scalar(side[:, :, 0], pos[:], -1.0, 1.0, ALU.mult, ALU.add).then_inc(corner_step, 1)
                dve.tensor_scalar(side[:, :, 1], pos[:], -1.0, 2.0, ALU.mult, ALU.add).then_inc(corner_step, 1)
                chain.n += 2
                chain(dve.scalar_tensor_tensor(low[:, 0:M], lo[:, :, 0], float(W), lo[:, :, 1], ALU.mult, ALU.add))
                dve.tensor_scalar(index[b][:], low[:, 0:M], float(TABLE_PAD), None, ALU.add)\
                    .then_inc(index_ready, 1)
                dve.scalar_tensor_tensor(side[:, :, 0], pos[:], 1.0, side[:, :, 0], ALU.add, ALU.min)\
                    .then_inc(corner_step, 1)
                chain.n += 1
                chain(dve.tensor_tensor(side[:, :, 1], pos[:], side[:, :, 1], ALU.min))
                chain(dve.tensor_scalar(side[:], side[:], 0.0, None, ALU.max))
                sd = side.rearrange("p (m a) s -> p m a s", a=2)
                for dy in range(2):
                    yw = sd[:, :, 0, dy:dy + 1].to_broadcast([P, M, 2])
                    chain(dve.tensor_tensor(weights[b].rearrange("p (m d s) -> p m d s", d=2, s=2)[:, :, dy, :],
                                            sd[:, :, 1, :], yw, ALU.mult))

            def tile(j, r, u):
                T = tile_no(j, r, u)
                q = quads[u]
                q4 = q.rearrange("p k (j c) -> p (k j) c", c=P)
                w = weights[j % B][:, bass.ds((TPC * r + u) * (TAPS * CORNERS), TAPS * CORNERS)]
                dve.wait_ge(quads_in[u], 16 * TAPS * (chunk_no(j, r) + 1))
                dve.tensor_tensor(q4, q4, bc(w, P), ALU.mult).then_inc(weighted, 1)
                if u:
                    gather_up(j, r, u - 1)
                dve.wait_ge(weighted, T + 1)
                dve.tensor_tensor(q[:, :, 0:2 * P], q[:, :, 0:2 * P], q[:, :, 2 * P:], ALU.add).then_inc(paired, 1)
                if u == TPC - 1:
                    gather_up(j, r, u)

            def gather_up(j, r, u):
                T = tile_no(j, r, u)
                dve.wait_ge(paired, T + 1)
                dve.wait_ge(turn_done, 3 * T + 3)
                dve.tensor_tensor(sampled[u][:], quads[u][:, :, 0:P], quads[u][:, :, P:2 * P], ALU.add)\
                    .then_inc(sampled_ready, 1)

            dve.sem_inc(pos_ready, 1)
            sections(dve, norm, prepare, tile, finish, late=True)

        @block.gpsimd
        def _(pool):
            apart = Apart(pool, pool_spare)

            def tile(j, r, u):
                T = tile_no(j, r, u)
                if isinstance(r, int) and r == 0 and u == 0:
                    pool.wait_ge(index_ready, j + 1)
                if not (isinstance(r, int) and r == 0 and j == 0):
                    apart.wait_ge(sampled_ready, T - TPC + 1)
                pool.tensor_copy(idx[u][:], index[j % B][:, bass.ds((TPC * r + u) * TAPS, TAPS)])\
                    .then_inc(idx_ready, 1)
                if isinstance(r, int) and r == 0 and u == 0:
                    apart.wait_ge(stored, 16 * CORNERS * (1 + NCH * (j + 1)))
                    apart.wait_ge(ends_stored, 16 * 2 * JOBS)
                apart.wait_ge(idx_ready, T + 1)
                for k in range(TAPS):
                    pool.indirect_dma_start(quads[u][:, k, :], None, table[j].rearrange("n s c -> n (s c)"),
                                            bass.IndirectOffsetOnAxis(idx[u][:, k:k + 1], 0))\
                        .then_inc(quads_in[u], 16)

            pool.memset(osb[:], 0.0).then_inc(zeroed, 1)
            pool.memset(zeros[:], 0.0).then_inc(zeroed, 1)
            for j in range(JOBS):
                tile(j, 0, 0)
                tile(j, 0, 1)
                tile(j, 0, 2)
                with pool.Fori(1, NCH) as r:
                    for u in range(TPC):
                        tile(j, r, u)

        @block.sync
        def _(sp):
            sp.wait_ge(zeroed, 2)
            for j in range(JOBS):
                flat = table[j].rearrange("n s c -> n (s c)")
                sp.dma_start(flat[0:TABLE_PAD, :], zeros[:]).then_inc(ends_stored, 16)
                sp.dma_start(flat[HW:HW + TABLE_PAD, :], zeros[:]).then_inc(ends_stored, 16)
            sp.wait_ge(ends_stored, 16 * 2 * JOBS)
            for j in range(JOBS):
                flat = table[j].rearrange("n s c -> n (s c)")
                with sp.Fori(0, NCH) as r:
                    sp.wait_ge(x_saved, 1 + chunk_no(j, r) + 1)
                    for s in range(CORNERS):
                        at = TABLE_PAD + r * CH - (s // 2 * W + s % 2)
                        to = flat[bass.ds(at, CH), s * P:(s + 1) * P].rearrange("(t p) c -> p t c", p=P)
                        sp.dma_start(to, xt[:]).then_inc(stored, 16)
            for b in range(B):
                for h in range(2):
                    sp.wait_ge(added, 2 * b + h + 1)
                    sp.dma_start(out[:, b, HALVES[h]], x[:, b, HALVES[h]]).then_inc(out_stored, 16)
            sp.wait_ge(stored, 16 * CORNERS * (1 + NCH * JOBS))
            sp.wait_ge(out_stored, 16 * 2 * B)


def layer3(nc, tools, a, x, xpad, gm32, gm8, ident, scale, shift, out):
    group_norm_scale(nc, tools, x, gm32, scale, shift)
    apply_padded(nc, tools, x, scale, shift, xpad)
    deformable(nc, tools, a, x, xpad, ident, gm8, out)


def program(nc, a, out, layers=(0, 1, 2, 3)):
    tools = Tools(nc)
    with ExitStack() as ctx:
        x = tools.sb(ctx, "x", [P, B, HW])
        xpad = tools.sb(ctx, "xpad", [P, B * PADDED + WP])
        ident = tools.sb(ctx, "ident", [P, P])[:]
        gm32 = tools.sb(ctx, "gm32", [P, P])[:]
        gm8 = tools.sb(ctx, "gm8", [P, P])[:]
        scale = tools.sb(ctx, "scale", [P, B])[:]
        shift = tools.sb(ctx, "shift", [P, B])[:]
        zeroed = tools.sem(ctx, "xpad_zeroed")
        stored = tools.sem(ctx, "stored")

        load(nc, tools, [(x[:], a["x"]), (ident, a["ident"]), (gm32, a["gm32"]), (gm8, a["gm8"])])
        with nc.Block() as block:
            @block.gpsimd
            def _(pool):
                pool.memset(xpad[:], 0.0).then_inc(zeroed, 1)

        with ExitStack() as code_ctx:
            codes = (tools.sb(code_ctx, "ch", [P, CODES], BF16), tools.sb(code_ctx, "cl", [P, CODES], BF16),
                     tools.sb(code_ctx, "nc2", [P, GROUPS * PER])[:],
                     nc.dram_tensor("half_norms", [CODES // PER, PER], F32).ap())
            if 0 in layers:
                layer0(nc, tools, a, x, xpad, gm32, ident, scale, shift, codes)
            if 1 in layers:
                layer1(nc, tools, a, x, gm32, ident, scale, shift, codes)
        if 2 in layers:
            layer2(nc, tools, a, x, xpad, gm32, scale, shift)
        if 3 in layers:
            layer3(nc, tools, a, x, xpad, gm32, gm8, ident, scale, shift, out)
        else:
            with nc.Block() as block:
                @block.sync
                def _(sp):
                    sp.dma_start(out, x[:]).then_inc(stored, 16)
                    sp.wait_ge(stored, 16)


def layouts(i):
    f = np.float32
    t = np.ascontiguousarray

    def taps(w):
        return t(w.reshape(w.shape[0], P, TAPS).transpose(1, 2, 0))

    n = np.arange(N).reshape(TILES, P).T % HW
    k = np.arange(TAPS)
    base = np.stack([(n // W)[:, :, None] - 1 + k // 3, (n % W)[:, :, None] - 1 + k % 3], -1)
    base = base.reshape(P, TILES, 2 * TAPS)
    return {
        "x": t(i["x"].reshape(B, P, HW).transpose(1, 0, 2)),
        "w_cat": taps(i["L0_conv_W_cat"]),
        "w_scale": t(i["L0_conv_W_scale"].reshape(P, NB + 1, P).transpose(2, 1, 0)),
        "gamma_beta": t(np.stack([i["L0_conv_gamma"], i["L0_conv_beta"]], 1)),
        "codes_t": t(i["L1_conv_codebook"].reshape(GROUPS, P, PER, P).transpose(3, 0, 2, 1))
        .reshape(P, GROUPS, PER * P),
        "codes": i["L1_conv_codebook"].reshape(CODES // PER, PER * P),
        "wk": t(i["L2_conv_Wk"].reshape(P, TAPS, P).transpose(2, 1, 0)),
        "bk": i["L2_conv_bk"].reshape(P, TAPS),
        **{f"w_off{s}": taps(i[f"L3_conv_off{s}_w"]) for s in (1, 2)},
        **{f"b_off{s}": i[f"L3_conv_off{s}_b"].reshape(2 * TAPS, 1) for s in (1, 2)},
        **{f"w_tap{s}": taps(i[f"L3_conv_dw{s}"]) for s in (1, 2)},
        **{f"gn{s}": t(np.stack([i[f"L3_conv_gn{s}_s"], i[f"L3_conv_gn{s}_b"]], 1)) for s in (1, 2)},
        "base": base.astype(f),
        "ident": np.eye(P, dtype=f),
        "gm32": np.kron(np.eye(32), np.full((4, 4), 1 / 4)).astype(f),
        "gm8": np.kron(np.eye(8), np.full((16, 16), 1 / 16)).astype(f),
        "id3a": np.tile(np.eye(NA, dtype=f), (3, 1)),
        "id3b": np.tile(np.eye(TAPS, dtype=f), (3, 1)),
    }


def kernel(**inputs):
    import concourse.bacc as bacc
    from concourse.bass_utils import run_bass_kernel_spmd

    arrays = layouts({k: np.asarray(v) for k, v in inputs.items()})
    nc = bacc.Bacc("TRN2", target_bir_lowering=False, num_devices=1)
    a = {k: nc.dram_tensor(f"in_{k}", v.shape, mybir.dt.from_np(v.dtype), kind="ExternalInput").ap()
         for k, v in arrays.items()}
    out = nc.dram_tensor("out", [P, B, HW], F32, kind="ExternalOutput").ap()
    program(nc, a, out)
    r = run_bass_kernel_spmd(nc, [{f"in_{k}": v for k, v in arrays.items()}], core_ids=[0])
    return r.results[0]["out"].transpose(1, 0, 2).reshape(B, P, H, W)
```

```python
from contextlib import ExitStack

import numpy as np

import concourse.bass as bass
from concourse import mybir

P = 128
B, H, W = 2, 48, 48
HW = H * W
N = B * HW
WP = W + 2
HP = H + 2
PADDED = HP * WP
EPS = 1e-5

ROWS = 8
CH = ROWS * W
NCH = H // ROWS
TPC = CH // P
TILES = N // P
DIL = (1, 6, 12, 24, 36)
NB = len(DIL)
TAPS = 9
NG = NB * TAPS
NA = 4 * TAPS

CODES = 8192
GROUPS = 8
PER = CODES // P // GROUPS
PX = 512
NPX = N // PX

ALU = mybir.AluOpType
ACT = mybir.ActivationFunctionType
AX = mybir.AxisListType.X
F32 = mybir.dt.float32
BF16 = mybir.dt.bfloat16
U32 = mybir.dt.uint32
ROUND = float(2 ** 23)


def bc(ap, n):
    return ap.unsqueeze(len(ap.shape)).to_broadcast([*ap.shape, n])


def overlapped(v, half, rows):
    part, row, col = v.ap
    ap = [list(part), [row[0] * (rows - half), 2], [row[0], half], list(col)]
    return bass.AP(tensor=v.tensor, offset=v.offset, ap=ap)


class Tools:

    def __init__(self, nc):
        self.nc, self.n = nc, 0

    def sb(self, ctx, name, shape, dt=F32):
        self.n += 1
        return ctx.enter_context(self.nc.sbuf_tensor(f"{name}_{self.n}", shape, dt))

    def ps(self, ctx, name, shape, dt=F32):
        self.n += 1
        return ctx.enter_context(self.nc.psum_tensor(f"{name}_{self.n}", shape, dt))

    def sem(self, ctx, name):
        self.n += 1
        return ctx.enter_context(self.nc.semaphore(f"{name}_{self.n}"))


class Apart:

    def __init__(self, eng, spare):
        self.eng, self.spare = eng, spare

    def wait_ge(self, sem, value):
        self.eng.wait_ge(sem, value)
        self.eng.sem_inc(self.spare, 1)


class Chain:

    def __init__(self, eng, sem):
        self.eng, self.sem, self.n = eng, sem, 0

    def __call__(self, ins):
        self.n += 1
        ins.then_inc(self.sem, 1)
        self.eng.wait_ge(self.sem, self.n)


def inv_sqrt(eng, chain, var, tmp, out, ready, rooted):
    chain(eng.tensor_scalar(var, var, EPS, None, ALU.add))
    eng.sem_inc(ready, 1)
    eng.wait_ge(rooted, 1)
    chain(eng.reciprocal(out, tmp))
    chain(eng.tensor_tensor(tmp, out, out, ALU.mult))
    chain(eng.tensor_tensor(tmp, tmp, var, ALU.mult))
    chain(eng.tensor_scalar(tmp, tmp, -0.5, 1.5, ALU.mult, ALU.add))
    chain(eng.tensor_tensor(out, out, tmp, ALU.mult))


class ImageNorm:
    PS = 2

    def __init__(self, tools, ctx):
        self.stats = tools.sb(ctx, "n_stats", [P, NCH, 6])
        self.mv = tools.sb(ctx, "n_mean_var", [P, 2])
        self.gg = tools.sb(ctx, "n_group", [P, 2])
        self.var = tools.sb(ctx, "n_var", [P, 1])
        self.tmp = tools.sb(ctx, "n_tmp", [P, 1])
        self.scale = tools.sb(ctx, "n_scale", [P, 1])
        self.shift = tools.sb(ctx, "n_shift", [P, 1])
        self.step = tools.sem(ctx, "norm_step")
        self.moments_ready = tools.sem(ctx, "moments_ready")
        self.group_ready = tools.sem(ctx, "group_ready")
        self.var_ready = tools.sem(ctx, "var_ready")
        self.rooted = tools.sem(ctx, "rooted")
        self.affine = tools.sem(ctx, "affine_ready")
        self.steps = 0

    def chained(self, dve, ins):
        self.steps += 1
        ins.then_inc(self.step, 1)
        dve.wait_ge(self.step, self.steps)

    def dve_moments(self, dve, src, wait=lambda q: None):
        for q in range(NCH):
            wait(q)
            last = dve.bn_stats(self.stats[:, q, :], src[:, q * CH:(q + 1) * CH])
        self.chained(dve, last)
        mean, square = self.mv[:, 0:1], self.mv[:, 1:2]
        self.chained(dve, dve.bn_aggr(self.mv[:], self.stats.rearrange("p q s -> p (q s)")))
        self.chained(dve, dve.scalar_tensor_tensor(square, mean, mean, square, ALU.mult, ALU.add))
        dve.sem_inc(self.moments_ready, 1)

    def pe(self, pe, use, gmat, ps):
        pe.wait_ge(self.moments_ready, use + 1)
        pe.matmul(ps, gmat, self.mv[:], start=True, stop=True).then_inc(self.group_ready, 1)

    def act(self, act, use):
        act.wait_ge(self.var_ready, use + 1)
        act.sqrt(self.tmp[:], self.var[:]).then_inc(self.rooted, 1)
        act.wait_ge(self.affine, use + 1)

    def dve_affine(self, dve, use, ps, gn=None):
        gg, var, tmp, scale, shift = self.gg, self.var[:], self.tmp[:], self.scale[:], self.shift[:]
        mean = gg[:, 0:1]
        dve.wait_ge(self.group_ready, use + 1)
        self.chained(dve, dve.tensor_copy(gg[:], ps))
        self.chained(dve, dve.tensor_tensor(var, mean, mean, ALU.mult))
        self.chained(dve, dve.scalar_tensor_tensor(var, gg[:, 1:2], EPS, var, ALU.add, ALU.subtract))
        dve.sem_inc(self.var_ready, 1)
        dve.wait_ge(self.rooted, use + 1)
        self.chained(dve, dve.reciprocal(scale, tmp))
        self.chained(dve, dve.scalar_tensor_tensor(tmp, scale, var, scale, ALU.mult, ALU.mult))
        self.chained(dve, dve.tensor_scalar(tmp, tmp, -0.5, 1.5, ALU.mult, ALU.add))
        if gn is None:
            self.chained(dve, dve.tensor_tensor(scale, scale, tmp, ALU.mult))
            self.chained(dve, dve.scalar_tensor_tensor(shift, mean, -1.0, scale, ALU.mult, ALU.mult))
        else:
            self.chained(dve, dve.scalar_tensor_tensor(scale, scale, gn[:, 0:1], tmp, ALU.mult, ALU.mult))
            self.chained(dve, dve.tensor_tensor(shift, mean, scale, ALU.mult))
            self.chained(dve, dve.tensor_tensor(shift, gn[:, 1:2], shift, ALU.subtract))
        dve.sem_inc(self.affine, 1)


class Depthwise:
    PS = ImageNorm.PS + TAPS

    def __init__(self, tools, ctx, a, x, xpad, gm32):
        self.a, self.x, self.xpad, self.gm32 = a, x, xpad, gm32
        self.wk = tools.sb(ctx, "wk", [P, TAPS, P])
        self.bk = tools.sb(ctx, "bk", [P, TAPS])
        self.kern = tools.sb(ctx, "kern", [P, TAPS])
        self.pooled = tools.sb(ctx, "pooled", [P, 1])
        self.norm = ImageNorm(tools, ctx)
        self.loaded = tools.sem(ctx, "wk_loaded")
        self.pooled_ready = tools.sem(ctx, "pooled_ready")
        self.kern_ready = tools.sem(ctx, "kern_ready")
        self.applied = tools.sem(ctx, "applied")
        self.done = [tools.sem(ctx, "tap_done") for _ in range(B)]

    def sp(self, sp):
        sp.dma_start(self.wk[:], self.a["wk"]).then_inc(self.loaded, 16)
        sp.dma_start(self.bk[:], self.a["bk"]).then_inc(self.loaded, 16)

    def pe_norm(self, pe, b, ps):
        self.norm.pe(pe, b, self.gm32, ps[:, 0:2])

    def pe_kernels(self, pe, b, ps):
        pe.wait_ge(self.loaded, 32)
        pe.wait_ge(self.pooled_ready, b + 1)
        for k in range(TAPS):
            mm = pe.matmul(ps[:, 2 + k:3 + k], self.wk[:, k, :], self.pooled[:], start=True, stop=True)
        mm.then_inc(self.kern_ready, 1)

    def act_norm(self, act, b):
        self.norm.act(act, b)
        to = self.xpad[:, b * PADDED:(b + 1) * PADDED].rearrange("p (r w) -> p r w", w=WP)[:, 1:H + 1, 1:W + 1]
        act.activation(to, self.x[:, b, :].rearrange("p (r w) -> p r w", w=W), ACT.Identity,
                       bias=self.norm.shift[:], scale=self.norm.scale[:]).then_inc(self.applied, 1)

    def dve_norm(self, dve, b, ps):
        norm = self.norm
        norm.dve_affine(dve, b, ps[:, 0:2])
        norm.chained(dve, dve.scalar_tensor_tensor(self.pooled[:], norm.mv[:, 0:1], norm.scale[:], norm.shift[:],
                                                   ALU.mult, ALU.add))
        dve.sem_inc(self.pooled_ready, 1)

    def dve_kernels(self, dve, b, ps):
        dve.wait_ge(self.kern_ready, b + 1)
        self.norm.chained(dve, dve.tensor_tensor(self.kern[:], ps[:, 2:2 + TAPS], self.bk[:], ALU.add))
        self.norm.chained(dve, dve.tensor_scalar(self.kern[:], self.kern[:], 0.0, None, ALU.max))
        dve.wait_ge(self.applied, b + 1)

    def tap(self, dve, b, k):
        v = self.xpad[:, b * PADDED:(b + 1) * PADDED].rearrange("p (r w) -> p r w", w=WP)
        v = v[:, k // 3:k // 3 + H, k % 3:k % 3 + W]
        xb = self.x[:, b, :].rearrange("p (r w) -> p r w", w=W)
        if k:
            dve.wait_ge(self.done[b], k)
        dve.scalar_tensor_tensor(xb, v, self.kern[:, k:k + 1], xb, ALU.mult, ALU.add).then_inc(self.done[b], 1)


def begin(nc, tools, x, xpad, gm32, loads):
    with ExitStack() as ctx:
        norm = ImageNorm(tools, ctx)
        ps = tools.ps(ctx, "n_ps", [P, ImageNorm.PS])
        x_in = [tools.sem(ctx, "x_in") for _ in range(B)]
        gm_in = tools.sem(ctx, "gm_in")
        loaded = tools.sem(ctx, "loaded")
        zeroed = tools.sem(ctx, "xpad_zeroed")
        applied = tools.sem(ctx, "applied")
        block = ctx.enter_context(nc.Block())

        @block.sync
        def _(sp):
            sp.dma_start(x[:, 0, :], loads[0][1][:, 0, :]).then_inc(x_in[0], 16)
            sp.dma_start(gm32, loads[1][1]).then_inc(gm_in, 16)
            sp.dma_start(x[:, 1, :], loads[0][1][:, 1, :]).then_inc(x_in[1], 16)
            for to, array in loads[2:]:
                sp.dma_start(to, array).then_inc(loaded, 16)
            sp.wait_ge(loaded, 16 * len(loads[2:]))

        @block.gpsimd
        def _(pool):
            pool.memset(xpad[:], 0.0).then_inc(zeroed, 1)

        @block.vector
        def _(dve):
            for b in range(B):
                dve.wait_ge(x_in[b], 16)
                norm.dve_moments(dve, x[:, b, :])
                if b:
                    dve.wait_ge(applied, b)
                norm.dve_affine(dve, b, ps[:])

        @block.tensor
        def _(pe):
            pe.wait_ge(gm_in, 16)
            for b in range(B):
                norm.pe(pe, b, gm32, ps[:])

        @block.scalar
        def _(act):
            for b in range(B):
                norm.act(act, b)
                act.wait_ge(zeroed, 1)
                to = xpad[:, b * PADDED:(b + 1) * PADDED].rearrange("p (r w) -> p r w", w=WP)
                act.activation(to[:, 1:H + 1, 1:W + 1], x[:, b, :].rearrange("p (r w) -> p r w", w=W),
                               ACT.Identity, bias=norm.shift[:], scale=norm.scale[:]).then_inc(applied, 1)


def guidance(nc, tools, xpad, w_guide, ident, ident_b, a_sel, b_sel, wta, wtb, beside):
    SLOTS = 2
    with ExitStack() as ctx:
        gps = [tools.ps(ctx, "g_ps", [P, 512])[0:NG, 0:CH] for _ in range(SLOTS)]
        gtp = [tools.ps(ctx, "gt_ps", [P, 512])[:, 0:CH].rearrange("p (t n) -> p t n", t=TPC)
               for _ in range(SLOTS)]
        wap = [tools.ps(ctx, "wa_ps", [P, 1024], BF16)[0:3 * NA, 0:CH] for _ in range(SLOTS)]
        wbp = [tools.ps(ctx, "wb_ps", [P, 1024], BF16)[0:3 * TAPS, 0:CH] for _ in range(SLOTS)]
        gsb = tools.sb(ctx, "g_sb", [P, SLOTS, CH])
        mx = tools.sb(ctx, "g_max", [P, SLOTS, TPC * NB])
        e = tools.sb(ctx, "g_exp", [P, SLOTS, TPC * NB, TAPS])
        den = tools.sb(ctx, "g_den", [P, SLOTS, TPC * NB])
        res = tools.sb(ctx, "g_res", [P, SLOTS, TPC, NG])
        wa = tools.sb(ctx, "w_a", [P, SLOTS, TPC, 3, NA], BF16)
        wb = tools.sb(ctx, "w_b", [P, SLOTS, TPC, 3, TAPS], BF16)
        zeroed = tools.sem(ctx, "g_sb_zeroed")
        cast = tools.sem(ctx, "cast")
        conv_done = tools.sem(ctx, "conv_done")
        gps_free = tools.sem(ctx, "gps_free")
        g_saved = tools.sem(ctx, "g_saved")
        turned = tools.sem(ctx, "turned")
        step = [tools.sem(ctx, f"soft_step{b}") for b in range(SLOTS)]
        shifted = tools.sem(ctx, "shifted")
        exped = tools.sem(ctx, "exped")
        split_done = tools.sem(ctx, "split_done")
        back = tools.sem(ctx, "turned_back")
        saved = tools.sem(ctx, "weights_saved")
        STEPS = 12
        block = ctx.enter_context(nc.Block())

        @block.gpsimd
        def _(pool):
            pool.memset(gsb[:], 0.0).then_inc(zeroed, 1)
            beside.pool(pool)

        @block.sync
        def _(sp):
            beside.sp(sp)

        @block.tensor
        def _(pe):
            def conv(r, b):
                pe.wait_ge(gps_free, B * r + b + 1)
                for t in range(TAPS):
                    at = b * PADDED + r * (ROWS * WP) + (t // 3) * WP + t % 3
                    win = xpad[:, bass.ds(at, ROWS * WP)].rearrange("p (r w) -> p r w", w=WP)[:, :, 0:W]
                    mm = pe.matmul(gps[b], w_guide[:, t, :], win, start=t == 0, stop=t == TAPS - 1)
                mm.then_inc(conv_done, 1)

            def turn(r):
                for b in range(B):
                    pe.wait_ge(g_saved, B * r + b + 1)
                    for t in range(TPC):
                        mm = pe.transpose(gtp[b][:, t, :], gsb[:, b, t * P:(t + 1) * P], ident)
                    mm.then_inc(turned, 1)

            def turn_back(r):
                for b in range(B):
                    pe.wait_ge(split_done, B * r + b + 1)
                    for t in range(TPC):
                        pe.transpose(wap[b][:, t * P:(t + 1) * P],
                                     wa[:, b, t, :, :].rearrange("p s k -> p (s k)"), ident_b)
                        mm = pe.transpose(wbp[b][:, t * P:(t + 1) * P],
                                          wb[:, b, t, :, :].rearrange("p s k -> p (s k)"), ident_b)
                    mm.then_inc(back, 1)

            pe.sem_inc(gps_free, SLOTS)
            for b in range(B):
                conv(0, b)
            pe.wait_ge(cast, 1)
            with pe.Fori(0, NCH - 1) as r:
                turn(r)
                conv(r + 1, 0)
                turn_back(r)
                conv(r + 1, 1)
            turn(NCH - 1)
            turn_back(NCH - 1)

        @block.scalar
        def _(act):
            act.wait_ge(zeroed, 1)
            with act.Fori(0, NCH) as r:
                for b in range(B):
                    act.wait_ge(conv_done, B * r + b + 1)
                    act.copy(gsb[0:NG, b, :], gps[b]).then_inc(g_saved, 1)
                    act.wait_ge(g_saved, B * r + b + 1)
                    act.sem_inc(gps_free, 1)
                for b in range(B):
                    act.wait_ge(shifted, B * r + b + 1)
                    act.activation(e[:, b], e[:, b], ACT.Exp).then_inc(exped, 1)
                for b in range(B):
                    act.wait_ge(back, B * r + b + 1)
                    at = b * HW + r * CH
                    act.copy(wta[:, bass.ds(at, CH)], wap[b])
                    act.copy(wtb[:, bass.ds(at, CH)], wbp[b]).then_inc(saved, 1)
                act.wait_ge(saved, B * r + B)

        @block.vector
        def _(dve):
            dve.tensor_copy(ident_b, ident).then_inc(cast, 1)
            for sel, identities in (a_sel, b_sel):
                dve.tensor_copy(sel[:], bc(identities[:], P)).then_inc(cast, 1)
            with dve.Fori(0, NCH) as r:
                def chained(b, n, ins):
                    ins.then_inc(step[b], 1)
                    dve.wait_ge(step[b], STEPS * r + n)

                for b in range(B):
                    dve.wait_ge(turned, B * r + b + 1)
                    g = gtp[b][:, :, 0:NG].rearrange("p t (n k) -> p t n k", k=TAPS)
                    chained(b, 1, dve.tensor_reduce(mx[:, b], g, AX, ALU.max))
                    dve.tensor_tensor(e[:, b].rearrange("p (t n) k -> p t n k", t=TPC), g,
                                      bc(mx[:, b].rearrange("p (t n) -> p t n", t=TPC), TAPS),
                                      ALU.subtract).then_inc(shifted, 1)
                for b in range(B):
                    dve.wait_ge(exped, B * r + b + 1)
                    chained(b, 2, dve.tensor_reduce(den[:, b], e[:, b], AX, ALU.add))
                    chained(b, 3, dve.reciprocal(den[:, b], den[:, b]))
                    r4 = res[:, b].rearrange("p t (n k) -> p (t n) k", k=TAPS)
                    chained(b, 4, dve.tensor_tensor(r4, e[:, b], bc(den[:, b], TAPS), ALU.mult))
                    ra, rb = res[:, b, :, 0:NA], res[:, b, :, NA:NG]
                    dve.tensor_copy(wa[:, b, :, 0, :], ra).then_inc(step[b], 1)
                    chained(b, 6, dve.tensor_copy(wb[:, b, :, 0, :], rb))
                    dve.tensor_tensor(ra, ra, wa[:, b, :, 0, :], ALU.subtract).then_inc(step[b], 1)
                    chained(b, 8, dve.tensor_tensor(rb, rb, wb[:, b, :, 0, :], ALU.subtract))
                    dve.tensor_copy(wa[:, b, :, 1, :], ra).then_inc(step[b], 1)
                    chained(b, 10, dve.tensor_copy(wb[:, b, :, 1, :], rb))
                    dve.tensor_tensor(wa[:, b, :, 2, :], ra, wa[:, b, :, 1, :], ALU.subtract).then_inc(step[b], 1)
                    chained(b, STEPS, dve.tensor_tensor(wb[:, b, :, 2, :], rb, wb[:, b, :, 1, :], ALU.subtract))
                    dve.sem_inc(split_done, 1)


POOLED = 4
DIRECT = (1, 3, 5)


def branch_ops():
    ops = []
    for q in range(H // (2 * ROWS)):
        for i, d in enumerate(DIL):
            taps = []
            for k in range(TAPS):
                dy, dx = (k // 3 - 1) * d, (k % 3 - 1) * d
                r0, r1 = max(2 * ROWS * q, -dy), min(2 * ROWS * (q + 1), H - dy)
                c0, c1 = max(0, -dx), min(W, W - dx)
                if r1 <= r0 or c1 <= c0:
                    continue
                n = r1 - r0
                halves = 1 if n * (c1 - c0) <= 512 else 2
                half = -(-n // halves)
                taps.append(dict(q=q, i=i, k=k, dy=dy, dx=dx, r0=r0, n=n, half=half, halves=halves,
                                 c0=c0, c1=c1, way="pe"))
            if i < POOLED:
                taps.sort(key=lambda o: o["k"] != TAPS // 2)
                whole = [o for o in taps[1:] if o["half"] * o["halves"] == o["n"]]
                odd = len(taps) - 1 - len(whole)
                for m, o in enumerate(whole):
                    if m not in DIRECT[odd:]:
                        o["way"] = "pool"
                taps[0]["way"] = "acc"
            ops += taps
    return ops


def pieces(o):
    out = []
    for h in range(o["halves"]):
        start = o["r0"] + (o["n"] - o["half"]) * h
        at = start if h == 0 else o["r0"] + o["half"]
        while at < start + o["half"]:
            to = min(start + o["half"], (at // ROWS + 1) * ROWS)
            out.append((h, at - start, to - at, at, at // ROWS % 2))
            at = to
    return out


def last_use(m, count, slots):
    return m - slots if m >= slots else max(j for j in range(count) if j % slots == m % slots) - count


def branches(nc, tools, xpad, wta, wtb, sel_a, sel_b, w_scale, y, stats, beside):
    SPREADS, LAG, ACCS, POOLS, DIRECTS = 3, 3, POOLED, 5, 4
    ops = branch_ops()
    M, CHUNKS = len(ops), H // (2 * ROWS)
    ways = {way: [n for n, o in enumerate(ops) if o["way"] == way] for way in ("acc", "pool", "pe")}
    of_way = {n: m for ns in ways.values() for m, n in enumerate(ns)}
    n_acc, n_pool, n_pe = (len(ways[way]) for way in ("acc", "pool", "pe"))
    STATS_AT = 12
    ends = [max(n for n, o in enumerate(ops) if o["q"] == q) for q in range(CHUNKS)]
    adds = [[n] if o["way"] == "pe" else [] for n, o in enumerate(ops)]
    for n in ways["acc"]:
        q, i = ops[n]["q"], ops[n]["i"]
        at = max(m for m, o in enumerate(ops) if o["q"] == q and o["i"] == i + 1)
        adds[at if i + 1 < POOLED else ends[q]].append(n)
    with ExitStack() as ctx:
        spread = [tools.ps(ctx, "spread", [P, 2, 512]) for _ in range(SPREADS)]
        yps = tools.ps(ctx, "y_ps", [P, 2, 512])
        buf = {way: [tools.sb(ctx, f"prod_{way}", [P, 2 * ROWS * W]) for _ in range(slots)]
               for way, slots in (("acc", ACCS), ("pool", POOLS), ("pe", DIRECTS))}
        spread_ready = tools.sem(ctx, "spread_ready")
        prod_ready = tools.sem(ctx, "prod_ready")
        pooled = tools.sem(ctx, "pooled")
        direct_free = tools.sem(ctx, "direct_free")
        acc_free = tools.sem(ctx, "acc_free")
        y_ready = tools.sem(ctx, "y_ready")
        y_free = tools.sem(ctx, "y_free")
        pe_spare = tools.sem(ctx, "pe_spare")
        block = ctx.enter_context(nc.Block())

        def product(n):
            slots = buf[ops[n]["way"]]
            return slots[of_way[n] % len(slots)]

        @block.tensor
        def _(pe):
            apart = Apart(pe, pe_spare)
            pe.sem_inc(direct_free, DIRECTS)
            pe.sem_inc(acc_free, ACCS)
            with pe.Fori(0, B) as b:
                def spread_op(n):
                    o = ops[n]
                    half, c0, c1 = o["half"], o["c0"], o["c1"]
                    apart.wait_ge(prod_ready, SPREADS + b * M + last_use(n, M, SPREADS) + 1)
                    wt, sel, kk = (wta, sel_a, o["i"] * TAPS + o["k"]) if o["i"] < 4 else (wtb, sel_b, o["k"])
                    for h in range(o["halves"]):
                        at = b * HW + (o["r0"] + (o["n"] - half) * h) * W
                        v = wt[:, bass.ds(at, half * W)].rearrange("p (r w) -> p r w", w=W)[:, :, c0:c1]
                        to = spread[n % SPREADS][:, h, 0:half * (c1 - c0)].rearrange("p (r w) -> p r w", r=half)
                        mm = pe.matmul(to, sel[:, kk, :], v, start=True, stop=True)
                    mm.then_inc(spread_ready, 1)

                def start_chunk(q):
                    pe.wait_ge(y_free, b * CHUNKS + q + 1)
                    for j in range(2):
                        v = xpad[:, bass.ds(b * PADDED + ((2 * q + j) * ROWS + 1) * WP, ROWS * WP)]
                        pe.matmul(yps[:, j, 0:CH].rearrange("p (r w) -> p r w", w=W), w_scale[:, 0, :],
                                  v.rearrange("p (r w) -> p r w", w=WP)[:, :, 1:W + 1], start=True, stop=False,
                                  skip_group_check=True)

                def add_op(n, last):
                    o, m = ops[n], of_way[n]
                    cols = o["c1"] - o["c0"]
                    if o["way"] == "acc":
                        m_last = max(of_way[j] for j in ways["pool"] if (ops[j]["q"], ops[j]["i"]) == (o["q"], o["i"]))
                        pe.wait_ge(pooled, POOLS + b * n_pool + m_last + 1)
                    else:
                        pe.wait_ge(prod_ready, SPREADS + b * M + n + 1)
                    for h, hr, rows, row, bank in pieces(o):
                        src = product(n)[:, (h * o["half"] + hr) * cols:(h * o["half"] + hr + rows) * cols]
                        dst = yps[:, bank, 0:CH].rearrange("p (r w) -> p r w", w=W)[
                            :, row % ROWS:row % ROWS + rows, o["c0"]:o["c1"]]
                        mm = pe.matmul(dst, w_scale[:, o["i"] + 1, :], src.rearrange("p (r w) -> p r w", r=rows),
                                       start=False, stop=last, skip_group_check=True)
                    mm.then_inc(acc_free if o["way"] == "acc" else direct_free, 1)

                for n in range(LAG):
                    spread_op(n)
                begun = -1
                for n in range(M):
                    if n + LAG < M:
                        spread_op(n + LAG)
                    q = ops[n]["q"]
                    for m in adds[n]:
                        if q > begun:
                            start_chunk(q)
                            begun = q
                        add_op(m, last=n == ends[q] and m == adds[n][-1])
                    if n == ends[q]:
                        pe.wait_ge(acc_free, ACCS + b * n_acc + (q + 1) * POOLED)
                        pe.sem_inc(y_ready, 1)

        @block.vector
        def _(dve):
            dve.sem_inc(prod_ready, SPREADS)
            free = {"acc": (acc_free, ACCS, n_acc), "pool": (pooled, POOLS, n_pool), "pe": (direct_free, DIRECTS, n_pe)}
            with dve.Fori(0, B) as b:
                for n, o in enumerate(ops):
                    sem, slots, count = free[o["way"]]
                    dve.wait_ge(sem, slots + b * count + last_use(of_way[n], count, slots) + 1)
                    dve.wait_ge(spread_ready, b * M + n + 1)
                    half, halves, cols = o["half"], o["halves"], o["c1"] - o["c0"]
                    v = xpad[:, bass.ds(b * PADDED + (o["r0"] + o["dy"] + 1) * WP, o["n"] * WP)]
                    v = v.rearrange("p (r w) -> p r w", w=WP)[:, :, o["c0"] + o["dx"] + 1:o["c1"] + o["dx"] + 1]
                    to = product(n)[:, 0:halves * half * cols]
                    w = spread[n % SPREADS]
                    if halves == 1:
                        to = to.rearrange("p (r w) -> p r w", r=half)
                        w = w[:, 0, 0:half * cols].rearrange("p (r w) -> p r w", r=half)
                    else:
                        to = to.rearrange("p (h r w) -> p h r w", h=2, r=half)
                        w = w[:, :, 0:half * cols].rearrange("p h (r w) -> p h r w", r=half)
                        v = overlapped(v, half, o["n"])
                    dve.tensor_tensor(to, w, v, ALU.mult).then_inc(prod_ready, 1)
                    if o["q"] and n == ends[o["q"] - 1] + STATS_AT:
                        dve.wait_ge(y_free, 1 + b * CHUNKS + o["q"])
                        for j in range(2):
                            at = b * NCH + 2 * (o["q"] - 1) + j
                            dve.bn_stats(stats.rearrange("p q s -> p (q s)")[:, bass.ds(at * 6, 6)],
                                         y[:, bass.ds(at * CH, CH)])

        @block.sync
        def _(sp):
            beside.sp(sp)

        @block.gpsimd
        def _(pool):
            pool.sem_inc(pooled, POOLS)
            with pool.Fori(0, B) as b:
                acc = None
                for n, o in enumerate(ops):
                    if o["way"] == "acc":
                        acc = product(n).rearrange("p (r w) -> p r w", w=W)
                    if o["way"] != "pool":
                        continue
                    pool.wait_ge(prod_ready, SPREADS + b * M + n + 1)
                    pool.wait_ge(pooled, POOLS + b * n_pool + of_way[n])
                    row, cols = o["r0"] - 2 * ROWS * o["q"], o["c1"] - o["c0"]
                    to = acc[:, row:row + o["n"], o["c0"]:o["c1"]]
                    v = product(n)[:, 0:o["n"] * cols].rearrange("p (r w) -> p r w", w=cols)
                    pool.tensor_tensor(to, to, v, ALU.add).then_inc(pooled, 1)

        @block.scalar
        def _(act):
            act.sem_inc(y_free, 1)
            beside.act(act)
            with act.Fori(0, B) as b:
                for q in range(CHUNKS):
                    act.wait_ge(y_ready, b * CHUNKS + q + 1)
                    to = y[:, bass.ds(b * HW + q * 2 * CH, 2 * CH)].rearrange("p (h n) -> p h n", h=2)
                    act.copy(to, yps[:, :, 0:CH]).then_inc(y_free, 1)


def layer0(nc, tools, a, x, xpad, gm32, gm8, ident, codes, then):
    with ExitStack() as ctx:
        w_guide = tools.sb(ctx, "w_guide", [P, TAPS, NG])
        w_scale = tools.sb(ctx, "w_scale", [P, NB + 1, P])
        gb = tools.sb(ctx, "gamma_beta", [P, 2])
        ident_b = tools.sb(ctx, "ident_b", [P, P], BF16)
        y = tools.sb(ctx, "y", [P, N])
        stats = tools.sb(ctx, "y_stats", [P, N // CH, 6])
        with ExitStack() as ctx:
            sel_a = tools.sb(ctx, "sel_a", [3 * NA, NA, P], BF16)
            sel_b = tools.sb(ctx, "sel_b", [3 * TAPS, TAPS, P], BF16)
            id3a = tools.sb(ctx, "id3a", [3 * NA, NA])
            id3b = tools.sb(ctx, "id3b", [3 * TAPS, TAPS])
            wta = tools.sb(ctx, "wta", [3 * NA, N], BF16)
            wtb = tools.sb(ctx, "wtb", [3 * TAPS, N], BF16)
            begin(nc, tools, x, xpad, gm32,
                  [(x[:], a["x"]), (gm32, a["gm32"]), (ident, a["ident"]), (gm8, a["gm8"]), (id3a[:], a["id3a"]),
                   (id3b[:], a["id3b"]), (w_guide[:], a["w_cat"]), (w_scale[:], a["w_scale"]),
                   (gb[:], a["gamma_beta"])])
            ch, cl, nc2, half_norms = codes
            with ExitStack() as parts:
                guidance(nc, tools, xpad, w_guide, ident, ident_b[:], (sel_a, id3a), (sel_b, id3b), wta, wtb,
                         CodeSplit(nc, tools, parts, a, ch, cl))
            with ExitStack() as parts:
                beside = CodeNorms(nc, tools, parts, a, nc2, half_norms)
                branches(nc, tools, xpad, wta, wtb, sel_a, sel_b, w_scale, y, stats, beside)
        then(y, stats, gb)


def norm_between(nc, tools, x, y, stats, gb, gm32, norm, z, zh, zl):
    with ExitStack() as ctx:
        ps = tools.ps(ctx, "n_ps", [P, ImageNorm.PS])
        mv = tools.sb(ctx, "bn_mv", [P, 2])
        tmp = tools.sb(ctx, "bn_tmp", [P, 1])
        s = tools.sb(ctx, "bn_scale", [P, 1])
        t = tools.sb(ctx, "bn_shift", [P, 1])
        step = tools.sem(ctx, "bn_step")
        var_ready = tools.sem(ctx, "bn_var_ready")
        rooted = tools.sem(ctx, "bn_rooted")
        affine = tools.sem(ctx, "bn_affine")
        y_normed = tools.sem(ctx, "y_normed")
        added = tools.sem(ctx, "y_added")
        z_ready = tools.sem(ctx, "z_ready")
        block = ctx.enter_context(nc.Block())

        @block.vector
        def _(dve):
            chain = Chain(dve, step)
            for b in range(B):
                for q in range(NCH - 2, NCH):
                    last = dve.bn_stats(stats[:, b * NCH + q, :], y[:, b * HW + q * CH:b * HW + (q + 1) * CH])
            chain(last)
            chain(dve.bn_aggr(mv[:], stats.rearrange("p q s -> p (q s)")))
            inv_sqrt(dve, chain, mv[:, 1:2], tmp[:], s[:], var_ready, rooted)
            chain(dve.tensor_tensor(s[:], s[:], gb[:, 0:1], ALU.mult))
            chain(dve.tensor_tensor(t[:], mv[:, 0:1], s[:], ALU.mult))
            chain(dve.tensor_tensor(t[:], gb[:, 1:2], t[:], ALU.subtract))
            dve.sem_inc(affine, 1)
            for b in range(B):
                dve.wait_ge(y_normed, b + 1)
                dve.tensor_tensor(x[:, b, :], x[:, b, :], y[:, b * HW:(b + 1) * HW], ALU.add).then_inc(added, 1)
                dve.wait_ge(added, b + 1)
                norm.dve_moments(dve, x[:, b, :])
                if b:
                    dve.wait_ge(z_ready, 1)
                norm.dve_affine(dve, b, ps[:])
            dve.wait_ge(z_ready, 2)
            dve.tensor_tensor(zl[:, 0:HW], z[:, 0:HW], zh[:, 0:HW], ALU.subtract)

        @block.tensor
        def _(pe):
            for b in range(B):
                norm.pe(pe, b, gm32, ps[:])

        @block.scalar
        def _(act):
            act.wait_ge(var_ready, 1)
            act.sqrt(tmp[:], mv[:, 1:2]).then_inc(rooted, 1)
            act.wait_ge(affine, 1)
            for b in range(B):
                v = y[:, b * HW:(b + 1) * HW]
                act.activation(v, v, ACT.Identity, bias=t[:], scale=s[:]).then_inc(y_normed, 1)
            norm.act(act, 0)
            act.activation(z[:, 0:HW], x[:, 0, :], ACT.Identity, bias=norm.shift[:], scale=norm.scale[:])\
                .then_inc(z_ready, 1)
            act.wait_ge(z_ready, 1)
            act.copy(zh[:, 0:HW], z[:, 0:HW]).then_inc(z_ready, 1)
            norm.act(act, 1)


class CodeSplit:
    SLOTS = 2

    def __init__(self, nc, tools, ctx, a, ch, cl):
        self.a, self.ch, self.cl = a, ch, cl
        self.ct = tools.sb(ctx, "codes_t", [P, self.SLOTS, PER * P])
        self.ct_in = [tools.sem(ctx, "codes_t_in") for _ in range(self.SLOTS)]
        self.high = tools.sem(ctx, "high_ready")
        self.low = tools.sem(ctx, "low_ready")

    def sp(self, sp):
        for g in range(GROUPS):
            s = g % self.SLOTS
            if g >= self.SLOTS:
                sp.wait_ge(self.low, g - self.SLOTS + 1)
            sp.dma_start(self.ct[:, s, :], self.a["codes_t"][:, g, :]).then_inc(self.ct_in[s], 16)

    def pool(self, pool):
        for g in range(GROUPS):
            s, v = g % self.SLOTS, slice(g * PER * P, (g + 1) * PER * P)
            pool.wait_ge(self.ct_in[s], 16 * (g // self.SLOTS + 1))
            pool.tensor_copy(self.ch[:, v], self.ct[:, s, :]).then_inc(self.high, 1)
            pool.wait_ge(self.high, g + 1)
            pool.tensor_tensor(self.cl[:, v], self.ct[:, s, :], self.ch[:, v], ALU.subtract).then_inc(self.low, 1)


class CodeNorms:
    SLOTS = 2

    def __init__(self, nc, tools, ctx, a, nc2, half_norms):
        self.a, self.nc2, self.half_norms = a, nc2, half_norms
        self.cn = tools.sb(ctx, "codes_n", [P, self.SLOTS, PER * P])
        self.junk = tools.sb(ctx, "squares", [P, PER, P])
        self.c2 = tools.sb(ctx, "c2", [P, GROUPS * PER])
        self.cn_in = [tools.sem(ctx, "codes_n_in") for _ in range(self.SLOTS)]
        self.squared = tools.sem(ctx, "squared")
        self.halved = tools.sem(ctx, "halved")
        self.stored = tools.sem(ctx, "half_norms_stored")

    def sp(self, sp):
        for g in range(GROUPS):
            s = g % self.SLOTS
            if g >= self.SLOTS:
                sp.wait_ge(self.squared, PER * (g - self.SLOTS + 1))
            sp.dma_start(self.cn[:, s, :], self.a["codes"][g * P:(g + 1) * P, :]).then_inc(self.cn_in[s], 16)
        sp.wait_ge(self.halved, 2)
        sp.dma_start(self.half_norms.rearrange("(g p) j -> p g j", p=P),
                     self.c2.rearrange("p (g j) -> p g j", g=GROUPS)).then_inc(self.stored, 16)
        sp.wait_ge(self.stored, 16)

    def act(self, act):
        for g in range(GROUPS):
            s = g % self.SLOTS
            act.wait_ge(self.cn_in[s], 16 * (g // self.SLOTS + 1))
            if g:
                act.wait_ge(self.squared, PER * g)
            for j in range(PER):
                act.activation(self.junk[:, j, :], self.cn[:, s, j * P:(j + 1) * P], ACT.Square,
                               accum_out=self.c2[:, g * PER + j:g * PER + j + 1]).then_inc(self.squared, 1)
        act.wait_ge(self.squared, GROUPS * PER)
        act.mul(self.nc2, self.c2[:], -0.5).then_inc(self.halved, 1)
        act.wait_ge(self.halved, 1)
        act.mul(self.c2[:], self.c2[:], 0.5).then_inc(self.halved, 1)


def search(nc, tools, a, half_norms, ident, z, zh, zl, ch, cl, nc2, x, norm, depthwise):
    PXT, STEPS = PX // P, GROUPS // 2
    NPR = 2 * PER
    BY_ACT = 2
    BY_DVE = NPR - BY_ACT
    TURN_AT = 9
    Z_TURN_AT = 12
    SLOT = [0, 1, 2, 3, 0, 4, 1, 2, 0, 3, 4, 1, 0, 2, 3, 4]
    LAST = [max(j for j in range(k - NPR, k) if SLOT[j % NPR] == SLOT[k]) for k in range(NPR)]
    with ExitStack() as ctx:
        score = [tools.ps(ctx, "score", [P, PX]) for _ in range(max(SLOT) + 1)]
        turn_ps = tools.ps(ctx, "turn_ps", [P, 2, PXT, P])
        z_ps = tools.ps(ctx, "z_ps", [P, PXT, P])
        run = [[tools.sb(ctx, "run", [P, PX]) for _ in range(2)] for _ in range(2)]
        maxima = [tools.sb(ctx, "maxima", [P, PXT, GROUPS * P]) for _ in range(2)]
        best = tools.sb(ctx, "best", [P, PXT, 8])
        block_id = tools.sb(ctx, "block_id", [P, PXT, 8], U32)
        zc = tools.sb(ctx, "zc", [P, PX])
        zt = tools.sb(ctx, "zt", [P, PXT, P])
        cand = [tools.sb(ctx, "cand", [P, PER * P]) for _ in range(2)]
        half = tools.sb(ctx, "half", [P, PXT, PER])
        fine = tools.sb(ctx, "fine", [P, PXT, PER])
        fine_best = tools.sb(ctx, "fine_best", [P, PXT, 8])
        fine_id = tools.sb(ctx, "fine_id", [P, PXT, 8], U32)
        code = tools.sb(ctx, "code", [P, PXT], U32)
        zq = tools.sb(ctx, "zq", [P, PXT, P])
        delta = tools.sb(ctx, "delta", [P, PX])

        score_ready = tools.sem(ctx, "score_ready")
        act_took = tools.sem(ctx, "act_took")
        dve_took = tools.sem(ctx, "dve_took")
        turned = tools.sem(ctx, "runs_turned")
        kept = tools.sem(ctx, "maxima_kept")
        zc_ready = tools.sem(ctx, "zc_ready")
        zt_turned = tools.sem(ctx, "zt_turned")
        zt_ready = tools.sem(ctx, "zt_ready")
        max_done = tools.sem(ctx, "max_done")
        found = tools.sem(ctx, "found")
        cand_in = [tools.sem(ctx, "cand_in") for _ in range(2)]
        multiplied = tools.sem(ctx, "multiplied")
        summed = tools.sem(ctx, "summed")
        sel_step = tools.sem(ctx, "sel_step")
        zq_in = tools.sem(ctx, "zq_in")
        zq_turned = tools.sem(ctx, "zq_turned")
        delta_ready = tools.sem(ctx, "delta_ready")
        added = tools.sem(ctx, "added")
        z1_ready = tools.sem(ctx, "z1_ready")
        dve_spare = tools.sem(ctx, "dve_spare")
        pool_spare = tools.sem(ctx, "pool_spare")
        block = ctx.enter_context(nc.Block())

        def schedule(eng, step):
            for s in range(STEPS):
                step(0, 0, s, True, False)
            eng.wait_ge(z1_ready, 3)
            with eng.Fori(0, (NPX - 1) // 2) as i:
                for h in range(2):
                    for s in range(STEPS):
                        step(2 * i + 1 + h, (1 + h) % 2, s, True, True)
            for s in range(STEPS):
                step(NPX, NPX % 2, s, False, True)

        def first(n):
            return isinstance(n, int) and n == 0

        @block.tensor
        def _(pe):
            def turn(n, s):
                S = n * STEPS + s
                pe.wait_ge(dve_took, BY_DVE * (S + 1))
                if not first(n) or s >= 1:
                    pe.wait_ge(kept, S)
                for h in range(2):
                    for u in range(PXT):
                        mm = pe.transpose(turn_ps[:, h, u, :], run[s % 2][h][:, u * P:(u + 1) * P], ident)
                mm.then_inc(turned, 1)

            def turn_z(n):
                pe.wait_ge(zc_ready, n)
                pe.wait_ge(delta_ready, n)
                for u in range(PXT):
                    mm = pe.transpose(z_ps[:, u, :], zc[:, u * P:(u + 1) * P], ident)
                mm.then_inc(zt_turned, 1)

            def step(n, par, s, main, post):
                S = n * STEPS + s
                for k in range(NPR if main else 0):
                    last = LAST[k]
                    if last >= BY_ACT:
                        pe.wait_ge(dve_took, BY_DVE * S + last - BY_ACT + 1)
                    elif last >= 0:
                        pe.wait_ge(act_took, BY_ACT * S + last + 1)
                    elif not first(n) or s > 0:
                        pe.wait_ge(dve_took, BY_DVE * S + last + 1)
                    m = (2 * s + k % 2) * PER + k // 2
                    w = slice(m * P, (m + 1) * P)
                    at = bass.ds(n * PX, PX)
                    o = score[SLOT[k]][:]
                    pe.matmul(o, ch[:, w], zh[:, at], start=True, stop=False)
                    pe.matmul(o, ch[:, w], zl[:, at], start=False, stop=False)
                    pe.matmul(o, cl[:, w], zh[:, at], start=False, stop=True).then_inc(score_ready, 1)
                    if k == TURN_AT and (s or not first(n)):
                        turn(n, s - 1)
                    if k == Z_TURN_AT and post and s == 0:
                        turn_z(n)
                if not main and s == 0:
                    turn(n, -1)
                if not main and s == 2:
                    depthwise.pe_norm(pe, 0, score[0])
                    depthwise.pe_kernels(pe, 0, score[0])
                if post and s == 0 and not main:
                    turn_z(n)
                if post and s == STEPS - 1:
                    pe.wait_ge(zq_in, 16 * PXT * n)
                    for u in range(PXT):
                        mm = pe.transpose(z_ps[:, u, :], zq[:, u, :], ident)
                    mm.then_inc(zq_turned, 1)

            pe.sem_inc(zq_turned, 1)
            schedule(pe, step)

        @block.scalar
        def _(act):
            def sum_products(n, u):
                act.wait_ge(multiplied, PXT * (n - 1) + u + 1)
                for j in range(PER):
                    v = cand[u % 2][:, j * P:(j + 1) * P]
                    act.activation(v, v, ACT.Identity, accum_out=fine[:, u, j:j + 1]).then_inc(summed, 1)

            def step(n, par, s, main, post):
                S = n * STEPS + s
                if main:
                    if not first(n) or s >= 2:
                        act.wait_ge(turned, S - 1)
                    for k in range(BY_ACT):
                        m = (2 * s + k) * PER
                        act.wait_ge(score_ready, NPR * S + k + 1)
                        act.activation(run[s % 2][k][:], score[SLOT[k]][:], ACT.Identity, bias=nc2[:, m:m + 1])\
                            .then_inc(act_took, 1)
                if post and s == 0:
                    act.copy(zc[:], z[:, bass.ds((n - 1) * PX, PX)]).then_inc(zc_ready, 1)
                if post and s >= 2:
                    sum_products(n, 2 * (s - 2) + 1)
                if (main and (s or not first(n))) or (not main and s == 0):
                    ps, ppar = (s - 1) % STEPS, par if s else 1 - par
                    if ps == 0 and main and not first(n):
                        act.wait_ge(found, 1 + PXT * (n - 1))
                    act.wait_ge(turned, S)
                    for h in range(2):
                        g = 2 * ps + h
                        cp = act.copy(maxima[ppar][:, :, g * P:(g + 1) * P], turn_ps[:, h])
                    cp.then_inc(kept, 1)
                if post and s == 0:
                    act.wait_ge(zt_turned, n)
                    act.copy(zt[:], z_ps[:]).then_inc(zt_ready, 1)
                if post and s in (1, 2):
                    sum_products(n, 2 * (s - 1))
                if not main and s == 1:
                    depthwise.act_norm(act, 0)

            schedule(act, step)

        @block.vector
        def _(dve):
            apart = Apart(dve, dve_spare)

            def find(n, u):
                if u == 0:
                    apart.wait_ge(kept, STEPS * n)
                dve.max(best[:, u, :], maxima[1 - par_of[0]][:, u, :]).then_inc(max_done, 1)

            def place(n, u):
                apart.wait_ge(max_done, PXT * (n - 1) + u + 1)
                dve.max_index(block_id[:, u, :], best[:, u, :], maxima[1 - par_of[0]][:, u, :]).then_inc(found, 1)


            def subtract(n, u):
                dve.wait_ge(summed, PER * (PXT * (n - 1) + u + 1))
                dve.tensor_tensor(fine[:, u, :], fine[:, u, :], half[:, u, :], ALU.subtract).then_inc(sel_step, 1)

            def fine_find(n, u):
                apart.wait_ge(sel_step, 1 + 4 * (PXT * (n - 1) + u) + 1)
                dve.max(fine_best[:, u, :], fine[:, u, :]).then_inc(sel_step, 1)

            def fine_place(n, u):
                apart.wait_ge(sel_step, 1 + 4 * (PXT * (n - 1) + u) + 2)
                dve.max_index(fine_id[:, u, :], fine_best[:, u, :], fine[:, u, :]).then_inc(sel_step, 1)

            def select(n, u):
                c = n - 1
                dve.wait_ge(sel_step, 1 + 4 * (PXT * c + u) + 3)
                dve.wait_ge(found, 1 + PXT * c + u + 1)
                dve.scalar_tensor_tensor(code[:, u:u + 1], block_id[:, u, 0:1], float(PER),
                                         fine_id[:, u, 0:1], ALU.mult, ALU.add).then_inc(sel_step, 1)

            def depthwise_part(part, u):
                if (part, u) == (place, 3):
                    dve.wait_ge(added, 1 + 2 * -(-HW // PX))
                    depthwise.norm.dve_moments(dve, x[:, 0:HW])
                    depthwise.dve_norm(dve, 0, score[0])
                if (part, u) == (select, 0):
                    depthwise.dve_kernels(dve, 0, score[0])
                if part == select and u:
                    for k in (2 * u - 2, 2 * u - 1):
                        depthwise.tap(dve, 0, k)

            par_of = [0]
            parts = {(0, 12): (find, 0), (0, 14): (place, 0), (1, 2): (find, 1), (1, 4): (place, 1),
                     (1, 6): (find, 2), (1, 8): (place, 2), (1, 10): (find, 3), (1, 12): (place, 3),
                     **{(s, k + i): (part, u)
                        for s, k, u in ((2, 4, 0), (2, 9, 1), (3, 2, 2), (3, 6, 3))
                        for i, part in enumerate((subtract, fine_find, fine_place, select))}}

            def step(n, par, s, main, post):
                S = n * STEPS + s
                par_of[0] = par
                for k in range(BY_ACT, NPR):
                    if main:
                        g, m = 2 * s + k % 2, (2 * s + k % 2) * PER + k // 2
                        dve.wait_ge(score_ready, NPR * S + k + 1)
                        if k < 2 * BY_ACT:
                            dve.wait_ge(act_took, BY_ACT * S + k - BY_ACT + 1)
                        else:
                            dve.wait_ge(dve_took, BY_DVE * S + k - BY_ACT - 1)
                        r = run[s % 2][k % 2][:]
                        dve.scalar_tensor_tensor(r, score[SLOT[k]][:], nc2[:, m:m + 1], r,
                                                 ALU.add, ALU.max).then_inc(dve_took, 1)
                    if post and (s, k) in parts:
                        part, u = parts[s, k]
                        part(n, u)
                        if not main:
                            depthwise_part(part, u)
                if post and s == STEPS - 1:
                    dve.wait_ge(zq_turned, 1 + n)
                    dve.wait_ge(added, 1 + 2 * (n - 1))
                    dve.tensor_tensor(delta[:], z_ps.rearrange("p u c -> p (u c)"), z[:, bass.ds((n - 1) * PX, PX)],
                                      ALU.subtract)\
                        .then_inc(delta_ready, 1)

            dve.sem_inc(found, 1)
            dve.sem_inc(delta_ready, 1)
            dve.sem_inc(sel_step, 1)
            schedule(dve, step)
            for k in range(2 * (PXT - 1), TAPS):
                depthwise.tap(dve, 0, k)

        @block.sync
        def _(sp):
            depthwise.sp(sp)

        @block.gpsimd
        def _(pool):
            apart = Apart(pool, pool_spare)

            def gather(n, u):
                c = n - 1
                apart.wait_ge(found, 1 + PXT * c + u + 1)
                if u >= 2:
                    apart.wait_ge(summed, PER * (PXT * c + u - 1))
                else:
                    apart.wait_ge(sel_step, 1 + 4 * PXT * c)
                off = bass.IndirectOffsetOnAxis(block_id[:, u, 0:1], 0)
                pool.indirect_dma_start(cand[u % 2][:], None, a["codes"], off).then_inc(cand_in[u % 2], 16)
                pool.indirect_dma_start(half[:, u, :], None, half_norms, off).then_inc(cand_in[u % 2], 16)

            def multiply(n, u):
                pool.wait_ge(cand_in[u % 2], 32 * (2 * (n - 1) + u // 2 + 1))
                if u == 0:
                    pool.wait_ge(zt_ready, n)
                v = cand[u % 2].rearrange("p (j c) -> p j c", c=P)
                zb = zt[:, u, :].unsqueeze(1).to_broadcast([P, PER, P])
                pool.tensor_tensor(v, v, zb, ALU.mult).then_inc(multiplied, 1)

            def fetch(n, u):
                c = n - 1
                apart.wait_ge(sel_step, 1 + 4 * (PXT * c + u + 1))
                if u == 0:
                    apart.wait_ge(zq_turned, 1 + c)
                pool.indirect_dma_start(zq[:, u, :], None, a["codes"].rearrange("r (j c) -> (r j) c", c=P),
                                        bass.IndirectOffsetOnAxis(code[:, u:u + 1], 0)).then_inc(zq_in, 16)

            def step(n, par, s, main, post):
                if not post:
                    return
                if s == 1:
                    gather(n, 0)
                    gather(n, 1)
                    multiply(n, 0)
                    multiply(n, 1)
                if s == 2:
                    gather(n, 2)
                    multiply(n, 2)
                    gather(n, 3)
                    fetch(n, 0)
                    multiply(n, 3)
                    fetch(n, 1)
                if s == STEPS - 1:
                    fetch(n, 2)
                    fetch(n, 3)
                    at = bass.ds((n - 1) * PX, PX)
                    pool.wait_ge(delta_ready, 1 + n)
                    pool.tensor_tensor(delta[:], delta[:], z[:, at], ALU.add).then_inc(added, 1)
                    pool.wait_ge(added, 1 + 2 * (n - 1) + 1)
                    pool.tensor_tensor(x[:, at], x[:, at], delta[:], ALU.add).then_inc(added, 1)

            pool.sem_inc(added, 1)
            v = slice(HW, 2 * HW)
            pool.tensor_scalar(z[:, v], x[:, v], norm.scale[:], norm.shift[:], ALU.mult, ALU.add)\
                .then_inc(z1_ready, 1)
            pool.wait_ge(z1_ready, 1)
            pool.tensor_copy(zh[:, v], z[:, v]).then_inc(z1_ready, 1)
            pool.wait_ge(z1_ready, 2)
            pool.tensor_tensor(zl[:, v], z[:, v], zh[:, v], ALU.subtract).then_inc(z1_ready, 1)
            schedule(pool, step)


TABLE_PAD = W + 1
CORNERS = 4
JOBS = 2 * B
ITILES = TILES // B


def layer3(nc, tools, a, x, xpad, gm32, gm8, ident, depthwise, out):
    QUAD = CORNERS * P
    M = ITILES * TAPS
    LEAD_STORES = 2
    HALVES = [slice(h * HW // 2, (h + 1) * HW // 2) for h in range(2)]
    with ExitStack() as ctx:
        y = tools.sb(ctx, "y3", [P, B, HW])
        w_tap = [tools.sb(ctx, "w_tap", [P, TAPS, P]) for _ in range(2)]
        gn = [tools.sb(ctx, "gn_sb", [P, 2]) for _ in range(2)]
        w_off = [tools.sb(ctx, "w_off", [P, TAPS, 2 * TAPS]) for _ in range(2)]
        b_off = [tools.sb(ctx, "b_off", [2 * TAPS, 1]) for _ in range(2)]
        base = tools.sb(ctx, "base", [P, ITILES, 2 * TAPS])
        table = [nc.dram_tensor(f"corners{j}", [TABLE_PAD + HW, CORNERS, P], F32).ap() for j in range(JOBS)]
        zeros = tools.sb(ctx, "zeros", [TABLE_PAD, QUAD])
        osb = tools.sb(ctx, "off_sb", [P, CH])
        xc = tools.sb(ctx, "x_chunk", [P, CH])
        xt = tools.sb(ctx, "x_turned", [P, NCH, CH])
        pos = tools.sb(ctx, "pos", [P, 2 * M])
        low = tools.sb(ctx, "low", [P, 2 * M])
        entry = tools.sb(ctx, "entry", [P, M])
        side = tools.sb(ctx, "side_weights", [P, 2 * M, 2])
        weights = [tools.sb(ctx, "weights", [P, M * CORNERS]) for _ in range(B)]
        index = [tools.sb(ctx, "index", [P, M], U32) for _ in range(B)]
        off_ps = tools.ps(ctx, "off_ps", [P, 512])[0:2 * TAPS, 0:CH]
        otp = tools.ps(ctx, "off_t_ps", [P, 512])[:, 0:CH].rearrange("p (t n) -> p t n", t=TPC)
        xtp = tools.ps(ctx, "x_t_ps", [P, 512])[:, 0:CH].rearrange("p (t n) -> p t n", t=TPC)
        idx = [tools.sb(ctx, "chunk_index", [P, TPC * TAPS], U32) for _ in range(2)]
        quads = [tools.sb(ctx, "quads", [P, TAPS, QUAD]) for _ in range(TPC)]
        sampled = [tools.sb(ctx, "sampled", [P, TAPS, P]) for _ in range(TPC)]
        turned = [tools.sb(ctx, "sampled_t", [P, 3 * P]) for _ in range(3)]
        tps = [tools.ps(ctx, "sampled_t_ps", [P, 512])[:, 0:3 * P] for _ in range(3)]
        yps = tools.ps(ctx, "mixed_ps", [P, 512])[:, 0:P]
        lead_ps = [xtp.rearrange("p t c -> p (t c)"), *tps]
        norm_ = ImageNorm(tools, ctx)
        gps = tools.ps(ctx, "n_ps", [P, ImageNorm.PS + Depthwise.PS])
        nps, dps = gps[:, 0:ImageNorm.PS], gps[:, ImageNorm.PS:]

        zeroed = tools.sem(ctx, "zeroed")
        chunk_ready = tools.sem(ctx, "chunk_ready")
        x_turned = tools.sem(ctx, "x_turned")
        x_saved = tools.sem(ctx, "x_saved")
        ends_stored = tools.sem(ctx, "table_ends_stored")
        stored = tools.sem(ctx, "table_stored")
        conv_done = tools.sem(ctx, "off_conv_done")
        off_saved = tools.sem(ctx, "off_saved")
        off_turned = tools.sem(ctx, "off_turned")
        pos_ready = tools.sem(ctx, "pos_ready")
        corner_step = tools.sem(ctx, "corner_step")
        index_ready = tools.sem(ctx, "index_ready")
        idx_ready = tools.sem(ctx, "idx_ready")
        quads_in = [tools.sem(ctx, "quads_in") for _ in range(TPC)]
        weighted = tools.sem(ctx, "weighted")
        paired = tools.sem(ctx, "paired")
        sampled_ready = tools.sem(ctx, "sampled_ready")
        turn_done = tools.sem(ctx, "turn_done")
        turn_saved = tools.sem(ctx, "turn_saved")
        mixed = tools.sem(ctx, "mixed")
        y_saved = tools.sem(ctx, "y_saved")
        relued = tools.sem(ctx, "relued")
        added = tools.sem(ctx, "added")
        out_stored = tools.sem(ctx, "out_stored")
        pool_spare = tools.sem(ctx, "pool_spare")

        loads = [(base[:], a["base"][:, 0:ITILES])] + [
            (to[s][:], a[f"{name}{s + 1}"]) for s in range(2)
            for to, name in ((w_off, "w_off"), (b_off, "b_off"), (w_tap, "w_tap"), (gn, "gn"))]
        loaded = tools.sem(ctx, "weights_loaded")
        block = ctx.enter_context(nc.Block())

        def sections(eng, norm, prepare, tile, lead, finish=lambda j: None, late=False):
            def double(k, r, c):
                nxt = k + 1 < JOBS
                if nxt and not late:
                    prepare(k + 1, c, "turn")
                tile(k, r, 0)
                if nxt and not late:
                    prepare(k + 1, c + 1, "x")
                    prepare(k + 1, c + 1, "conv")
                    prepare(k + 1, c + 1, "turn")
                tile(k, r, 1)
                if nxt and late:
                    prepare(k + 1, c, "turn")
                tile(k, r, 2)
                if nxt and late:
                    prepare(k + 1, c + 1, "turn")

            norm(0)
            if late:
                lead()
            else:
                lead("x")
                lead("norm")
                with eng.Fori(0, NCH) as r:
                    prepare(0, r, "conv")
                    prepare(0, r, "turn")
            for k in range(JOBS):
                nxt = k + 1 < JOBS
                if late and k == 0:
                    norm(k + 1)
                else:
                    tile(k, 0, 0)
                    if not late:
                        norm(k + 1)
                    tile(k, 0, 1)
                    if late:
                        norm(k + 1)
                    tile(k, 0, 2)
                if nxt:
                    prepare(k + 1, 0, "x")
                    prepare(k + 1, 0, "conv")
                double(k, 1, 0)
                if nxt:
                    prepare(k + 1, 2, "x")
                    prepare(k + 1, 2, "conv")
                with eng.Fori(2, NCH - 2) as r:
                    if nxt and not late:
                        prepare(k + 1, r, "turn")
                    tile(k, r, 0)
                    tile(k, r, 1)
                    if nxt and late:
                        prepare(k + 1, r, "turn")
                    tile(k, r, 2)
                    if nxt:
                        prepare(k + 1, r + 1, "x")
                        prepare(k + 1, r + 1, "conv")
                double(k, NCH - 2, NCH - 2)
                if nxt:
                    finish(k + 1)
                for u in range(TPC):
                    tile(k, NCH - 1, u)
            norm(JOBS + 1)

        def tile_no(j, r, u):
            return ITILES * j + TPC * r + u

        def chunk_no(j, r):
            return NCH * j + r

        def stored_by(j):
            return 16 * CORNERS * (1 + LEAD_STORES + NCH * j)

        def inner(b):
            return xpad[:, b * PADDED:(b + 1) * PADDED].rearrange("p (r w) -> p r w", w=WP)[:, 1:H + 1, 1:W + 1]

        @block.tensor
        def _(pe):
            def norm(m):
                norm_.pe(pe, m, gm32 if m < B else gm8, nps)
                if m == 0:
                    pe.wait_ge(loaded, 16 * len(loads))

            def prepare(j, r, part):
                C = chunk_no(j, r)
                if part == "x":
                    pe.wait_ge(chunk_ready, C + 1)
                    pe.wait_ge(x_saved, C + 1)
                    for t in range(TPC):
                        mm = pe.transpose(xtp[:, t, :], xc[:, t * P:(t + 1) * P], ident)
                    mm.then_inc(x_turned, 1)
                elif part == "conv":
                    pe.wait_ge(off_saved, C + 1)
                    for t in range(TAPS):
                        at = j % B * PADDED + r * (ROWS * WP) + (t // 3) * WP + t % 3
                        win = xpad[:, bass.ds(at, ROWS * WP)].rearrange("p (r w) -> p r w", w=WP)[:, :, 0:W]
                        mm = pe.matmul(off_ps, w_off[j // B][:, t, :], win, start=t == 0, stop=t == TAPS - 1)
                    mm.then_inc(conv_done, 1)
                else:
                    pe.wait_ge(off_saved, C + 2)
                    pe.wait_ge(pos_ready, C + 1)
                    for t in range(TPC):
                        mm = pe.transpose(otp[:, t, :], osb[:, t * P:(t + 1) * P], ident)
                    mm.then_inc(off_turned, 1)

            def tile(j, r, u):
                T = tile_no(j, r, u)
                pe.wait_ge(sampled_ready, TPC + T + 1)
                for g in range(3):
                    pe.wait_ge(turn_saved, 3 * T + g + 1)
                    for k in range(3):
                        mm = pe.transpose(tps[g][:, k * P:(k + 1) * P], sampled[u][:, 3 * g + k, :], ident)
                    mm.then_inc(turn_done, 1)
                pe.wait_ge(y_saved, T + 1)
                for g in range(3):
                    pe.wait_ge(turn_saved, 3 + 3 * T + g + 1)
                    for k in range(3):
                        mm = pe.matmul(yps, w_tap[j // B][:, 3 * g + k, :], turned[g][:, k * P:(k + 1) * P],
                                       start=g + k == 0, stop=g + k == 4)
                    mm.then_inc(mixed, 1)

            pe.sem_inc(x_turned, 1)
            pe.sem_inc(off_turned, 1)
            pe.sem_inc(turn_done, 3 * TPC)
            pe.sem_inc(mixed, 3)

            def lead(part):
                if part == "x":
                    pe.wait_ge(chunk_ready, NCH)
                    for c in range(NCH):
                        if c >= len(lead_ps):
                            pe.wait_ge(x_saved, 1 + c - len(lead_ps) + 1)
                        for t in range(TPC):
                            at = (TPC * c + t) * P
                            mm = pe.transpose(lead_ps[c % len(lead_ps)][:, t * P:(t + 1) * P],
                                              y[:, 1, at:at + P], ident)
                        mm.then_inc(x_turned, 1)
                elif part == "norm":
                    depthwise.pe_norm(pe, 1, dps)
                    depthwise.pe_kernels(pe, 1, dps)
                    pe.wait_ge(relued, 2)
                    pe.wait_ge(x_saved, 1 + NCH)

            sections(pe, norm, prepare, tile, lead)

        @block.scalar
        def _(act):
            def norm(m):
                b = m % B
                norm_.act(act, m)
                if m == 0:
                    act.activation(y[:, 1, :], x[:, 0, :], ACT.Identity, bias=norm_.shift[:], scale=norm_.scale[:])\
                        .then_inc(chunk_ready, NCH)
                    act.wait_ge(loaded, 16 * len(loads))
                for h in range(2):
                    src = to = (x if m < B else y)[:, b, HALVES[h]]
                    if m < JOBS:
                        src = src.rearrange("p (r w) -> p r w", w=W)
                        to = inner(b)[:, h * H // 2:(h + 1) * H // 2, :]
                    act.activation(to, src, ACT.Identity if m < B else ACT.Relu,
                                   bias=norm_.shift[:], scale=norm_.scale[:])\
                        .then_inc(relued, 1)

            def prepare(j, r, part):
                C = chunk_no(j, r)
                if part == "x":
                    at = j % B * PADDED + (r * ROWS + 1) * WP + 1
                    v = xpad[:, bass.ds(at, ROWS * WP)].rearrange("p (r w) -> p r w", w=WP)[:, :, 0:W]
                    act.wait_ge(x_turned, C + 1)
                    act.wait_ge(relued, 2 * (j + 1))
                    act.copy(xc.rearrange("p (r w) -> p r w", w=W), v).then_inc(chunk_ready, 1)
                    act.wait_ge(x_turned, C + 2)
                    act.wait_ge(stored, stored_by(j - 1))
                    act.copy(xt.rearrange("p r c -> p (r c)")[:, bass.ds(r * CH, CH)],
                             xtp.rearrange("p t c -> p (t c)")).then_inc(x_saved, 1)
                elif part == "conv":
                    act.wait_ge(conv_done, C + 1)
                    act.wait_ge(off_turned, C + 1)
                    act.activation(osb[0:2 * TAPS, :], off_ps, ACT.Identity, bias=b_off[j // B][:])\
                        .then_inc(off_saved, 1)

            def tile(j, r, u):
                T = tile_no(j, r, u)
                for g in range(3):
                    act.wait_ge(turn_done, 3 * TPC + 3 * T + g + 1)
                    act.wait_ge(mixed, 3 * T + g + 1)
                    act.copy(turned[g][:], tps[g]).then_inc(turn_saved, 1)
                act.wait_ge(mixed, 3 + 3 * T + 3)
                act.copy(y[:, j % B, bass.ds((TPC * r + u) * P, P)], yps).then_inc(y_saved, 1)

            act.sem_inc(x_saved, 1)
            act.sem_inc(off_saved, 1)
            act.sem_inc(stored, 16 * CORNERS)
            act.sem_inc(turn_saved, 3)
            act.sem_inc(y_saved, 1)
            act.wait_ge(zeroed, 2)

            def lead(part):
                if part == "x":
                    for c in range(NCH):
                        act.wait_ge(x_turned, c + 2)
                        act.copy(xt[:, c, :], lead_ps[c % len(lead_ps)]).then_inc(x_saved, 1)
                elif part == "norm":
                    depthwise.act_norm(act, 1)

            sections(act, norm, prepare, tile, lead)

        @block.vector
        def _(dve):
            corner_chain = Chain(dve, corner_step)

            def norm(m):
                b, j = m % B, m - B
                if j < 0:
                    dve.wait_ge(depthwise.done[b], TAPS)
                    norm_.dve_moments(dve, x[:, b, :])
                else:
                    norm_.dve_moments(dve, y[:, b, :],
                                      lambda q: dve.wait_ge(y_saved, 1 + ITILES * j + TPC * (q + 1)))
                norm_.dve_affine(dve, m, nps, gn[j // B] if j >= 0 else None)
                if j >= B:
                    for h in range(2):
                        v = HALVES[h]
                        dve.wait_ge(relued, 2 * m + h + 1)
                        dve.tensor_tensor(x[:, b, v], x[:, b, v], y[:, b, v], ALU.add).then_inc(added, 1)

            def prepare(j, r, part):
                if part == "turn":
                    C = chunk_no(j, r)
                    dve.wait_ge(off_turned, 1 + C + 1)
                    at = bass.ds(r * (TPC * 2 * TAPS), TPC * 2 * TAPS)
                    dve.tensor_tensor(pos[:, at].rearrange("p (t k) -> p t k", t=TPC), otp[:, :, 0:2 * TAPS],
                                      base.rearrange("p t k -> p (t k)")[:, at].rearrange("p (t k) -> p t k", t=TPC),
                                      ALU.add).then_inc(pos_ready, 1)

            def place(j, r, rows):
                chain = corner_chain
                dve.wait_ge(pos_ready, 1 + chunk_no(j, r + rows))
                n = TPC * TAPS
                v, m = slice(2 * n * r, 2 * n * (r + rows)), slice(n * r, n * (r + rows))
                chain(dve.tensor_scalar(low[:, v], pos[:, v], -0.5, 0.0, ALU.add, ALU.max))
                chain(dve.tensor_scalar(low[:, v], low[:, v], float(H - 2), ROUND, ALU.min, ALU.add))
                chain(dve.tensor_scalar(low[:, v], low[:, v], -ROUND, None, ALU.add))
                lo = low[:, v].rearrange("p (m a) -> p m a", a=2)
                chain(dve.scalar_tensor_tensor(entry[:, m], lo[:, :, 0], float(W), lo[:, :, 1], ALU.mult, ALU.add))
                dve.tensor_scalar(index[j % B][:, m], entry[:, m], float(TABLE_PAD), None, ALU.add)\
                    .then_inc(index_ready, rows)

            def weigh(j, r, rows):
                chain = corner_chain
                n = TPC * TAPS
                v = slice(2 * n * r, 2 * n * (r + rows))
                p, sd = pos[:, v], side[:, v, :]
                chain(dve.tensor_tensor(p, p, low[:, v], ALU.subtract))
                dve.tensor_scalar(sd[:, :, 0], p, -1.0, 1.0, ALU.mult, ALU.add).then_inc(corner_step, 1)
                dve.tensor_scalar(sd[:, :, 1], p, -1.0, 2.0, ALU.mult, ALU.add).then_inc(corner_step, 1)
                dve.wait_ge(corner_step, chain.n + 1)
                dve.scalar_tensor_tensor(sd[:, :, 0], p, 1.0, sd[:, :, 0], ALU.add, ALU.min)\
                    .then_inc(corner_step, 1)
                dve.wait_ge(corner_step, chain.n + 2)
                chain.n += 3
                chain(dve.tensor_tensor(sd[:, :, 1], p, sd[:, :, 1], ALU.min))
                chain(dve.tensor_scalar(sd, sd, 0.0, None, ALU.max))
                sd = sd.rearrange("p (m a) s -> p m a s", a=2)
                w = weights[j % B][:, n * CORNERS * r:n * CORNERS * (r + rows)]
                for dy in range(2):
                    yw = sd[:, :, 0, dy:dy + 1].to_broadcast([P, n * rows, 2])
                    chain(dve.tensor_tensor(w.rearrange("p (m d s) -> p m d s", d=2, s=2)[:, :, dy, :],
                                            sd[:, :, 1, :], yw, ALU.mult))

            def finish(j):
                place(j, 0, NCH)
                weigh(j, 0, NCH)

            def lead():
                depthwise.norm.dve_moments(dve, x[:, 1, :])
                depthwise.dve_norm(dve, 1, dps)
                depthwise.dve_kernels(dve, 1, dps)
                dve.wait_ge(loaded, 16 * len(loads))
                TAPS_AT = 2, 2, 1, 1, 0, 0
                taps = iter(range(TAPS))

                def depthwise_taps(n):
                    for _ in range(n):
                        depthwise.tap(dve, 1, next(taps))

                depthwise_taps(3)
                for r, n in enumerate(TAPS_AT):
                    prepare(0, r, "turn")
                    place(0, r, 1)
                    if r == 2:
                        weigh(0, 0, 1)
                    if r >= 2 and r - 2 < TPC:
                        tile(0, 0, r - 2)
                    depthwise_taps(n)
                weigh(0, 1, NCH - 1)

            def tile(j, r, u):
                T = tile_no(j, r, u)
                q = quads[u]
                q4 = q.rearrange("p k (j c) -> p (k j) c", c=P)
                w = weights[j % B][:, bass.ds((TPC * r + u) * (TAPS * CORNERS), TAPS * CORNERS)]
                dve.wait_ge(quads_in[u], 16 * TAPS * (chunk_no(j, r) + 1))
                dve.tensor_tensor(q4, q4, bc(w, P), ALU.mult).then_inc(weighted, 1)
                if u:
                    gather_up(j, r, u - 1)
                dve.wait_ge(weighted, T + 1)
                dve.tensor_tensor(q[:, :, 0:2 * P], q[:, :, 0:2 * P], q[:, :, 2 * P:], ALU.add).then_inc(paired, 1)
                if u == TPC - 1:
                    gather_up(j, r, u)

            def gather_up(j, r, u):
                T = tile_no(j, r, u)
                dve.wait_ge(paired, T + 1)
                dve.wait_ge(turn_done, 3 * T + 3)
                dve.tensor_tensor(sampled[u][:], quads[u][:, :, 0:P], quads[u][:, :, P:2 * P], ALU.add)\
                    .then_inc(sampled_ready, 1)

            dve.sem_inc(pos_ready, 1)
            sections(dve, norm, prepare, tile, lead, finish, late=True)

        @block.gpsimd
        def _(pool):
            apart = Apart(pool, pool_spare)

            def chunk(j, r, par):
                apart.wait_ge(index_ready, chunk_no(j, r) + 1)
                pool.tensor_copy(idx[par][:], index[j % B][:, bass.ds(r * (TPC * TAPS), TPC * TAPS)])\
                    .then_inc(idx_ready, 1)
                apart.wait_ge(idx_ready, chunk_no(j, r) + 1)
                for u in range(TPC):
                    apart.wait_ge(sampled_ready, tile_no(j, r, u) + 1)
                    for k in range(TAPS):
                        at = u * TAPS + k
                        pool.indirect_dma_start(quads[u][:, k, :], None, table[j].rearrange("n s c -> n (s c)"),
                                                bass.IndirectOffsetOnAxis(idx[par][:, at:at + 1], 0))\
                            .then_inc(quads_in[u], 16)

            pool.sem_inc(sampled_ready, TPC)
            pool.memset(osb[:], 0.0).then_inc(zeroed, 1)
            pool.memset(zeros[:], 0.0).then_inc(zeroed, 1)
            for j in range(JOBS):
                apart.wait_ge(stored, stored_by(j))
                apart.wait_ge(ends_stored, 16 * 2 * JOBS)
                with pool.Fori(0, NCH // 2) as i:
                    for par in range(2):
                        chunk(j, 2 * i + par, par)

        @block.sync
        def _(sp):
            for to, array in loads:
                sp.dma_start(to, array).then_inc(loaded, 16)
            sp.wait_ge(zeroed, 2)
            for j in range(JOBS):
                flat = table[j].rearrange("n s c -> n (s c)")
                sp.dma_start(flat[0:TABLE_PAD, :], zeros[:]).then_inc(ends_stored, 16)
                sp.dma_start(flat[HW:HW + TABLE_PAD, :], zeros[:]).then_inc(ends_stored, 16)
            sp.wait_ge(ends_stored, 16 * 2 * JOBS)

            def store(j, r, rows):
                flat = table[j].rearrange("n s c -> n (s c)")
                for s in range(CORNERS):
                    at = TABLE_PAD + r * CH - (s // 2 * W + s % 2)
                    to = flat[bass.ds(at, rows * CH), s * P:(s + 1) * P].rearrange("(t p) c -> p t c", p=P)
                    v = xt.rearrange("p r c -> p (r c)")[:, bass.ds(r * CH, rows * CH)]
                    sp.dma_start(to, v.rearrange("p (t c) -> p t c", c=P)).then_inc(stored, 16)

            for h in range(LEAD_STORES):
                rows = NCH // LEAD_STORES
                sp.wait_ge(x_saved, 1 + (h + 1) * rows)
                store(0, h * rows, rows)
            for j in range(1, JOBS):
                with sp.Fori(0, NCH) as r:
                    sp.wait_ge(x_saved, 1 + chunk_no(j, r) + 1)
                    store(j, r, 1)
            for b in range(B):
                for h in range(2):
                    sp.wait_ge(added, 2 * b + h + 1)
                    sp.dma_start(out[:, b, HALVES[h]], x[:, b, HALVES[h]]).then_inc(out_stored, 16)
            sp.wait_ge(stored, stored_by(JOBS - 1))
            sp.wait_ge(out_stored, 16 * 2 * B)


def program(nc, a, out):
    tools = Tools(nc)
    with ExitStack() as ctx:
        x = tools.sb(ctx, "x", [P, B, HW])
        xpad = tools.sb(ctx, "xpad", [P, B * PADDED + WP])
        ident = tools.sb(ctx, "ident", [P, P])[:]
        gm32 = tools.sb(ctx, "gm32", [P, P])[:]
        gm8 = tools.sb(ctx, "gm8", [P, P])[:]
        depthwise = Depthwise(tools, ctx, a, x, xpad, gm32)
        with ExitStack() as ctx1:
            codes = (tools.sb(ctx1, "ch", [P, CODES], BF16), tools.sb(ctx1, "cl", [P, CODES], BF16),
                     tools.sb(ctx1, "nc2", [P, GROUPS * PER])[:],
                     nc.dram_tensor("half_norms", [CODES // PER, PER], F32).ap())
            ch, cl, nc2, half_norms = codes

            def layer1(y, stats, gb):
                with ExitStack() as ctx2:
                    z = tools.sb(ctx2, "z", [P, N])
                    zh = tools.sb(ctx2, "zh", [P, N], BF16)
                    zl = tools.sb(ctx2, "zl", [P, N], BF16)
                    norm = ImageNorm(tools, ctx2)
                    norm_between(nc, tools, x, y, stats, gb, gm32, norm, z, zh, zl)
                    search(nc, tools, a, half_norms, ident, z, zh, zl, ch, cl, nc2,
                           x.rearrange("p b n -> p (b n)"), norm, depthwise)

            layer0(nc, tools, a, x, xpad, gm32, gm8, ident, codes, layer1)
        layer3(nc, tools, a, x, xpad, gm32, gm8, ident, depthwise, out)


def layouts(i):
    f = np.float32
    t = np.ascontiguousarray

    def taps(w):
        return t(w.reshape(w.shape[0], P, TAPS).transpose(1, 2, 0))

    n = np.arange(N).reshape(TILES, P).T % HW
    k = np.arange(TAPS)
    base = np.stack([(n // W)[:, :, None] - 1 + k // 3, (n % W)[:, :, None] - 1 + k % 3], -1)
    base = base.reshape(P, TILES, 2 * TAPS)
    return {
        "x": t(i["x"].reshape(B, P, HW).transpose(1, 0, 2)),
        "w_cat": taps(i["L0_conv_W_cat"]),
        "w_scale": t(i["L0_conv_W_scale"].reshape(P, NB + 1, P).transpose(2, 1, 0)),
        "gamma_beta": t(np.stack([i["L0_conv_gamma"], i["L0_conv_beta"]], 1)),
        "codes_t": t(i["L1_conv_codebook"].reshape(GROUPS, P, PER, P).transpose(3, 0, 2, 1))
        .reshape(P, GROUPS, PER * P),
        "codes": i["L1_conv_codebook"].reshape(CODES // PER, PER * P),
        "wk": t(i["L2_conv_Wk"].reshape(P, TAPS, P).transpose(2, 1, 0)),
        "bk": i["L2_conv_bk"].reshape(P, TAPS),
        **{f"w_off{s}": taps(i[f"L3_conv_off{s}_w"]) for s in (1, 2)},
        **{f"b_off{s}": i[f"L3_conv_off{s}_b"].reshape(2 * TAPS, 1) for s in (1, 2)},
        **{f"w_tap{s}": taps(i[f"L3_conv_dw{s}"]) for s in (1, 2)},
        **{f"gn{s}": t(np.stack([i[f"L3_conv_gn{s}_s"], i[f"L3_conv_gn{s}_b"]], 1)) for s in (1, 2)},
        "base": base.astype(f),
        "ident": np.eye(P, dtype=f),
        "gm32": np.kron(np.eye(32), np.full((4, 4), 1 / 4)).astype(f),
        "gm8": np.kron(np.eye(8), np.full((16, 16), 1 / 16)).astype(f),
        "id3a": np.tile(np.eye(NA, dtype=f), (3, 1)),
        "id3b": np.tile(np.eye(TAPS, dtype=f), (3, 1)),
    }


def kernel(**inputs):
    import concourse.bacc as bacc
    from concourse.bass_utils import run_bass_kernel_spmd

    arrays = layouts({k: np.asarray(v) for k, v in inputs.items()})
    nc = bacc.Bacc("TRN2", target_bir_lowering=False, num_devices=1)
    a = {k: nc.dram_tensor(f"in_{k}", v.shape, mybir.dt.from_np(v.dtype), kind="ExternalInput").ap()
         for k, v in arrays.items()}
    out = nc.dram_tensor("out", [P, B, HW], F32, kind="ExternalOutput").ap()
    program(nc, a, out)
    r = run_bass_kernel_spmd(nc, [{f"in_{k}": v for k, v in arrays.items()}], core_ids=[0])
    return r.results[0]["out"].transpose(1, 0, 2).reshape(B, P, H, W)
```
